# Optimizing a Trainium2 kernel written in Bass

```python
import numpy as np
import jax
import jax.numpy as jnp

def _softmax(x, axis=-1):
    return jax.nn.softmax(x, axis=axis)

def _gelu(x):
    return jax.nn.gelu(x, approximate=True)

def _silu(x):
    return jax.nn.silu(x)

def _sigmoid(x):
    return jax.nn.sigmoid(x)

def _layernorm(x, axis=-1, eps=1e-05):
    m = jnp.mean(x, axis=axis, keepdims=True)
    v = jnp.var(x, axis=axis, keepdims=True)
    return (x - m) / jnp.sqrt(v + eps)

def _scatter_add(tgt, idx, src, axis=0):
    return tgt.at[idx].add(src)

def _segment_sum(src, seg, n):
    return jax.ops.segment_sum(src, seg, n)
kernel_name = 'mk_flamingo_gated_d2_seqx_r2_5f6f96'

def setup_inputs(seed: int=0):
    np.random.seed(seed)
    _w = jnp.asarray

    def _rec_inputs():
        import jax
        import jax.numpy as jnp
        _rk = jax.random.key(seed)
        x = -0.0002928 + 1 * jax.random.normal(jax.random.fold_in(_rk, 1), (8, 512, 512), jnp.float32)
        _lenS = 512 - jax.random.randint(jax.random.fold_in(_rk, 7), (8,), 0, max(1, 512 // 4) + 1, jnp.int32)
        _lenS2 = 512 - jax.random.randint(jax.random.fold_in(_rk, 8), (8,), 0, max(1, 512 // 4) + 1, jnp.int32)
        _ctx_1024P = jax.random.normal(jax.random.fold_in(_rk, 11), (8, 16, 512), jnp.float32)
        _ctx_1024c = jax.random.dirichlet(jax.random.fold_in(_rk, 511), 0.3 * jnp.ones((16,), jnp.float32), (8, 512))
        _ctx_1024t = jnp.einsum('bsk,bkd->bsd', _ctx_1024c, _ctx_1024P)
        _ctx_1024t = _ctx_1024t * jax.lax.rsqrt(jnp.mean(jnp.square(_ctx_1024t)) + 1e-12) * 0.953939
        ctx_1024 = -1.39393e-06 + 0.999914 * (_ctx_1024t + 0.3 * jax.random.normal(jax.random.fold_in(_rk, 611), (8, 512, 512), jnp.float32))
        _g = jax.random.normal(jax.random.fold_in(_rk, 9001), (2, 2), jnp.float32)
        _g = jnp.sign(_g) * jnp.maximum(jnp.abs(_g), 1.0) + (_g == 0) * 1.0
        g_xattn = _g[0]
        g_ffn = _g[1]
        return (x, ctx_1024, g_xattn, g_ffn)
    x, ctx_1024, g_xattn, g_ffn = _rec_inputs()

    def _L0_xattn_setup():
        import jax, jax.numpy as jnp
        import numpy as np
        D_MODEL = 512
        NUM_HEADS = 16
        HEAD_DIM = D_MODEL // NUM_HEADS
        key = jax.random.key(seed)
        ks = jax.random.split(key, 11)
        B, S, D = (2, 1024, D_MODEL)
        s = 1.0 / np.sqrt(D)
        inp = {'query': jax.random.normal(ks[0], (B, S, D), jnp.float32), 'key': jax.random.normal(ks[1], (B, S, D), jnp.float32), 'value': jax.random.normal(ks[2], (B, S, D), jnp.float32), 'Wq': jax.random.normal(ks[3], (D, D), jnp.float32) * s, 'bq': jnp.zeros((D,), jnp.float32), 'Wk': jax.random.normal(ks[4], (D, D), jnp.float32) * s, 'bk': jnp.zeros((D,), jnp.float32), 'Wv': jax.random.normal(ks[5], (D, D), jnp.float32) * s, 'bv': jnp.zeros((D,), jnp.float32), 'Wo': jax.random.normal(ks[6], (D, D), jnp.float32) * s, 'bo': jnp.zeros((D,), jnp.float32)}
        return inp
    _L0_xattn_all = _L0_xattn_setup()
    _L0_xattn_in = {k: v for k, v in _L0_xattn_all.items() if k in ('Wq', 'bq', 'Wk', 'bk', 'Wv', 'bv', 'Wo', 'bo')}
    del _L0_xattn_all

    def _L0_ffn_setup():
        import jax, jax.numpy as jnp
        import numpy as np
        BLOCK = 32
        W_BITS = 4
        ACT_BITS = 16

        def act_qdq(x):
            qmax = 2.0 ** (ACT_BITS - 1) - 1.0
            scale = jnp.maximum(jnp.max(jnp.abs(x)) / qmax, 1e-12)
            return jnp.clip(jnp.round(x / scale), -qmax - 1.0, qmax) * scale

        def fixed_qdq_u16(x):
            scale = 1.0 / 65536.0
            return jnp.clip(jnp.round(x / scale), 0.0, 65535.0) * scale

        def lpbq_dequant(w):
            O, I = w.shape
            qmax = 2.0 ** (W_BITS - 1) - 1.0
            wb = w.reshape(O, I // BLOCK, BLOCK)
            s = jnp.maximum(jnp.max(jnp.abs(wb), axis=-1, keepdims=True) / qmax, 1e-12)
            wq = jnp.clip(jnp.round(wb / s), -qmax - 1.0, qmax) * s
            return wq.reshape(O, I)
        key = jax.random.key(seed)
        k1, k2, k3, k4 = jax.random.split(key, 4)
        B, S, H, I = (2, 2048, 512, 1536)
        x = jax.random.normal(k1, (B, S, H), jnp.float32)
        w_gate = jax.random.normal(k2, (I, H), jnp.float32) * 0.02
        w_up = jax.random.normal(k3, (I, H), jnp.float32) * 0.02
        w_down = jax.random.normal(k4, (H, I), jnp.float32) * 0.02
        return {'x': x, 'w_gate': w_gate, 'w_up': w_up, 'w_down': w_down}
    _L0_ffn_all = _L0_ffn_setup()
    _L0_ffn_in = {k: v for k, v in _L0_ffn_all.items() if k in ('w_gate', 'w_up', 'w_down')}
    del _L0_ffn_all

    def _L1_xattn_setup():
        import jax, jax.numpy as jnp
        import numpy as np
        EMBED_DIM = 512
        NUM_HEADS = 16
        HEAD_DIM = EMBED_DIM // NUM_HEADS
        WINDOW = 256
        B, S_Q, S_K = (2, 1024, 1024)

        def apply_rope(x):
            Dh = x.shape[-1]
            half = Dh // 2
            pos = jnp.arange(x.shape[2], dtype=jnp.float32)
            inv_freq = 1.0 / 10000.0 ** (jnp.arange(0, half, dtype=jnp.float32) / half)
            ang = pos[:, None] * inv_freq[None, :]
            cos = jnp.cos(ang)[None, None, :, :].astype(x.dtype)
            sin = jnp.sin(ang)[None, None, :, :].astype(x.dtype)
            x1, x2 = (x[..., :half], x[..., half:])
            return jnp.concatenate([x1 * cos - x2 * sin, x1 * sin + x2 * cos], axis=-1)
        key = jax.random.key(seed)
        ks = jax.random.split(key, 11)
        scale = 1.0 / np.sqrt(EMBED_DIM)
        inp = {'query': jax.random.normal(ks[0], (B, S_Q, EMBED_DIM), jnp.float32), 'key': jax.random.normal(ks[1], (B, S_K, EMBED_DIM), jnp.float32), 'value': jax.random.normal(ks[2], (B, S_K, EMBED_DIM), jnp.float32), 'Wq': jax.random.normal(ks[3], (EMBED_DIM, EMBED_DIM), jnp.float32) * scale, 'bq': jnp.zeros((EMBED_DIM,), jnp.float32), 'Wk': jax.random.normal(ks[4], (EMBED_DIM, EMBED_DIM), jnp.float32) * scale, 'bk': jnp.zeros((EMBED_DIM,), jnp.float32), 'Wv': jax.random.normal(ks[5], (EMBED_DIM, EMBED_DIM), jnp.float32) * scale, 'bv': jnp.zeros((EMBED_DIM,), jnp.float32), 'Wo': jax.random.normal(ks[6], (EMBED_DIM, EMBED_DIM), jnp.float32) * scale, 'bo': jnp.zeros((EMBED_DIM,), jnp.float32)}
        return inp
    _L1_xattn_all = _L1_xattn_setup()
    _L1_xattn_in = {k: v for k, v in _L1_xattn_all.items() if k in ('Wq', 'bq', 'Wk', 'bk', 'Wv', 'bv', 'Wo', 'bo')}
    del _L1_xattn_all

    def _L1_ffn_setup():
        import math
        import jax, jax.numpy as jnp
        import numpy as np
        E = 8
        K = 2
        CF = 1.25
        D = 512
        F = 1024
        B, S = (4, 1024)
        key = jax.random.key(seed)
        ks = jax.random.split(key, 8)
        sd = 1.0 / math.sqrt(D)
        sf = 1.0 / math.sqrt(F)
        return {'x': jax.random.normal(ks[0], (B, S, D), jnp.float32), 'router_w': jax.random.normal(ks[1], (D, E), jnp.float32) * sd, 'router_b': jnp.zeros((E,), jnp.float32), 'w1': jax.random.normal(ks[2], (E, D, F), jnp.float32) * sd, 'b1': jax.random.normal(ks[3], (E, F), jnp.float32) * 0.01, 'w2': jax.random.normal(ks[4], (E, F, D), jnp.float32) * sf, 'b2': jax.random.normal(ks[5], (E, D), jnp.float32) * 0.01}
    _L1_ffn_all = _L1_ffn_setup()
    _L1_ffn_in = {k: v for k, v in _L1_ffn_all.items() if k in ('router_w', 'router_b', 'w1', 'b1', 'w2', 'b2')}
    del _L1_ffn_all
    return {'x': x, 'ctx_1024': ctx_1024, 'g_xattn': g_xattn, 'g_ffn': g_ffn, 'L0_xattn_Wq': _L0_xattn_in['Wq'], 'L0_xattn_bq': _L0_xattn_in['bq'], 'L0_xattn_Wk': _L0_xattn_in['Wk'], 'L0_xattn_bk': _L0_xattn_in['bk'], 'L0_xattn_Wv': _L0_xattn_in['Wv'], 'L0_xattn_bv': _L0_xattn_in['bv'], 'L0_xattn_Wo': _L0_xattn_in['Wo'], 'L0_xattn_bo': _L0_xattn_in['bo'], 'L0_ffn_w_gate': _L0_ffn_in['w_gate'], 'L0_ffn_w_up': _L0_ffn_in['w_up'], 'L0_ffn_w_down': _L0_ffn_in['w_down'], 'L1_xattn_Wq': _L1_xattn_in['Wq'], 'L1_xattn_bq': _L1_xattn_in['bq'], 'L1_xattn_Wk': _L1_xattn_in['Wk'], 'L1_xattn_bk': _L1_xattn_in['bk'], 'L1_xattn_Wv': _L1_xattn_in['Wv'], 'L1_xattn_bv': _L1_xattn_in['bv'], 'L1_xattn_Wo': _L1_xattn_in['Wo'], 'L1_xattn_bo': _L1_xattn_in['bo'], 'L1_ffn_router_w': _L1_ffn_in['router_w'], 'L1_ffn_router_b': _L1_ffn_in['router_b'], 'L1_ffn_w1': _L1_ffn_in['w1'], 'L1_ffn_b1': _L1_ffn_in['b1'], 'L1_ffn_w2': _L1_ffn_in['w2'], 'L1_ffn_b2': _L1_ffn_in['b2']}

def reference(x, ctx_1024, g_xattn, g_ffn, L0_xattn_Wq, L0_xattn_bq, L0_xattn_Wk, L0_xattn_bk, L0_xattn_Wv, L0_xattn_bv, L0_xattn_Wo, L0_xattn_bo, L0_ffn_w_gate, L0_ffn_w_up, L0_ffn_w_down, L1_xattn_Wq, L1_xattn_bq, L1_xattn_Wk, L1_xattn_bk, L1_xattn_Wv, L1_xattn_bv, L1_xattn_Wo, L1_xattn_bo, L1_ffn_router_w, L1_ffn_router_b, L1_ffn_w1, L1_ffn_b1, L1_ffn_w2, L1_ffn_b2):
    import jax
    import jax.numpy as jnp

    def _L0_xattn_ref(query, key, value, Wq, bq, Wk, bk, Wv, bv, Wo, bo):
        import jax, jax.numpy as jnp
        import numpy as np
        D_MODEL = 512
        NUM_HEADS = 16
        HEAD_DIM = D_MODEL // NUM_HEADS
        B, S, D = query.shape
        H, Hd = (NUM_HEADS, HEAD_DIM)
        Q = (query @ Wq.T + bq).reshape(B, S, H, Hd).transpose(0, 2, 1, 3)
        K = (key @ Wk.T + bk).reshape(B, S, H, Hd).transpose(0, 2, 1, 3)
        V = (value @ Wv.T + bv).reshape(B, S, H, Hd).transpose(0, 2, 1, 3)
        scale = 1.0 / jnp.sqrt(jnp.asarray(Hd, Q.dtype))
        scores = jnp.einsum('bhqd,bhkd->bhqk', Q, K) * scale
        attn = jax.nn.softmax(scores, axis=-1)
        out = jnp.einsum('bhqk,bhkd->bhqd', attn, V)
        out = out.transpose(0, 2, 1, 3).reshape(B, S, D)
        return out @ Wo.T + bo

    def _L0_ffn_ref(x, w_gate, w_up, w_down):
        import jax, jax.numpy as jnp
        import numpy as np
        BLOCK = 32
        W_BITS = 4
        ACT_BITS = 16

        def act_qdq(x):
            qmax = 2.0 ** (ACT_BITS - 1) - 1.0
            scale = jnp.maximum(jnp.max(jnp.abs(x)) / qmax, 1e-12)
            return jnp.clip(jnp.round(x / scale), -qmax - 1.0, qmax) * scale

        def fixed_qdq_u16(x):
            scale = 1.0 / 65536.0
            return jnp.clip(jnp.round(x / scale), 0.0, 65535.0) * scale

        def lpbq_dequant(w):
            O, I = w.shape
            qmax = 2.0 ** (W_BITS - 1) - 1.0
            wb = w.reshape(O, I // BLOCK, BLOCK)
            s = jnp.maximum(jnp.max(jnp.abs(wb), axis=-1, keepdims=True) / qmax, 1e-12)
            wq = jnp.clip(jnp.round(wb / s), -qmax - 1.0, qmax) * s
            return wq.reshape(O, I)
        x = act_qdq(x)
        up = act_qdq(x @ lpbq_dequant(w_up).T)
        gate = act_qdq(x @ lpbq_dequant(w_gate).T)
        sig = fixed_qdq_u16(jax.nn.sigmoid(gate))
        gate = act_qdq(gate * sig)
        o = act_qdq(gate * up)
        return o @ lpbq_dequant(w_down).T

    def _L1_xattn_ref(query, key, value, Wq, bq, Wk, bk, Wv, bv, Wo, bo):
        import jax, jax.numpy as jnp
        import numpy as np
        EMBED_DIM = 512
        NUM_HEADS = 16
        HEAD_DIM = EMBED_DIM // NUM_HEADS
        WINDOW = 256
        B, S_Q, S_K = (2, 1024, 1024)

        def apply_rope(x):
            Dh = x.shape[-1]
            half = Dh // 2
            pos = jnp.arange(x.shape[2], dtype=jnp.float32)
            inv_freq = 1.0 / 10000.0 ** (jnp.arange(0, half, dtype=jnp.float32) / half)
            ang = pos[:, None] * inv_freq[None, :]
            cos = jnp.cos(ang)[None, None, :, :].astype(x.dtype)
            sin = jnp.sin(ang)[None, None, :, :].astype(x.dtype)
            x1, x2 = (x[..., :half], x[..., half:])
            return jnp.concatenate([x1 * cos - x2 * sin, x1 * sin + x2 * cos], axis=-1)
        Bq, Sq, D = query.shape
        Sk = key.shape[1]
        H, Dh = (NUM_HEADS, HEAD_DIM)

        def proj(x, W, b):
            return (x @ W.T + b).reshape(x.shape[0], x.shape[1], H, Dh).transpose(0, 2, 1, 3)
        q = apply_rope(proj(query, Wq, bq))
        k = apply_rope(proj(key, Wk, bk))
        v = proj(value, Wv, bv)
        q = q * Dh ** (-0.5)
        scores = jnp.einsum('bhqd,bhkd->bhqk', q, k)
        q_idx = jnp.arange(Sq)[:, None]
        kv_idx = jnp.arange(Sk)[None, :]
        rel = kv_idx - q_idx
        mask = (rel > 0) | (rel < -WINDOW)
        mask4 = mask[None, None, :, :]
        neg = jnp.finfo(scores.dtype).min
        scores = jnp.where(mask4, neg, scores)
        probs = jax.nn.softmax(scores, axis=-1)
        all_masked = jnp.all(mask4, axis=-1, keepdims=True)
        probs = jnp.where(all_masked, jnp.zeros((), probs.dtype), probs)
        out = jnp.einsum('bhqk,bhkd->bhqd', probs, v)
        out = out.transpose(0, 2, 1, 3).reshape(Bq, Sq, D)
        return out @ Wo.T + bo

    def _L1_ffn_ref(x, router_w, router_b, w1, b1, w2, b2):
        import math
        import jax, jax.numpy as jnp
        import numpy as np
        E = 8
        K = 2
        CF = 1.25
        D = 512
        F = 1024
        B, S = (4, 1024)
        b, s, d = x.shape
        xf = x.reshape(-1, d)
        T = b * s
        A = T * K
        cap = max(1, int(math.ceil(CF * A / E)))
        logits = xf @ router_w + router_b
        probs = jax.nn.softmax(logits, axis=-1)
        topk_p, topk_i = jax.lax.top_k(probs, K)
        topk_p = topk_p / jnp.clip(topk_p.sum(-1, keepdims=True), 1e-09)
        a_tok = jnp.repeat(jnp.arange(T), K)
        a_exp = topk_i.reshape(-1)
        a_w = topk_p.reshape(-1)
        order = jnp.argsort(a_exp)
        se, st, sw = (a_exp[order], a_tok[order], a_w[order])
        counts = jnp.bincount(se, length=E)
        starts = jnp.cumsum(counts) - counts
        rank = jnp.arange(A) - starts[se]
        keep = rank < cap
        slot = jnp.where(keep, se * cap + rank, E * cap)
        buf = jnp.zeros((E * cap + 1, d), x.dtype).at[slot].set(xf[st])
        buf = buf[:-1].reshape(E, cap, d)
        h = jax.nn.gelu(jnp.einsum('ecd,edf->ecf', buf, w1) + b1[:, None, :], approximate=False)
        eo = jnp.einsum('ecf,efd->ecd', h, w2) + b2[:, None, :]
        eo_flat = jnp.concatenate([eo.reshape(E * cap, d), jnp.zeros((1, d), x.dtype)], axis=0)
        w = jnp.where(keep, sw, 0.0)[:, None]
        out = jnp.zeros_like(xf).at[st].add(eo_flat[slot] * w)
        return out.reshape(b, s, d)
    x = x + jnp.tanh(g_xattn[0]) * _L0_xattn_ref(_layernorm(x, axis=-1), ctx_1024, ctx_1024, L0_xattn_Wq, L0_xattn_bq, L0_xattn_Wk, L0_xattn_bk, L0_xattn_Wv, L0_xattn_bv, L0_xattn_Wo, L0_xattn_bo)
    x = x + jnp.tanh(g_ffn[0]) * _L0_ffn_ref(_layernorm(x, axis=-1), L0_ffn_w_gate, L0_ffn_w_up, L0_ffn_w_down)
    x = x + jnp.tanh(g_xattn[1]) * _L1_xattn_ref(_layernorm(x, axis=-1), ctx_1024, ctx_1024, L1_xattn_Wq, L1_xattn_bq, L1_xattn_Wk, L1_xattn_bk, L1_xattn_Wv, L1_xattn_bv, L1_xattn_Wo, L1_xattn_bo)
    x = x + jnp.tanh(g_ffn[1]) * _L1_ffn_ref(_layernorm(x, axis=-1), L1_ffn_router_w, L1_ffn_router_b, L1_ffn_w1, L1_ffn_b1, L1_ffn_w2, L1_ffn_b2)
    return x

_drawn_inputs = setup_inputs


def setup_inputs(seed=0):
    import zlib

    import numpy as np

    out = dict(_drawn_inputs(seed))
    spreads = {'g_ffn': (-1.0, 0.566),
     'L0_xattn_bq': (0.0, 0.1),
     'L0_xattn_bk': (0.0, 0.8),
     'L0_xattn_bv': (0.0, 0.1),
     'L0_xattn_bo': (0.0, 0.1),
     'L1_xattn_bq': (0.0, 0.1),
     'L1_xattn_bk': (0.0, 0.1),
     'L1_xattn_bv': (0.0, 0.1),
     'L1_xattn_bo': (0.0, 0.1),
     'L1_ffn_router_b': (0.0, 0.1)}
    factors = {'L1_ffn_b1': 8.0, 'L1_ffn_b2': 8.0}
    for name, (base, spread) in spreads.items():
        noise = np.random.default_rng([zlib.crc32(name.encode()), seed]).standard_normal(out[name].shape)
        drawn = base * np.exp(spread * noise) if base else spread * noise
        out[name] = jnp.asarray(drawn.astype(out[name].dtype))
    for name, factor in factors.items():
        out[name] = (out[name] * factor).astype(out[name].dtype)
    return out
```

```python
from contextlib import ExitStack

import numpy as np
import concourse.bass as bass
from concourse import mybir

F32 = mybir.dt.float32
F32R = mybir.dt.float32r
BF16 = mybir.dt.bfloat16
I16 = mybir.dt.int16
U16 = mybir.dt.uint16
I32 = mybir.dt.int32
U32 = mybir.dt.uint32
ALU = mybir.AluOpType
ACT = mybir.ActivationFunctionType
AX = mybir.AxisListType

P = 128
B, S, D = 8, 512, 512
T = B * S
NT = T // P
DT = D // P
ST = S // P
H, HD = 16, 32
HG = P // HD
G = H // HG
EPS = 1e-5
WINDOW = 256
NEG = -1.0e30


def passed(eng, sem, value, seen):
    eng.wait_ge(sem, value)
    eng.sem_inc(seen, 1)


def stage_semaphores(nc, ctx, tag):
    made = []
    ctx.callback(nc.all_engine_barrier)
    ctx.callback(nc.clear_and_free_semaphores, made)

    def sem(name):
        made.append(nc.alloc_semaphore(tag + name))
        return made[-1]

    return sem


def f32(ap):
    return ap.bitcast(F32)




def attention(nc, layer, x_in, x_out, h_out, hmax_out, ctx_t, w_in, cols, rows, gate, consts):
    rope = masked = layer == 1
    tag = f"a{layer}_"
    SCALE = float(HD) ** -0.5
    span = WINDOW // P
    keys_of = [(max(0, q - span), q + 1) if masked else (0, ST) for q in range(ST)]
    queries_of = [(k, min(ST, k + span + 1)) if masked else (0, ST) for k in range(ST)]

    with ExitStack() as ctx:
        def sb(name, shape, dt=F32):
            return ctx.enter_context(nc.sbuf_tensor(tag + name, shape, dt))

        def ps(name, shape, dt=F32):
            return ctx.enter_context(nc.psum_tensor(tag + name, shape, dt))

        sem = stage_semaphores(nc, ctx, tag)

        w_hi = sb("w_hi", [P, 3, DT, D], F32R)
        w_lo = sb("w_lo", [P, 3, DT, D], F32R)
        wo = sb("wo", [P, DT, D])
        ctx_raw = sb("ctx_raw", [P, DT, S])
        ctx_hi = sb("ctx_hi", [P, DT, S], F32R)
        ctx_lo = sb("ctx_lo", [P, DT, S], F32R)
        x_tile = sb("x_tile", [P, 2, D])
        hn = sb("hn", [P, 2, D])
        ht_hi = sb("ht_hi", [P, DT, S], F32R)
        ht_lo = sb("ht_lo", [P, DT, S], F32R)
        qk_hi = sb("qk_hi", [P, 2, S], F32R)
        qk_lo = sb("qk_lo", [P, 2, S], F32R)
        NR = 3 * HD + 1
        q_stack = sb("q_stack", [P, 2, HG, S], F32R)
        k_stack = sb("k_stack", [P, 2, HG, S], F32R)
        v_sb = sb("v_sb", [P, ST, D])
        probs = sb("probs", [P, 2, HG, S])
        negmax = sb("negmax", [P, HG * ST])
        negmax_r = sb("negmax_r", [P, 32], F32R)
        negmax_t = sb("negmax_t", [P, 32])
        recip = sb("recip", [P, S])
        att = sb("att", [P, G, S])
        ones = sb("ones", [P, HD])
        ident = sb("ident", [P, P])
        b_col = {"q": sb("bq_col", [P, DT]), "k": sb("bk_col", [P, DT])}
        bv_row = sb("bv_row", [P, D])
        bo_row = sb("bo_row", [P, D])
        gate_col = sb("gate_col", [P, 1])
        tanh_g = sb("tanh_g", [P, 1])
        bn = sb("bn", [P, 2, 6])
        mv = sb("mv", [P, 2, 2])
        ve = sb("ve", [P, 2])
        rstd = sb("rstd", [P, 2])
        halfneg = sb("halfneg", [P, 1])
        x_new = sb("x_new", [P, 2, D])
        bn_o = sb("bn_o", [P, 2, 6])
        mv_o = sb("mv_o", [P, 2, 2])
        ve_o = sb("ve_o", [P, 2])
        rstd_o = sb("rstd_o", [P, 2])
        nmr_o = sb("nmr_o", [P, 2])
        h_new = sb("h_new", [P, 2, D])
        hmax = sb("hmax", [P, NT])
        hmax_all = sb("hmax_all", [P, 1])
        if masked:
            ident_b = sb("ident_b", [P, P], BF16)
            masks = sb("masks", [P, 2, P], BF16)
            masks_in = sb("masks_in", [P, 2, P])
            cos_t = sb("cos_t", [P, S])
            sin_t = sb("sin_t", [P, S])
            lin = sb("lin", [P, S])
            swapped = sb("swapped", [P, S])
            lin_cos = sb("lin_cos", [P, S])
            swap_sin = sb("swap_sin", [P, S])

        pj = ps("pj", [P, 2, 512])
        pa = ps("pa", [P, 2, 512])
        pst = ps("pst", [P, 2, 512])
        po = ps("po", [P, 512])
        psm = ps("psm", [P, 512])

        s_w = [sem("s_w0"), sem("s_w1"), sem("s_w2")]
        s_const = sem("s_const")
        s_w_hi = sem("s_w_hi")
        s_w_lo = sem("s_w_lo")
        s_setup = sem("s_setup")
        s_tanh = sem("s_tanh")
        s_x_in = [sem("s_x_in0"), sem("s_x_in1")]
        s_ctx_in = sem("s_ctx_in")
        s_ctx_hi = sem("s_ctx_hi")
        s_ctx_lo = sem("s_ctx_lo")
        s_bn = sem("s_bn")
        s_mv = sem("s_mv")
        s_ve = sem("s_ve")
        s_rstd = sem("s_rstd")
        s_hn = sem("s_hn")
        s_pj = sem("s_pj")
        s_pj_out = sem("s_pj_out")
        s_ht_hi = sem("s_ht_hi")
        s_qk_hi = sem("s_qk_hi")
        s_qk_lo = sem("s_qk_lo")
        s_stack = {"q": [sem("s_qst0"), sem("s_qst1")], "k": [sem("s_kst0"), sem("s_kst1")]}
        s_pa = sem("s_pa")
        s_max = sem("s_max")
        s_nm_r = sem("s_nm_r")
        s_nm_t = sem("s_nm_t")
        s_mrow = [sem("s_mrow0"), sem("s_mrow1")]
        s_st = sem("s_st")
        s_exp = sem("s_exp")
        s_pv = sem("s_pv")
        s_norm = sem("s_norm")
        s_xres = [sem("s_xres0"), sem("s_xres1")]
        s_xb = sem("s_xb")
        s_bn_o = sem("s_bn_o")
        s_mv_o = sem("s_mv_o")
        s_ve_o = sem("s_ve_o")
        s_rstd_o = sem("s_rstd_o")
        s_nmr_o = sem("s_nmr_o")
        s_h_new = sem("s_h_new")
        s_hmax = sem("s_hmax")
        s_store_x = [sem("s_store_x0"), sem("s_store_x1")]
        s_store_h = [sem("s_store_h0"), sem("s_store_h1")]
        s_lin = sem("s_lin")
        s_swap = sem("s_swap")
        s_rope = sem("s_rope")
        s_sin = sem("s_sin")
        s_last = sem("s_last")
        s_passed = sem("s_passed")
        s_passed_sp = sem("s_passed_sp")
        block = ctx.enter_context(nc.Block())

        V0, K0, T0, Q0, QK2, O0, PJ = 0, 4, 6, 10, 12, 16, 20
        QK = [("k", 0, K0), ("k", 1, K0 + 1), ("q", 0, Q0), ("q", 1, Q0 + 1),
              ("k", 2, QK2), ("q", 2, QK2 + 1), ("k", 3, QK2 + 2), ("q", 3, QK2 + 3)]
        NQK = len(QK)
        NSC = G * HG * ST
        STACK = 16 * 3
        MROW = 16 * (P // 32)
        NCONST = 16 * (7 + 3 * masked)

        def stacked(b, g):
            return (b * (G // 2) + g // 2 + 1) * STACK

        raw_of = [probs[:, 0], probs[:, 1], ctx_raw[:]]

        def tile_out(b, n):
            return b * PJ + n + 3

        def lo_written(b, n):
            return (s_qk_lo, b * NQK + n + 1) if rope else (s_pj_out, tile_out(b, QK[n][2]))

        def store(sp, b, t):
            passed(sp, s_h_new, b * ST + t + 1, s_passed_sp)
            sp.dma_start(x_out[b, t * P:(t + 1) * P, :], x_new[:, t % 2, :]).then_inc(s_store_x[t % 2], 16)
            sp.dma_start(h_out[b, t * P:(t + 1) * P, :], h_new[:, t % 2, :]).then_inc(s_store_h[t % 2], 16)

        @block.sync
        def _(sp):
            for m in range(3):
                sp.dma_start(raw_of[m], w_in[m]).then_inc(s_w[m], 16)
            sp.dma_start(wo[:], w_in[3]).then_inc(s_const, 16)
            loads = [(ident[:], consts["ident"]), (b_col["q"][:], cols["bq"]), (b_col["k"][:], cols["bk"]),
                     (bv_row[:], rows["bv"]), (bo_row[:], rows["bo"]), (gate_col[:], gate)]
            if masked:
                loads += [(masks_in[:], consts["masks"]),
                          (cos_t[:], consts["cos"]), (sin_t[:], consts["sin"])]
            for dst, src in loads:
                sp.dma_start(dst, src).then_inc(s_const, 16)
            sp.wait_ge(s_w_lo, 3)
            sp.dma_start(ctx_raw[:], ctx_t[0]).then_inc(s_ctx_in, 16)
            with sp.Fori(0, B) as b:
                for t in range(ST):
                    passed(sp, s_hn, b * ST + t + 1, s_passed_sp)
                    sp.dma_start(x_tile[:, t % 2, :], x_in[b, t * P:(t + 1) * P, :]).then_inc(s_x_in[t % 2], 16)

                def to_stack(n):
                    kind, g, _ = QK[n]
                    passed(sp, *lo_written(b, n), s_passed_sp)
                    if g >= 2:
                        passed(sp, s_st, b * NSC + (g - 1) * HG * ST, s_passed_sp)
                    dst = {"q": q_stack, "k": k_stack}[kind]
                    srcs = {"q": (qk_hi, qk_hi, qk_lo), "k": (qk_hi, qk_lo, qk_hi)}[kind]
                    for row, src in enumerate(srcs):
                        sp.dma_start(f32(dst[HD * row:HD * row + HD, g % 2, :, :]),
                                     f32(src[:, n % 2, :])).then_inc(s_stack[kind][g % 2], 16)

                def maximum_rows(g):
                    passed(sp, s_nm_t, b * G + g + 1, s_passed_sp)
                    row = f32(q_stack[3 * HD:NR, g % 2, :, :]).rearrange("r j (t a q) -> r (j t) a q", t=ST, a=P // 32)
                    for a in range(P // 32):
                        sp.dma_start(row[:, :, a, :],
                                     negmax_t[32 * a:32 * a + HG * ST, :]).then_inc(s_mrow[g % 2], 16)

                for n in range(4):
                    to_stack(n)
                maximum_rows(0)
                passed(sp, s_ctx_lo, b + 1, s_passed_sp)
                sp.dma_start(ctx_raw[:], ctx_t[b + 1]).then_inc(s_ctx_in, 16)
                for g in range(G):
                    if g + 1 < G:
                        maximum_rows(g + 1)
                    if g + 2 < G:
                        to_stack(2 * g + 4)
                        to_stack(2 * g + 5)
                for t in range(ST):
                    passed(sp, s_store_x[t % 2], (b * (ST // 2) + t // 2 + 1) * 16, s_passed_sp)
                    sp.dma_start(x_new[:, t % 2, :], x_in[b, t * P:(t + 1) * P, :]).then_inc(s_xres[t % 2], 16)
                    if t >= 1:
                        store(sp, b, t - 1)
                store(sp, b, ST - 1)
            for u in range(2):
                sp.wait_ge(s_store_x[u], (B * ST // 2 + 1) * 16)
                sp.wait_ge(s_store_h[u], (B * ST // 2 + 1) * 16)
            sp.wait_ge(s_ctx_in, (B + 1) * 16)
            if hmax_out is not None:
                sp.wait_ge(s_last, 1)
                sp.dma_start(hmax_out, hmax_all[:]).then_inc(s_last, 16)
                sp.wait_ge(s_last, 17)

        @block.scalar
        def _(act):
            for m in range(3):
                act.wait_ge(s_w[m], 16)
                act.activation(w_hi[:, m], raw_of[m], ACT.Copy).then_inc(s_w_hi, 1)
            act.wait_ge(s_const, NCONST)
            act.activation(tanh_g[:], gate_col[:], ACT.Tanh).then_inc(s_tanh, 1)
            with act.Fori(0, B) as b:
                act.wait_ge(s_ctx_in, b * 16 + 16)
                act.activation(ctx_hi[:], ctx_raw[:], ACT.Copy).then_inc(s_ctx_hi, 1)

                def qk_to_hi(n):
                    kind, g, tile = QK[n]
                    if n >= 2:
                        kk, gg, _ = QK[n - 2]
                        act.wait_ge(s_stack[kk][gg % 2], stacked(b, gg))
                    if rope:
                        act.wait_ge(s_rope, b * NQK + n + 1)
                        act.activation(qk_hi[:, n % 2, :], lin_cos[:], ACT.Copy).then_inc(s_qk_hi, 1)
                    else:
                        act.wait_ge(s_pj, b * PJ + tile + 1)
                        act.activation(qk_hi[:, n % 2, :], pj[:, tile % 2, :], ACT.Identity,
                                       bias=b_col[kind][:, g:g + 1]).then_inc(s_qk_hi, 1)

                qk_to_hi(0)
                qk_to_hi(1)
                for t in range(ST):
                    act.wait_ge(s_pj, b * PJ + T0 + t + 1)
                    act.activation(ht_hi[:, :, t * P:(t + 1) * P],
                                   pj[:, (T0 + t) % 2, :].rearrange("p (d t) -> p d t", d=DT),
                                   ACT.Copy).then_inc(s_ht_hi, 1)
                qk_to_hi(2)
                qk_to_hi(3)
                for g in range(G):
                    for k in range(ST):
                        q0, q1 = queries_of[k]
                        act.wait_ge(s_pv, b * G * ST + g * ST + k + 1)
                        for j in range(HG):
                            n = (g * ST + k) * HG + j
                            act.wait_ge(s_st, b * NSC + n + 1)
                            act.activation(probs[:, k % 2, j, q0 * P:q1 * P], pst[:, n % 2, q0 * P:q1 * P],
                                           ACT.Exp, scale=SCALE).then_inc(s_exp, 1)
                    if g + 2 < G:
                        qk_to_hi(2 * g + 4)
                        qk_to_hi(2 * g + 5)
                for t in range(ST):
                    act.wait_ge(s_nmr_o, b * ST + t + 1)
                    act.wait_ge(s_store_h[t % 2], (b * (ST // 2) + t // 2 + 1) * 16)
                    if hmax_out is not None:
                        act.wait_ge(s_hmax, b * ST + t + 1)
                    act.activation(h_new[:, t % 2, :], x_new[:, t % 2, :], ACT.Identity,
                                   bias=nmr_o[:, t % 2:t % 2 + 1], scale=rstd_o[:, t % 2:t % 2 + 1]).then_inc(s_h_new, 1)

        @block.gpsimd
        def _(pool):
            pool.wait_ge(s_setup, 4)
            with pool.Fori(0, B) as b:
                for t in range(ST):
                    pool.wait_ge(s_ve, b * ST + t + 1)
                    pool.tensor_tensor(rstd[:, t % 2:t % 2 + 1], ve[:, t % 2:t % 2 + 1], halfneg[:],
                                       ALU.pow).then_inc(s_rstd, 1)
                if rope:
                    for n in range(NQK):
                        pool.wait_ge(s_swap, (b * NQK + n + 1) * 2)
                        pool.tensor_tensor(swap_sin[:], swapped[:], sin_t[:], ALU.mult).then_inc(s_sin, 1)

                def add_bias(t):
                    pool.wait_ge(s_xres[t % 2], (b * (ST // 2) + t // 2 + 1) * 16)
                    pool.tensor_tensor(x_new[:, t % 2, :], x_new[:, t % 2, :], bo_row[:], ALU.add).then_inc(s_xb, 1)

                add_bias(0)
                add_bias(1)
                for t in range(ST):
                    pool.wait_ge(s_ve_o, b * ST + t + 1)
                    pool.tensor_tensor(rstd_o[:, t % 2:t % 2 + 1], ve_o[:, t % 2:t % 2 + 1], halfneg[:],
                                       ALU.pow).then_inc(s_rstd_o, 1)
                    if t + 2 < ST:
                        add_bias(t + 2)

        @block.vector
        def _(dve):
            dve.memset(ones[:], 1.0).then_inc(s_setup, 1)
            dve.memset(halfneg[:], -0.5).then_inc(s_setup, 1)
            dve.memset(f32(k_stack[3 * HD:NR]), 1.0).then_inc(s_setup, 1)
            dve.memset(f32(negmax_r[:, HG * ST:32]), 0.0).then_inc(s_setup, 1)
            for m in range(3):
                dve.wait_ge(s_w_hi, m + 1)
                dve.tensor_tensor(w_lo[:, m], raw_of[m], f32(w_hi[:, m]), ALU.subtract).then_inc(s_w_lo, 1)
            for s, n in ((s_hn, 2), (s_pj_out, 2), (s_max, 2), (s_exp, 2), (s_pv, 2), (s_norm, 1), (s_hmax, 2),
                         (s_store_x[0], 16), (s_store_x[1], 16), (s_store_h[0], 16), (s_store_h[1], 16)):
                dve.sem_inc(s, n)
            dve.wait_ge(s_tanh, 1)
            if masked:
                dve.tensor_copy(ident_b[:], ident[:]).then_inc(s_setup, 1)
                dve.tensor_copy(masks[:], masks_in[:]).then_inc(s_setup, 1)
            dve.tensor_scalar(bo_row[:], bo_row[:], tanh_g[:], None, ALU.mult).then_inc(s_setup, 1)
            with dve.Fori(0, B) as b:
                def stats(t):
                    u = t % 2
                    dve.wait_ge(s_x_in[u], (b * (ST // 2) + t // 2 + 1) * 16)
                    dve.bn_stats(bn[:, u, :], x_tile[:, u, :]).then_inc(s_bn, 1)
                    passed(dve, s_bn, b * ST + t + 1, s_passed)
                    dve.bn_aggr(mv[:, u, :], bn[:, u, :]).then_inc(s_mv, 1)
                    dve.wait_ge(s_mv, b * ST + t + 1)
                    dve.tensor_scalar(ve[:, u:u + 1], mv[:, u, 1:2], EPS, None, ALU.add).then_inc(s_ve, 1)

                def normalise(t):
                    u = t % 2
                    dve.wait_ge(s_rstd, b * ST + t + 1)
                    dve.tensor_scalar(hn[:, u, :], x_tile[:, u, :], mv[:, u, 0:1], rstd[:, u:u + 1],
                                      ALU.subtract, ALU.mult).then_inc(s_hn, 1)

                def values(t):
                    dve.wait_ge(s_pj, b * PJ + V0 + t + 1)
                    dve.tensor_tensor(v_sb[:, t, :], pj[:, (V0 + t) % 2, :], bv_row[:], ALU.add).then_inc(s_pj_out, 1)

                def qk_to_lo(n):
                    kind, g, tile = QK[n]
                    bias = b_col[kind][:, g:g + 1]
                    if rope:
                        dve.wait_ge(s_pj, b * PJ + tile + 1)
                        dve.tensor_scalar(lin[:], pj[:, tile % 2, :], bias, None, ALU.add).then_inc(s_pj_out, 1)
                        dve.wait_ge(s_pj_out, tile_out(b, tile))
                        dve.tensor_copy(swapped[0:P // 2, :], lin[P // 2:P, :]).then_inc(s_swap, 1)
                        dve.tensor_copy(swapped[P // 2:P, :], lin[0:P // 2, :]).then_inc(s_swap, 1)
                        dve.tensor_tensor(lin_cos[:], lin[:], cos_t[:], ALU.mult).then_inc(s_lin, 1)
                        dve.wait_ge(s_lin, b * NQK + n + 1)
                        dve.wait_ge(s_sin, b * NQK + n + 1)
                        dve.tensor_tensor(lin_cos[:], lin_cos[:], swap_sin[:], ALU.add).then_inc(s_rope, 1)
                        dve.wait_ge(s_qk_hi, b * NQK + n + 1)
                        dve.tensor_tensor(qk_lo[:, n % 2, :], lin_cos[:], f32(qk_hi[:, n % 2, :]),
                                          ALU.subtract).then_inc(s_qk_lo, 1)
                    else:
                        dve.wait_ge(s_qk_hi, b * NQK + n + 1)
                        dve.scalar_tensor_tensor(qk_lo[:, n % 2, :], pj[:, tile % 2, :], bias,
                                                 f32(qk_hi[:, n % 2, :]), ALU.add, ALU.subtract).then_inc(s_pj_out, 1)

                def ht_to_lo(t):
                    dve.wait_ge(s_ht_hi, b * ST + t + 1)
                    cut = (slice(None), slice(None), slice(t * P, (t + 1) * P))
                    dve.tensor_tensor(ht_lo[cut], pj[:, (T0 + t) % 2, :].rearrange("p (d t) -> p d t", d=DT),
                                      f32(ht_hi[cut]), ALU.subtract).then_inc(s_pj_out, 1)

                def maxima(g, q):
                    k0, k1 = keys_of[q]
                    for j in range(HG):
                        n = (g * ST + q) * HG + j
                        dve.wait_ge(s_pa, b * NSC + n + 1)
                        dve.tensor_reduce(negmax[:, j * ST + q:j * ST + q + 1], pa[:, n % 2, k0 * P:k1 * P],
                                          AX.X, ALU.max, negate=True).then_inc(s_max, 1)

                def maxima_to_rows(g):
                    C = HG * ST
                    n = b * G + g + 1
                    dve.wait_ge(s_max, b * NSC + (g + 1) * C + 2)
                    dve.tensor_copy(negmax_r[:, 0:C], negmax[:]).then_inc(s_nm_r, 1)
                    dve.wait_ge(s_nm_r, n)
                    if g >= 1:
                        dve.wait_ge(s_mrow[(g - 1) % 2], (b * 2 + (g - 1) // 2 + 1) * MROW)
                    dve.transpose(negmax_t[:], f32(negmax_r[:])).then_inc(s_nm_t, 1)

                def head_outputs(g):
                    dve.wait_ge(s_pv, b * G * ST + (g + 1) * ST + 2)
                    dve.reciprocal(recip[:], psm[:]).then_inc(s_norm, 1)
                    dve.wait_ge(s_norm, (b * G + g) * 2 + 2)
                    dve.tensor_tensor(att[:, g, :], po[:], recip[:], ALU.mult).then_inc(s_norm, 1)

                stats(0)
                stats(1)
                dve.wait_ge(s_ctx_hi, b + 1)
                dve.tensor_tensor(ctx_lo[:], ctx_raw[:], f32(ctx_hi[:]), ALU.subtract).then_inc(s_ctx_lo, 1)
                normalise(0)
                normalise(1)
                values(0)
                stats(2)
                values(1)
                stats(3)
                values(2)
                values(3)
                qk_to_lo(0)
                qk_to_lo(1)
                for t in range(ST):
                    ht_to_lo(t)
                    if t < 2:
                        normalise(t + 2)
                qk_to_lo(2)
                qk_to_lo(3)
                for q in range(ST):
                    maxima(0, q)
                maxima_to_rows(0)
                for g in range(G):
                    for k in range(ST):
                        if g + 1 < G:
                            maxima(g + 1, k)
                        if k == 0 and g >= 1:
                            head_outputs(g - 1)
                    if g + 1 < G:
                        maxima_to_rows(g + 1)
                    if g + 2 < G:
                        qk_to_lo(2 * g + 4)
                        qk_to_lo(2 * g + 5)
                head_outputs(G - 1)

                def out_stats(t):
                    u = t % 2
                    n = b * ST + t + 1
                    dve.wait_ge(s_pj, b * PJ + O0 + t + 1)
                    dve.wait_ge(s_xb, n)
                    dve.scalar_tensor_tensor(x_new[:, u, :], pj[:, (O0 + t) % 2, :], tanh_g[:], x_new[:, u, :],
                                             ALU.mult, ALU.add).then_inc(s_pj_out, 1)
                    dve.wait_ge(s_pj_out, tile_out(b, O0 + t))
                    dve.bn_stats(bn_o[:, u, :], x_new[:, u, :]).then_inc(s_bn_o, 1)
                    passed(dve, s_bn_o, n, s_passed)
                    dve.bn_aggr(mv_o[:, u, :], bn_o[:, u, :]).then_inc(s_mv_o, 1)
                    dve.wait_ge(s_mv_o, n)
                    dve.tensor_scalar(ve_o[:, u:u + 1], mv_o[:, u, 1:2], EPS, None, ALU.add).then_inc(s_ve_o, 1)

                def out_scale(t):
                    u = t % 2
                    dve.wait_ge(s_rstd_o, b * ST + t + 1)
                    dve.scalar_tensor_tensor(nmr_o[:, u:u + 1], mv_o[:, u, 0:1], -1.0, rstd_o[:, u:u + 1],
                                             ALU.mult, ALU.mult).then_inc(s_nmr_o, 1)

                def out_max(t):
                    if hmax_out is not None:
                        dve.wait_ge(s_h_new, b * ST + t + 1)
                        dve.tensor_reduce(hmax[:, bass.ds(b * ST + t, 1)], h_new[:, t % 2, :], AX.X, ALU.max,
                                          apply_absolute_value=True).then_inc(s_hmax, 1)

                for t in range(ST):
                    out_stats(t)
                    out_scale(t)
                    if t >= 1:
                        out_max(t - 1)
                out_max(ST - 1)
            if hmax_out is not None:
                dve.wait_ge(s_hmax, NT + 2)
                dve.tensor_reduce(hmax_all[:], hmax[:], AX.X, ALU.max).then_inc(s_last, 1)

        @block.tensor
        def _(pe):
            def open_tile(b, n):
                pe.wait_ge(s_pj_out, b * PJ + n + 1)
                return pj[:, n % 2, :]

            def three_passes(out, lhs, rhs):
                for d in range(DT):
                    (lh, ll), (rh, rl) = lhs(d), rhs(d)
                    for n, (l, r) in enumerate(((lh, rh), (lh, rl), (ll, rh))):
                        mm = pe.matmul(out, l, r, start=(d == 0 and n == 0), stop=(d == DT - 1 and n == 2))
                return mm

            pe.wait_ge(s_w_lo, 3)
            pe.wait_ge(s_setup, 5 + 2 * masked)
            with pe.Fori(0, B) as b:
                def project(n, lhs, rhs):
                    three_passes(open_tile(b, n), lhs, rhs).then_inc(s_pj, 1)

                def project_qk(n):
                    kind, g, tile = QK[n]
                    m = {"q": 0, "k": 1}[kind]
                    hi, lo = {"q": (ht_hi, ht_lo), "k": (ctx_hi, ctx_lo)}[kind]
                    cut = slice(g * P, (g + 1) * P)
                    project(tile, lambda d: (w_hi[:, m, d, cut], w_lo[:, m, d, cut]),
                            lambda d: (hi[:, d, :], lo[:, d, :]))

                def score_max(g, q, j):
                    n = (g * ST + q) * HG + j
                    k0, k1 = keys_of[q]
                    pe.wait_ge(s_max, b * NSC + n + 1)
                    out = pa[:, n % 2, :]
                    mm = pe.matmul(out[:, k0 * P:k1 * P], q_stack[0:3 * HD, g % 2, j, q * P:(q + 1) * P],
                                   k_stack[0:3 * HD, g % 2, j, k0 * P:k1 * P], start=True, stop=not masked)
                    if masked:
                        far = q - span >= 0
                        mm = pe.matmul(out[:, q * P:(q + 1) * P], ident_b[:], masks[:, 0, :], start=False, stop=not far)
                        if far:
                            mm = pe.matmul(out[:, k0 * P:(k0 + 1) * P], ident_b[:], masks[:, 1, :],
                                           start=False, stop=True)
                    mm.then_inc(s_pa, 1)

                def score(g, k, j):
                    n = (g * ST + k) * HG + j
                    q0, q1 = queries_of[k]
                    pe.wait_ge(s_exp, b * NSC + n + 1)
                    out = pst[:, n % 2, :]
                    mm = pe.matmul(out[:, q0 * P:q1 * P], k_stack[0:NR, g % 2, j, k * P:(k + 1) * P],
                                   q_stack[0:NR, g % 2, j, q0 * P:q1 * P], start=True, stop=not masked)
                    if masked:
                        far = k + span < ST
                        mm = pe.matmul(out[:, k * P:(k + 1) * P], ident_b[:], masks[:, 1, :], start=False, stop=not far)
                        if far:
                            mm = pe.matmul(out[:, (q1 - 1) * P:q1 * P], ident_b[:], masks[:, 0, :],
                                           start=False, stop=True)
                    mm.then_inc(s_st, 1)

                def value_products(g, k, sums):
                    if not sums:
                        pe.wait_ge(s_exp, b * NSC + (g * ST + k + 1) * HG + 2)
                        if k == 0:
                            pe.wait_ge(s_norm, (b * G + g) * 2 + 1)
                    q0, q1 = queries_of[k]
                    for j in range(HG):
                        h = g * HG + j
                        lhs = ones[:] if sums else v_sb[:, k, h * HD:(h + 1) * HD]
                        mm = pe.matmul((psm if sums else po)[HD * j:HD * j + HD, q0 * P:q1 * P], lhs,
                                       probs[:, k % 2, j, q0 * P:q1 * P], start=(k == 0), stop=(k == ST - 1),
                                       skip_group_check=masked)
                    if sums:
                        mm.then_inc(s_pv, 1)

                pe.wait_ge(s_ctx_lo, b + 1)
                for t in range(ST):
                    cut = slice(t * P, (t + 1) * P)
                    project(V0 + t, lambda d: (ctx_hi[:, d, cut], ctx_lo[:, d, cut]),
                            lambda d: (w_hi[:, 2, d, :], w_lo[:, 2, d, :]))
                project_qk(0)
                project_qk(1)
                for t in range(ST):
                    out = open_tile(b, T0 + t)
                    pe.wait_ge(s_hn, b * ST + t + 3)
                    for d in range(DT):
                        mm = pe.transpose(out[:, d * P:(d + 1) * P], hn[:, t % 2, d * P:(d + 1) * P], ident[:])
                    mm.then_inc(s_pj, 1)
                pe.wait_ge(s_pj_out, tile_out(b, T0 + ST - 1))
                project_qk(2)
                project_qk(3)
                for kind in "qk":
                    pe.wait_ge(s_stack[kind][0], stacked(b, 0))
                for q in range(ST):
                    for j in range(HG):
                        score_max(0, q, j)
                for g in range(G):
                    pe.wait_ge(s_mrow[g % 2], (b * 2 + g // 2 + 1) * MROW)
                    for k in range(ST):
                        before = (g, k - 1) if k else (g - 1, ST - 1)
                        score(g, k, 0)
                        score(g, k, 1)
                        if before[0] >= 0:
                            value_products(*before, False)
                        score(g, k, 2)
                        if before[0] >= 0:
                            value_products(*before, True)
                        score(g, k, 3)
                        if g + 1 < G:
                            if k == 0:
                                for kind in "qk":
                                    pe.wait_ge(s_stack[kind][(g + 1) % 2], stacked(b, g + 1))
                            for j in range(HG):
                                score_max(g + 1, k, j)
                    if g + 2 < G:
                        project_qk(2 * g + 4)
                        project_qk(2 * g + 5)
                value_products(G - 1, ST - 1, False)
                value_products(G - 1, ST - 1, True)
                pe.wait_ge(s_norm, (b * G + G) * 2 + 1)
                for t in range(ST):
                    out = open_tile(b, O0 + t)
                    for g in range(G):
                        mm = pe.matmul(out, att[:, g, t * P:(t + 1) * P], wo[:, g, :],
                                       start=(g == 0), stop=(g == G - 1))
                    mm.then_inc(s_pj, 1)


I = 1536
IT = I // P
QBLOCK = 32
QMAX_A = 2.0 ** 15 - 1.0
QMAX_W = 2.0 ** 3 - 1.0
SCALE_MIN = 1e-12
SIG_ONE = 65536.0
NQ = B * IT // 4


def gated_mlp(nc, h_in, hmax_in, x_in, x_out, weights, gate, ident_in, spill):
    with ExitStack() as whole:
        def keep(name, shape, dt=F32):
            return whole.enter_context(nc.sbuf_tensor("m_" + name, shape, dt))

        scale = {n: keep("scale_" + n, [P, 1]) for n in ("h", "gate", "up", "silu", "out")}
        inv = {n: keep("inv_" + n, [P, 1]) for n in ("h", "gate", "up", "silu", "out")}
        peak = keep("peak", [P, 2])
        peak_all = keep("peak_all", [P, 2])
        mix = keep("mix", [P, 4])

        def find_scale(dve, link, name, top, unit):
            if unit is None:
                link(dve.tensor_scalar(scale[name][:], top, 1.0 / QMAX_A, SCALE_MIN, ALU.mult, ALU.max))
                link(dve.reciprocal(inv[name][:], scale[name][:]))
            else:
                link(dve.tensor_scalar(mix[:, 1:2], top, unit, 1.0 / QMAX_A, ALU.mult, ALU.mult))
                link(dve.tensor_scalar(scale[name][:], mix[:, 1:2], SCALE_MIN, None, ALU.max))
                link(dve.reciprocal(mix[:, 2:3], scale[name][:]))
                link(dve.tensor_tensor(inv[name][:], mix[:, 2:3], unit, ALU.mult))

        with ExitStack() as ctx:
            w_hi = ctx.enter_context(nc.sbuf_tensor("m_w_hi", [P, 2, DT, I], F32R))
            w_lo = ctx.enter_context(nc.sbuf_tensor("m_w_lo", [P, 2, DT, I], F32R))
            ident = ctx.enter_context(nc.sbuf_tensor("m_ident", [P, P], F32))
            mlp_weights(nc, weights, ident_in, ident, w_hi, w_lo, spill)
            mlp_inner(nc, h_in, hmax_in, ident, w_hi, w_lo, spill, scale, inv, peak, peak_all, find_scale)
        silu_q = keep("silu_q", [P, NQ, 4 * S], I16)
        mlp_silu(nc, spill, silu_q, scale, inv, peak, peak_all, mix, find_scale)
        mlp_product(nc, spill, silu_q, scale, inv, peak, peak_all, mix, find_scale)
        mlp_down(nc, spill, silu_q, x_in, x_out, gate, scale, inv)


def mlp_weights(nc, weights, ident_in, ident, w_hi, w_lo, spill):
    with ExitStack() as ctx:
        def sb(name, shape, dt=F32):
            return ctx.enter_context(nc.sbuf_tensor("mw_" + name, shape, dt))

        sem = stage_semaphores(nc, ctx, "mw_")

        NU, RB = 9, 4
        NB = D // QBLOCK
        raw = sb("raw", [P, 3, D])
        amax = sb("amax", [P, 2, NB])
        step = sb("step", [P, 2, NB])
        rstep = sb("rstep", [P, 2, NB])
        wi = sb("wi", [P, 2, D], I16)
        wq = sb("wq", [P, 2, D])
        down_hi = sb("down_hi", [P, 2, DT, P], F32R)
        down_lo = sb("down_lo", [P, 2, DT, P], F32R)
        pt = ctx.enter_context(nc.psum_tensor("mw_pt", [P, 2, 512], F32))
        s_raw = [sem(f"s_raw{i}") for i in range(3)]
        s_ident = sem("s_ident")
        s_amax = sem("s_amax")
        s_step = sem("s_step")
        s_rstep = sem("s_rstep")
        s_wi = sem("s_wi")
        s_wq = sem("s_wq")
        s_pt = sem("s_pt")
        s_hi = sem("s_hi")
        s_lo = sem("s_lo")
        s_down = [sem("s_down0"), sem("s_down1")]
        s_passed = sem("s_passed")
        s_passed_act = sem("s_passed_act")
        units = [(m, c) for c in range(3) for m in range(3)]
        block = ctx.enter_context(nc.Block())

        def store(sp, b, n, c):
            passed(sp, s_lo, b * NU + n + 3, s_passed)
            for part, src in enumerate((down_hi, down_lo)):
                dst = spill["down"][part, :, 4 * c:4 * c + 4, bass.ds(b * P, P)]
                sp.dma_start(dst, f32(src[:, c % 2])).then_inc(s_down[c % 2], 16)

        def spread(a):
            return a.rearrange("p (k o) -> p k o", o=1).to_broadcast([P, NB, QBLOCK])

        def where(b, m, c):
            if m == 2:
                return down_hi[:, c % 2], down_lo[:, c % 2]
            cut = bass.ds(b * (3 * P) + c * P, P)
            return w_hi[:, m, :, cut], w_lo[:, m, :, cut]

        @block.sync
        def _(sp):
            sp.dma_start(ident[:], ident_in).then_inc(s_ident, 16)
            with sp.Fori(0, RB) as b:
                for n, (m, c) in enumerate(units):
                    passed(sp, s_wi, b * NU + n + 1, s_passed)
                    if m < 2:
                        src = weights[m][bass.ds(b * (3 * P) + c * P, P), :]
                    else:
                        src = weights[2][bass.ds(b * P, P), c * D:(c + 1) * D]
                    sp.dma_start(raw[:, n % 3, :], src).then_inc(s_raw[n % 3], 16)
                    if n == 5:
                        store(sp, b, 2, 0)
                store(sp, b, 5, 1)
                store(sp, b, 8, 2)
            sp.wait_ge(s_down[0], 16 * 2 * (2 * RB + 1))
            sp.wait_ge(s_down[1], 16 * 2 * (RB + 1))

        @block.vector
        def _(dve):
            dve.sem_inc(s_wi, 3)
            dve.sem_inc(s_lo, 2)
            dve.sem_inc(s_down[0], 32)
            dve.sem_inc(s_down[1], 32)
            with dve.Fori(0, RB) as b:
                def split(n):
                    m, c = units[n]
                    dve.wait_ge(s_hi, b * NU + n + 1)
                    hi, lo = where(b, m, c)
                    dve.tensor_tensor(lo, pt[:, n % 2, :].rearrange("p (d o) -> p d o", d=DT), f32(hi),
                                      ALU.subtract).then_inc(s_lo, 1)

                for n, (m, c) in enumerate(units):
                    u, i = n % 2, b * NU + n + 1
                    v = raw[:, n % 3, :].rearrange("p (k s) -> p k s", s=QBLOCK)
                    dve.wait_ge(s_raw[n % 3], (b * 3 + n // 3 + 1) * 16)
                    dve.tensor_reduce(amax[:, u, :], v, AX.X, ALU.max, apply_absolute_value=True).then_inc(s_amax, 1)
                    dve.wait_ge(s_amax, i)
                    dve.tensor_scalar(step[:, u, :], amax[:, u, :], 1.0 / QMAX_W, SCALE_MIN,
                                      ALU.mult, ALU.max).then_inc(s_step, 1)
                    dve.wait_ge(s_step, i)
                    dve.reciprocal(rstep[:, u, :], step[:, u, :]).then_inc(s_rstep, 1)
                    dve.wait_ge(s_rstep, i)
                    dve.tensor_tensor(wi[:, u, :].rearrange("p (k s) -> p k s", s=QBLOCK), v,
                                      spread(rstep[:, u, :]), ALU.mult).then_inc(s_wi, 1)
                    dve.wait_ge(s_wi, i + 3)
                    if n >= 2:
                        dve.wait_ge(s_pt, b * NU + n - 1)
                    dve.tensor_tensor(wq[:, u, :].rearrange("p (k s) -> p k s", s=QBLOCK),
                                      wi[:, u, :].rearrange("p (k s) -> p k s", s=QBLOCK),
                                      spread(step[:, u, :]), ALU.mult).then_inc(s_wq, 1)
                    if n >= 1:
                        split(n - 1)
                split(NU - 1)

        @block.tensor
        def _(pe):
            pe.wait_ge(s_ident, 16)
            with pe.Fori(0, RB) as b:
                for n in range(NU):
                    pe.wait_ge(s_wq, b * NU + n + 1)
                    pe.wait_ge(s_lo, b * NU + n + 1)
                    for d in range(DT):
                        mm = pe.transpose(pt[:, n % 2, d * P:(d + 1) * P], wq[:, n % 2, d * P:(d + 1) * P], ident[:])
                    mm.then_inc(s_pt, 1)

        @block.scalar
        def _(act):
            with act.Fori(0, RB) as b:
                for n, (m, c) in enumerate(units):
                    if m == 2:
                        before = b * 2 + c // 2 + 1 if c % 2 == 0 else b + 1
                        act.wait_ge(s_down[c % 2], before * 32)
                    passed(act, s_pt, b * NU + n + 1, s_passed_act)
                    hi, _ = where(b, m, c)
                    act.activation(hi, pt[:, n % 2, :].rearrange("p (d o) -> p d o", d=DT), ACT.Copy).then_inc(s_hi, 1)


def mlp_inner(nc, h_in, hmax_in, ident, w_hi, w_lo, spill, scale, inv, peak, peak_all, find_scale):
    with ExitStack() as ctx:
        def sb(name, shape, dt=F32):
            return ctx.enter_context(nc.sbuf_tensor("mi_" + name, shape, dt))

        sem = stage_semaphores(nc, ctx, "mi_")

        h_tile = sb("h_tile", [P, 2, D])
        h_int = sb("h_int", [P, 2, D], I16)
        h_q = sb("h_q", [P, 2, D])
        ht_hi = sb("ht_hi", [P, DT, S], F32R)
        ht_lo = sb("ht_lo", [P, DT, S], F32R)
        out = sb("out", [P, 2, 4, S])
        peaks = sb("peaks", [P, 2, B * IT])
        pt = ctx.enter_context(nc.psum_tensor("mi_pt", [P, 2, 512], F32))
        pm = ctx.enter_context(nc.psum_tensor("mi_pm", [P, 4, 512], F32))
        s_peak_in = sem("s_peak_in")
        s_all = sem("s_all")
        s_link = sem("s_link")
        s_h_in = [sem("s_h_in0"), sem("s_h_in1")]
        s_int = sem("s_int")
        s_q = sem("s_q")
        s_pt = sem("s_pt")
        s_hi = sem("s_hi")
        s_lo = sem("s_lo")
        s_pm = sem("s_pm")
        s_out = sem("s_out")
        s_peak = sem("s_peak")
        s_store = [sem("s_store0"), sem("s_store1")]
        s_passed = sem("s_passed")
        s_fin = sem("s_fin")
        NM = 2 * IT
        NC = NM // 4
        tiles = [(m, 4 * c + k) for c in range(IT // 4) for m in range(2) for k in range(4)]
        block = ctx.enter_context(nc.Block())

        def hi(act, b, t):
            act.wait_ge(s_pt, b * ST + t + 1)
            act.activation(ht_hi[:, :, t * P:(t + 1) * P], pt[:, t % 2, :].rearrange("p (d t) -> p d t", d=DT),
                           ACT.Copy).then_inc(s_hi, 1)

        def lo(dve, b, t):
            dve.wait_ge(s_hi, b * ST + t + 1)
            dve.tensor_tensor(ht_lo[:, :, t * P:(t + 1) * P], pt[:, t % 2, :].rearrange("p (d t) -> p d t", d=DT),
                              f32(ht_hi[:, :, t * P:(t + 1) * P]), ALU.subtract).then_inc(s_lo, 1)

        @block.sync
        def _(sp):
            sp.dma_start(peak[:, 0:1], hmax_in).then_inc(s_peak_in, 16)

            def load(b, t):
                passed(sp, s_int, b * ST + t + 1, s_passed)
                sp.dma_start(h_tile[:, t % 2, :], h_in[b, t * P:(t + 1) * P, :]).then_inc(s_h_in[t % 2], 16)

            with sp.Fori(0, B) as b:
                for t in range(ST):
                    load(b, t)
                for c in range(NC):
                    passed(sp, s_peak, b * NM + 4 * c + 4, s_passed)
                    m, i = tiles[4 * c]
                    sp.dma_start(spill["raw"][m][b * (IT // 4) + i // 4], out[:, c % 2]).then_inc(s_store[c % 2], 16)
            for u in range(2):
                sp.wait_ge(s_store[u], 16 * (B * NC // 2 + 1))

        @block.scalar
        def _(act):
            with act.Fori(0, B) as b:
                for t in range(ST):
                    act.wait_ge(s_int, b * ST + t + 3)
                    if t >= 2:
                        act.wait_ge(s_pt, b * ST + t - 1)
                    act.activation(h_q[:, t % 2, :], h_int[:, t % 2, :], ACT.Copy).then_inc(s_q, 1)
                    if t >= 1:
                        hi(act, b, t - 1)
                hi(act, b, ST - 1)
                for n in range(NM):
                    act.wait_ge(s_pm, b * NM + n + 1)
                    if n % 4 == 0:
                        act.wait_ge(s_store[n // 4 % 2], (b * (NC // 2) + n // 8 + 1) * 16)
                    act.activation(out[:, n // 4 % 2, n % 4, :], pm[:, n % 4, :], ACT.Copy).then_inc(s_out, 1)

        @block.gpsimd
        def _(pool):
            pool.wait_ge(s_peak_in, 16)
            pool.partition_all_reduce(peak_all[:, 0:1], peak[:, 0:1], P, bass.bass_isa.ReduceOp.max).then_inc(s_all, 1)
            pool.wait_ge(s_fin, 2)
            pool.partition_all_reduce(peak_all[:], peak[:], P, bass.bass_isa.ReduceOp.max).then_inc(s_all, 1)

        @block.vector
        def _(dve):
            chain = [0]

            def link(ins):
                chain[0] += 1
                ins.then_inc(s_link, 1)
                dve.wait_ge(s_link, chain[0])

            dve.sem_inc(s_int, 2)
            dve.sem_inc(s_lo, 2)
            dve.sem_inc(s_store[0], 16)
            dve.sem_inc(s_store[1], 16)
            dve.wait_ge(s_all, 1)
            find_scale(dve, link, "h", peak_all[:, 0:1], None)
            with dve.Fori(0, B) as b:
                for t in range(ST):
                    dve.wait_ge(s_h_in[t % 2], (b * (ST // 2) + t // 2 + 1) * 16)
                    if t >= 2:
                        dve.wait_ge(s_q, b * ST + t - 1)
                    dve.tensor_scalar(h_int[:, t % 2, :], h_tile[:, t % 2, :], inv["h"][:], None,
                                      ALU.mult).then_inc(s_int, 1)
                    if t >= 1:
                        lo(dve, b, t - 1)
                lo(dve, b, ST - 1)
                for n, (m, i) in enumerate(tiles):
                    dve.wait_ge(s_out, b * NM + n + 1)
                    dve.tensor_reduce(peaks[:, m, bass.ds(b * IT + i, 1)], out[:, n // 4 % 2, n % 4, :], AX.X, ALU.max,
                                      apply_absolute_value=True).then_inc(s_peak, 1)
            dve.wait_ge(s_peak, B * NM)
            for m in range(2):
                dve.tensor_reduce(peak[:, m:m + 1], peaks[:, m, :], AX.X, ALU.max).then_inc(s_fin, 1)
            dve.wait_ge(s_all, 2)
            find_scale(dve, link, "gate", peak_all[:, 0:1], scale["h"][:])
            find_scale(dve, link, "up", peak_all[:, 1:2], scale["h"][:])

        @block.tensor
        def _(pe):
            with pe.Fori(0, B) as b:
                for t in range(ST):
                    pe.wait_ge(s_q, b * ST + t + 1)
                    pe.wait_ge(s_lo, b * ST + t + 1)
                    for d in range(DT):
                        mm = pe.transpose(pt[:, t % 2, d * P:(d + 1) * P], h_q[:, t % 2, d * P:(d + 1) * P], ident[:])
                    mm.then_inc(s_pt, 1)
                pe.wait_ge(s_lo, b * ST + ST + 2)
                for n, (m, i) in enumerate(tiles):
                    if n >= 4:
                        pe.wait_ge(s_out, b * NM + n - 3)
                    cut = slice(i * P, (i + 1) * P)
                    for d in range(DT):
                        ops = ((w_hi, ht_hi), (w_hi, ht_lo), (w_lo, ht_hi))
                        for p, (w, h) in enumerate(ops):
                            mm = pe.matmul(pm[:, n % 4, :], w[:, m, d, cut], h[:, d, :],
                                           start=(d == 0 and p == 0), stop=(d == DT - 1 and p == 2))
                    mm.then_inc(s_pm, 1)


def sigmoid_u16(dve, sig, out):
    return dve.tensor_scalar(out, sig, SIG_ONE, SIG_ONE - 1.0, ALU.mult, ALU.min)


def mlp_silu(nc, spill, silu_q, scale, inv, peak, peak_all, mix, find_scale):
    with ExitStack() as ctx:
        def sb(name, shape, dt=F32):
            return ctx.enter_context(nc.sbuf_tensor("ms_" + name, shape, dt))

        sem = stage_semaphores(nc, ctx, "ms_")

        W = 4 * S
        raw = sb("raw", [P, 2, W])
        sig = sb("sig", [P, 2, W])
        sig_q = sb("sig_q", [P, 2, W], U16)
        gabs = sb("gabs", [P, 2, W], I16)
        prod = sb("prod", [P, W])
        quad_peak = sb("quad_peak", [P, 2])
        s_raw = [sem("s_raw0"), sem("s_raw1")]
        s_int = sem("s_int")
        s_sig = sem("s_sig")
        s_abs = sem("s_abs")
        s_sig_q = sem("s_sig_q")
        s_peak = sem("s_peak")
        s_all = sem("s_all")
        s_link = sem("s_link")
        s_passed = sem("s_passed")
        s_passed_act = sem("s_passed_act")
        s_passed_dve = sem("s_passed_dve")
        s_top = sem("s_top")
        LAST = NQ // 2 - 1
        block = ctx.enter_context(nc.Block())

        @block.sync
        def _(sp):
            with sp.Fori(0, NQ // 2) as i:
                for u in range(2):
                    passed(sp, s_int, i * 2 + u + 1, s_passed)
                    sp.dma_start(raw[:, u].rearrange("p (k t) -> p k t", k=4), spill["raw"][0][i * 2 + u]).then_inc(s_raw[u], 16)

        @block.scalar
        def _(act):
            with act.Fori(0, NQ // 2) as i:
                for u in range(2):
                    n = i * 2 + u
                    q = silu_q[:, bass.ds(n, 1), :].rearrange("p o w -> p (o w)")
                    act.wait_ge(s_sig_q, n + 1)
                    passed(act, s_int, n + 3, s_passed_act)
                    act.activation(sig[:, u], q, ACT.Sigmoid, scale=scale["gate"][:]).then_inc(s_sig, 1)
                    passed(act, s_peak, n + 1, s_passed_act)
                    act.activation(gabs[:, u], q, ACT.Abs).then_inc(s_abs, 1)

        @block.vector
        def _(dve):
            chain = [0]

            def link(ins):
                chain[0] += 1
                ins.then_inc(s_link, 1)
                dve.wait_ge(s_link, chain[0])

            def to_int(i, u, n):
                dve.wait_ge(s_raw[u], (i + 1) * 16)
                dve.tensor_scalar(silu_q[:, bass.ds(n, 1), :].rearrange("p o w -> p (o w)"), raw[:, u],
                                  inv["gate"][:], None, ALU.mult).then_inc(s_int, 1)

            def body(i, last):
                for u in range(2):
                    n = i * 2 + u
                    if not (last and u == 1):
                        to_int(i + u, 1 - u, n + 1)
                    dve.wait_ge(s_sig, n + 1)
                    sigmoid_u16(dve, sig[:, u], sig_q[:, u]).then_inc(s_sig_q, 1)
                    dve.wait_ge(s_sig_q, n + 3)
                    passed(dve, s_abs, n + 1, s_passed_dve)
                    dve.tensor_tensor_reduce(prod[:], gabs[:, u], sig_q[:, u], 1.0, 0.0, ALU.mult, ALU.max,
                                             quad_peak[:, u:u + 1]).then_inc(s_peak, 1)
                    dve.wait_ge(s_peak, n + 3)
                    dve.wait_ge(s_top, n + 1)
                    dve.tensor_tensor(peak[:, 0:1], peak[:, 0:1], quad_peak[:, u:u + 1], ALU.max).then_inc(s_top, 1)

            for s in (s_int, s_sig_q, s_peak):
                dve.sem_inc(s, 2)
            dve.memset(peak[:, 0:1], 0.0).then_inc(s_top, 1)
            to_int(0, 0, 0)
            with dve.Fori(0, LAST) as i:
                body(i, False)
            body(LAST, True)
            dve.wait_ge(s_all, 1)
            link(dve.tensor_scalar(mix[:, 0:1], scale["gate"][:], 1.0 / SIG_ONE, None, ALU.mult))
            find_scale(dve, link, "silu", peak_all[:, 0:1], mix[:, 0:1])

        @block.gpsimd
        def _(pool):
            pool.wait_ge(s_top, NQ + 1)
            pool.partition_all_reduce(peak_all[:, 0:1], peak[:, 0:1], P, bass.bass_isa.ReduceOp.max).then_inc(s_all, 1)


def mlp_product(nc, spill, silu_q, scale, inv, peak, peak_all, mix, find_scale):
    with ExitStack() as ctx:
        def sb(name, shape, dt=F32):
            return ctx.enter_context(nc.sbuf_tensor("mp_" + name, shape, dt))

        sem = stage_semaphores(nc, ctx, "mp_")

        W = 4 * S
        raw = sb("raw", [P, 2, W])
        sig = sb("sig", [P, 2, W])
        sig_q = sb("sig_q", [P, W], U16)
        silu = sb("silu", [P, W])
        uabs = sb("uabs", [P, 2, W], I16)
        sabs = sb("sabs", [P, 2, W], I16)
        prod = sb("prod", [P, W])
        quad_peak = sb("quad_peak", [P, 2])
        s_raw = [sem("s_raw0"), sem("s_raw1")]
        s_sig = sem("s_sig")
        s_sig_q = sem("s_sig_q")
        s_silu = sem("s_silu")
        s_int = sem("s_int")
        s_uabs = sem("s_uabs")
        s_sabs = sem("s_sabs")
        s_peak = sem("s_peak")
        s_all = sem("s_all")
        s_link = sem("s_link")
        s_passed = sem("s_passed")
        s_passed_act = sem("s_passed_act")
        s_passed_dve = sem("s_passed_dve")
        s_top = sem("s_top")
        LAST = NQ // 2 - 1
        block = ctx.enter_context(nc.Block())

        def quad(n):
            return silu_q[:, bass.ds(n, 1), :].rearrange("p o w -> p (o w)")

        @block.sync
        def _(sp):
            with sp.Fori(0, NQ // 2) as i:
                for u in range(2):
                    passed(sp, s_uabs, i * 2 + u + 1, s_passed)
                    sp.dma_start(raw[:, u].rearrange("p (k t) -> p k t", k=4), spill["raw"][1][i * 2 + u]).then_inc(s_raw[u], 16)

        @block.scalar
        def _(act):
            def sigmoid(u, n):
                passed(act, s_sig_q, n + 1, s_passed_act)
                act.activation(sig[:, u], quad(n), ACT.Sigmoid, scale=scale["gate"][:]).then_inc(s_sig, 1)

            def body(i, last):
                for u in range(2):
                    n = i * 2 + u
                    if not (last and u == 1):
                        sigmoid(1 - u, n + 1)
                    act.wait_ge(s_raw[u], (i + 1) * 16)
                    act.wait_ge(s_peak, n + 1)
                    act.activation(uabs[:, u], raw[:, u], ACT.Abs, scale=inv["up"][:]).then_inc(s_uabs, 1)
                    passed(act, s_int, n + 1, s_passed_act)
                    act.activation(sabs[:, u], quad(n), ACT.Abs).then_inc(s_sabs, 1)

            act.wait_ge(s_uabs, 2)
            sigmoid(0, 0)
            with act.Fori(0, LAST) as i:
                body(i, False)
            body(LAST, True)

        @block.vector
        def _(dve):
            chain = [0]

            def link(ins):
                chain[0] += 1
                ins.then_inc(s_link, 1)
                dve.wait_ge(s_link, chain[0])

            def measure(u, n):
                dve.wait_ge(s_uabs, n + 3)
                passed(dve, s_sabs, n + 1, s_passed_dve)
                dve.tensor_tensor_reduce(prod[:], sabs[:, u], uabs[:, u], 1.0, 0.0, ALU.mult, ALU.max,
                                         quad_peak[:, u:u + 1]).then_inc(s_peak, 1)
                dve.wait_ge(s_peak, n + 3)
                dve.wait_ge(s_top, n + 1)
                dve.tensor_tensor(peak[:, 0:1], peak[:, 0:1], quad_peak[:, u:u + 1], ALU.max).then_inc(s_top, 1)

            def to_silu(u, n):
                dve.wait_ge(s_sig, n + 1)
                sigmoid_u16(dve, sig[:, u], sig_q[:]).then_inc(s_sig_q, 1)
                dve.wait_ge(s_sig_q, n + 3)
                dve.tensor_tensor(silu[:], quad(n), sig_q[:], ALU.mult).then_inc(s_silu, 1)
                dve.wait_ge(s_silu, n + 1)
                dve.tensor_scalar(quad(n), silu[:], inv["silu"][:], None, ALU.mult).then_inc(s_int, 1)

            def body(i, last):
                for u in range(2):
                    n = i * 2 + u
                    if not (last and u == 1):
                        to_silu(1 - u, n + 1)
                    measure(u, n)

            for s in (s_sig_q, s_peak, s_uabs):
                dve.sem_inc(s, 2)
            dve.memset(peak[:, 0:1], 0.0).then_inc(s_top, 1)
            to_silu(0, 0)
            with dve.Fori(0, LAST) as i:
                body(i, False)
            body(LAST, True)
            dve.wait_ge(s_all, 1)
            link(dve.tensor_tensor(mix[:, 0:1], scale["silu"][:], scale["up"][:], ALU.mult))
            find_scale(dve, link, "out", peak_all[:, 0:1], mix[:, 0:1])

        @block.gpsimd
        def _(pool):
            pool.wait_ge(s_top, NQ + 1)
            pool.partition_all_reduce(peak_all[:, 0:1], peak[:, 0:1], P, bass.bass_isa.ReduceOp.max).then_inc(s_all, 1)


def mlp_down(nc, spill, silu_q, x_in, x_out, gate, scale, inv):
    with ExitStack() as ctx:
        def sb(name, shape, dt=F32):
            return ctx.enter_context(nc.sbuf_tensor("md_" + name, shape, dt))

        sem = stage_semaphores(nc, ctx, "md_")

        W = 2 * S
        NP = IT // 2
        wd = [sb("wd_hi", [P, IT, D], F32R), sb("wd_lo", [P, IT, D], F32R)]
        raw = sb("raw", [P, 2, W])
        up_q = sb("up_q", [P, W], I16)
        prod = sb("prod", [P, W])
        prod_q = sb("prod_q", [P, 2, W], I16)
        p_hi = sb("p_hi", [P, 2, 2, S], F32R)
        p_lo = sb("p_lo", [P, 2, 2, S], F32R)
        x_new = sb("x_new", [P, 2, D])
        gate_col = sb("gate_col", [P, 1])
        tanh_g = sb("tanh_g", [P, 1])
        factor = sb("factor", [P, 1])
        pd = ctx.enter_context(nc.psum_tensor("md_pd", [P, 2, ST, 512], F32))
        s_wd = sem("s_wd")
        s_gate = sem("s_gate")
        s_raw = [sem("s_raw0"), sem("s_raw1")]
        s_up = sem("s_up")
        s_prod = sem("s_prod")
        s_int = sem("s_int")
        s_hi = sem("s_hi")
        s_lo = sem("s_lo")
        s_used = sem("s_used")
        s_x = [sem("s_x0"), sem("s_x1")]
        s_new = sem("s_new")
        s_store = [sem("s_store0"), sem("s_store1")]
        s_tanh = sem("s_tanh")
        s_factor = sem("s_factor")
        s_passed = sem("s_passed")
        block = ctx.enter_context(nc.Block())

        def store(sp, b, t):
            passed(sp, s_new, b * ST + t + 1 + 2 * ST, s_passed)
            sp.dma_start(x_out[b, t * P:(t + 1) * P, :], x_new[:, t % 2, :]).then_inc(s_store[t % 2], 16)

        @block.sync
        def _(sp):
            for part in range(2):
                sp.dma_start(f32(wd[part][:]), spill["down"][part]).then_inc(s_wd, 16)
            sp.dma_start(gate_col[:], gate).then_inc(s_gate, 16)

            with sp.Fori(0, B // 2) as bb:
                for v in range(2):
                    b = bb * 2 + v
                    for c in range(NP):
                        passed(sp, s_up, b * NP + c + 1, s_passed)
                        sp.dma_start(raw[:, c % 2].rearrange("p (k t) -> p k t", k=2),
                                     spill["raw"][1][b * (NP // 2) + c // 2][:, 2 * (c % 2):2 * (c % 2) + 2, :]
                                     ).then_inc(s_raw[c % 2], 16)
                    for t in range(ST):
                        passed(sp, s_store[t % 2], (b * 2 + t // 2 + 1) * 16, s_passed)
                        sp.dma_start(x_new[:, t % 2, :], x_in[b, t * P:(t + 1) * P, :]).then_inc(s_x[t % 2], 16)
                        if t >= 1:
                            store(sp, b, t - 1)
                    store(sp, b, ST - 1)
            for u in range(2):
                sp.wait_ge(s_store[u], 16 * (B * 2 + 1))

        @block.scalar
        def _(act):
            act.wait_ge(s_gate, 16)
            act.activation(tanh_g[:], gate_col[:], ACT.Tanh).then_inc(s_tanh, 1)
            with act.Fori(0, B // 2) as bb:
                for v in range(2):
                    for c in range(NP):
                        n = bb * (2 * NP) + v * NP + c
                        act.wait_ge(s_int, n + 1)
                        act.wait_ge(s_used, n + 1)
                        act.activation(p_hi[:, c % 2].rearrange("p k t -> p (k t)"), prod_q[:, c % 2], ACT.Copy).then_inc(s_hi, 1)

        @block.vector
        def _(dve):
            dve.sem_inc(s_up, 2)
            dve.sem_inc(s_used, 2)
            dve.sem_inc(s_new, 2 * ST)
            dve.sem_inc(s_store[0], 16)
            dve.sem_inc(s_store[1], 16)
            dve.wait_ge(s_tanh, 1)
            dve.tensor_tensor(factor[:], tanh_g[:], scale["out"][:], ALU.mult).then_inc(s_factor, 1)
            dve.wait_ge(s_factor, 1)
            with dve.Fori(0, B // 2) as bb:
                for v in range(2):
                    def to_lo(c):
                        dve.wait_ge(s_hi, bb * (2 * NP) + v * NP + c + 1)
                        dve.tensor_tensor(p_lo[:, c % 2].rearrange("p k t -> p (k t)"), prod_q[:, c % 2],
                                          f32(p_hi[:, c % 2]).rearrange("p k t -> p (k t)"), ALU.subtract).then_inc(s_lo, 1)

                    for c in range(NP):
                        n = bb * (2 * NP) + v * NP + c
                        i = n + 1
                        q = silu_q[:, bass.ds(bb * NP + v * (NP // 2) + c // 2, 1), (c % 2) * W:(c % 2 + 1) * W].rearrange("p o w -> p (o w)")
                        dve.wait_ge(s_raw[c % 2], (bb * NP + v * (NP // 2) + c // 2 + 1) * 16)
                        dve.tensor_scalar(up_q[:], raw[:, c % 2], inv["up"][:], None, ALU.mult).then_inc(s_up, 1)
                        dve.wait_ge(s_up, i + 2)
                        dve.tensor_tensor(prod[:], q, up_q[:], ALU.mult).then_inc(s_prod, 1)
                        dve.wait_ge(s_prod, i)
                        dve.tensor_scalar(prod_q[:, c % 2], prod[:], inv["out"][:], None, ALU.mult).then_inc(s_int, 1)
                        if c >= 1:
                            to_lo(c - 1)
                    to_lo(NP - 1)
                    for t in range(ST):
                        b = bb * 2 + v
                        dve.wait_ge(s_x[t % 2], (b * 2 + t // 2 + 1) * 16)
                        dve.wait_ge(s_used, (b + 1) * NP + 2)
                        dve.scalar_tensor_tensor(x_new[:, t % 2, :], pd[:, v, t, :], factor[:], x_new[:, t % 2, :],
                                                 ALU.mult, ALU.add).then_inc(s_new, 1)

        @block.tensor
        def _(pe):
            pe.wait_ge(s_wd, 32)
            with pe.Fori(0, B // 2) as bb:
                for v in range(2):
                    for c in range(NP):
                        pe.wait_ge(s_lo, bb * (2 * NP) + v * NP + c + 1)
                        if c == 0:
                            pe.wait_ge(s_new, bb * (2 * ST) + (v + 1) * ST)
                        for t in range(ST):
                            cut = slice(t * P, (t + 1) * P)
                            for k in range(2):
                                i = 2 * c + k
                                ops = ((p_hi, 0), (p_hi, 1), (p_lo, 0))
                                for p, (lhs, part) in enumerate(ops):
                                    mm = pe.matmul(pd[:, v, t, :], lhs[:, c % 2, k, cut], wd[part][:, i, :],
                                                   start=(i == 0 and p == 0), stop=(i == IT - 1 and p == 2))
                        mm.then_inc(s_used, 1)


E_N = 8
TOP = 2
F = 1024
FT = F // P
CAP = max(1, -(-5 * T * TOP // (4 * E_N)))
SLOTS = E_N * CAP
CT = 5
CW = CT * P
CHUNKS = SLOTS // CW
CE = CHUNKS // E_N
WEIGHT_MIN = 1e-9


def mixture(nc, h_in, x_in, x_out, router_w, router_b, w1, w2, b1, b2, gate, consts, spill):
    with ExitStack() as whole:
        def keep(name, shape, dt=F32):
            return whole.enter_context(nc.sbuf_tensor("x_" + name, shape, dt))

        token_of = keep("token_of", [P, SLOTS // P + CT], I32)
        slot_of = keep("slot_of", [P, NT, TOP], I32)
        weight = keep("weight", [P, NT, TOP])
        route(nc, h_in, router_w, router_b, gate, consts, spill["tokens"], token_of, slot_of, weight)
        experts(nc, h_in, w1, w2, b1, b2, consts["ident"], token_of, spill["expert_out"])
        combine(nc, spill["expert_out"], x_in, x_out, slot_of, weight)


def route(nc, h_in, router_w, router_b, gate, consts, tokens, token_of, slot_of, weight):
    with ExitStack() as ctx:
        def sb(name, shape, dt=F32):
            return ctx.enter_context(nc.sbuf_tensor("r_" + name, shape, dt))

        def ps(name, shape):
            return ctx.enter_context(nc.psum_tensor("r_" + name, shape, F32))

        sem = stage_semaphores(nc, ctx, "r_")

        h = sb("h", [P, 2, ST, D])
        h_t = sb("h_t", [P, 2, D])
        rw = sb("rw", [P, DT, E_N])
        rb = sb("rb", [P, E_N])
        ident = sb("ident", [P, P])
        before = sb("before", [P, P])
        ones = sb("ones", [P, P])
        expert = sb("expert", [P, NT, E_N])
        spare = sb("spare", [P, NT, TOP])
        token_id = sb("token_id", [P, NT], I32)
        gate_col = sb("gate_col", [P, 1])
        tanh_g = sb("tanh_g", [P, 1])
        zeros = sb("zeros", [P, (SLOTS + T * TOP) // P], I32)
        prob = sb("prob", [P, NT, E_N])
        row = sb("row", [P, NT])
        top_p = sb("top_p", [P, NT, 8])
        top_i = sb("top_i", [P, NT, 8], U32)
        top_e = sb("top_e", [P, NT, TOP])
        hot = [sb("hot0", [P, NT, E_N]), sb("hot1", [P, NT, E_N])]
        taken = sb("taken", [P, NT, E_N])
        base = [sb("base0", [P, NT, E_N]), sb("base1", [P, NT, E_N])]
        rank = sb("rank", [P, NT, TOP])
        kept = sb("kept", [P, NT, TOP])
        cell = sb("cell", [P, NT, TOP])
        put_at = sb("put_at", [P, NT, TOP], I32)
        table = sb("table", [SLOTS // P, P], I32)
        table_f = sb("table_f", [SLOTS // P, P])
        pt = ps("pt", [P, 2, 512])
        pl = ps("pl", [P, 2, 512])
        pr = ps("pr", [P, 2, 512])
        pk = ps("pk", [P, 512])
        s_const = sem("s_const")
        s_h = [sem("s_h0"), sem("s_h1")]
        s_pt = sem("s_pt")
        s_ht = sem("s_ht")
        s_logit = sem("s_logit")
        s_prob = sem("s_prob")
        s_link = sem("s_link")
        s_exp_in = sem("s_exp_in")
        s_exp = sem("s_exp")
        s_tanh = sem("s_tanh")
        s_taken = sem("s_taken")
        s_count = sem("s_count")
        s_put_at = sem("s_put_at")
        s_zero = sem("s_zero")
        s_zeroed = sem("s_zeroed")
        s_put = sem("s_put")
        s_table = sem("s_table")
        s_table_f = sem("s_table_f")
        s_turned = sem("s_turned")
        s_token_of = sem("s_token_of")
        s_passed = sem("s_passed")
        s_passed_dve = sem("s_passed_dve")
        NCONST = 8 * 16
        block = ctx.enter_context(nc.Block())

        def over_experts(a):
            return a.rearrange("p (t o) -> p t o", o=1).to_broadcast([P, NT, E_N])

        @block.sync
        def _(sp):
            for dst, src in ((ident, consts["ident"]), (before, consts["before"]), (expert, consts["expert"]),
                             (spare, consts["spare"]), (token_id, consts["token_id"]), (rw, router_w),
                             (rb, router_b), (gate_col, gate)):
                sp.dma_start(dst[:], src).then_inc(s_const, 16)
            sp.wait_ge(s_zero, 1)
            sp.dma_start(tokens.rearrange("(p n) o -> p (n o)", p=P), zeros[:]).then_inc(s_zeroed, 16)
            with sp.Fori(0, B // 2) as bb:
                for v in range(2):
                    passed(sp, s_pt, (bb * 2 + v + 1) * ST, s_passed)
                    sp.dma_start(h[:, v], h_in[bb * 2 + v].rearrange("(t p) d -> p t d", p=P)).then_inc(s_h[v], 16)
            sp.wait_ge(s_put, TOP * NT * 16)
            sp.dma_start(table[:], tokens[0:SLOTS].rearrange("(n p) o -> n (p o)", p=P)).then_inc(s_table, 16)

        @block.scalar
        def _(act):
            act.wait_ge(s_const, NCONST)
            act.activation(tanh_g[:], gate_col[:], ACT.Tanh).then_inc(s_tanh, 1)
            with act.Fori(0, B // 2) as bb:
                for n in range(2 * ST):
                    i = bb * (2 * ST) + n
                    act.wait_ge(s_pt, i + 1 + 2 * ST)
                    act.wait_ge(s_logit, i + 1)
                    act.activation(h_t[:, n % 2, :], pt[:, n % 2, :], ACT.Copy).then_inc(s_ht, 1)
            act.wait_ge(s_exp_in, 1)
            act.activation(prob[:], prob[:], ACT.Exp).then_inc(s_exp, 1)

        @block.tensor
        def _(pe):
            def logits(bb, n):
                i = bb * (2 * ST) + n
                v, t = n // ST, n % ST
                if t == 0:
                    pe.wait_ge(s_prob, bb * 2 + v + 1)
                pe.wait_ge(s_ht, i + 3)
                for d in range(DT):
                    mm = pe.matmul(pl[:, v, t * E_N:(t + 1) * E_N], h_t[:, n % 2, d * P:(d + 1) * P], rw[:, d, :],
                                   start=(d == 0), stop=(d == DT - 1))
                mm.then_inc(s_logit, 1)

            pe.wait_ge(s_const, NCONST)
            with pe.Fori(0, B // 2) as bb:
                for n in range(2 * ST):
                    v, t = n // ST, n % ST
                    if t == 0:
                        pe.wait_ge(s_h[v], (bb + 1) * 16)
                    pe.wait_ge(s_ht, bb * (2 * ST) + n + 1)
                    for d in range(DT):
                        mm = pe.transpose(pt[:, n % 2, d * P:(d + 1) * P], h[:, v, t, d * P:(d + 1) * P], ident[:])
                    mm.then_inc(s_pt, 1)
                    if n >= 1:
                        logits(bb, n - 1)
                logits(bb, 2 * ST - 1)
            pe.wait_ge(s_taken, 1)
            flat = taken[:].rearrange("p t e -> p (t e)")
            pe.matmul(pr[:, 0, :NT * E_N], before[:], flat, start=True, stop=True).then_inc(s_count, 1)
            pe.matmul(pr[:, 1, :NT * E_N], ones[:], flat, start=True, stop=True).then_inc(s_count, 1)
            pe.wait_ge(s_table_f, 1)
            pe.transpose(pk[:, :SLOTS // P], table_f[:], ident[:SLOTS // P, :SLOTS // P]).then_inc(s_turned, 1)

        @block.vector
        def _(dve):
            chain = [0]

            def link(ins):
                chain[0] += 1
                ins.then_inc(s_link, 1)
                dve.wait_ge(s_link, chain[0])

            dve.sem_inc(s_pt, 2 * ST)
            dve.sem_inc(s_ht, 2)
            dve.sem_inc(s_logit, 2)
            dve.sem_inc(s_prob, 2)
            dve.memset(zeros[:], 0).then_inc(s_zero, 1)
            link(dve.memset(ones[:], 1.0))
            dve.wait_ge(s_tanh, 1)
            with dve.Fori(0, B // 2) as bb:
                for v in range(2):
                    b = bb * 2 + v
                    dve.wait_ge(s_logit, (b + 1) * ST + 2)
                    dve.tensor_tensor(prob[:, bass.ds(b * ST, ST), :],
                                      pl[:, v, :ST * E_N].rearrange("p (t e) -> p t e", e=E_N),
                                      rb[:].rearrange("p (o e) -> p o e", o=1).to_broadcast([P, ST, E_N]),
                                      ALU.add).then_inc(s_prob, 1)
            dve.wait_ge(s_prob, B + 2)
            link(dve.tensor_reduce(row[:], prob[:], AX.X, ALU.max))
            dve.tensor_tensor(prob[:], prob[:], over_experts(row[:]), ALU.subtract).then_inc(s_exp_in, 1)
            dve.wait_ge(s_exp, 1)
            link(dve.tensor_reduce(row[:], prob[:], AX.X, ALU.add))
            link(dve.reciprocal(row[:], row[:]))
            link(dve.tensor_tensor(prob[:], prob[:], over_experts(row[:]), ALU.mult))
            for t in range(NT):
                ins = dve.max(top_p[:, t, :], prob[:, t, :])
            link(ins)
            for t in range(NT):
                ins = dve.max_index(top_i[:, t, :], top_p[:, t, :], prob[:, t, :])
            link(ins)
            link(dve.tensor_copy(top_e[:], top_i[:, :, 0:TOP]))
            for k in range(TOP):
                ins = dve.tensor_tensor(hot[k][:], expert[:], top_e[:, :, k:k + 1].to_broadcast([P, NT, E_N]),
                                        ALU.is_equal)
            link(ins)
            dve.tensor_tensor(taken[:], hot[0][:], hot[1][:], ALU.add).then_inc(s_taken, 1)
            link(dve.tensor_tensor(row[:], top_p[:, :, 0], top_p[:, :, 1], ALU.add))
            link(dve.tensor_scalar(row[:], row[:], WEIGHT_MIN, None, ALU.max))
            link(dve.reciprocal(row[:], row[:]))
            link(dve.tensor_scalar(row[:], row[:], tanh_g[:], None, ALU.mult))
            link(dve.tensor_tensor(weight[:], top_p[:, :, 0:TOP],
                                   row[:].rearrange("p (t o) -> p t o", o=1).to_broadcast([P, NT, TOP]), ALU.mult))
            dve.wait_ge(s_count, 2)
            link(dve.memset(base[0][:, 0:1, :], 0.0))
            link(dve.tensor_copy(base[0][:, 1:, :].rearrange("p t e -> p (t e)"), pr[:, 1, :(NT - 1) * E_N]))
            reach, u = 1, 0
            while reach < NT:
                old, new = base[u], base[1 - u]
                dve.tensor_copy(new[:, :reach, :], old[:, :reach, :])
                link(dve.tensor_tensor(new[:, reach:, :], old[:, reach:, :], old[:, :NT - reach, :], ALU.add))
                reach, u = 2 * reach, 1 - u
            ranks, spent = base[u], base[1 - u]
            link(dve.tensor_tensor(ranks[:].rearrange("p t e -> p (t e)"), ranks[:].rearrange("p t e -> p (t e)"),
                                   pr[:, 0, :NT * E_N], ALU.add))
            for k in range(TOP):
                link(dve.tensor_tensor(spent[:], hot[k][:], ranks[:], ALU.mult))
                link(dve.tensor_reduce(rank[:, :, k], spent[:], AX.X, ALU.add))
            link(dve.tensor_scalar(kept[:], rank[:], float(CAP), None, ALU.is_lt))
            link(dve.tensor_tensor(weight[:], weight[:], kept[:], ALU.mult))
            link(dve.scalar_tensor_tensor(cell[:], top_e[:], float(CAP), rank[:], ALU.mult, ALU.add))
            link(dve.tensor_tensor(cell[:], cell[:], spare[:], ALU.subtract))
            link(dve.tensor_tensor(cell[:], cell[:], kept[:], ALU.mult))
            link(dve.tensor_tensor(cell[:], cell[:], spare[:], ALU.add))
            dve.tensor_copy(put_at[:], cell[:]).then_inc(s_put_at, 1)
            link(dve.tensor_scalar(rank[:], rank[:], float(CAP - 1), None, ALU.min))
            dve.wait_ge(s_put_at, 1)
            link(dve.scalar_tensor_tensor(cell[:], top_e[:], float(CAP), rank[:], ALU.mult, ALU.add))
            link(dve.tensor_copy(slot_of[:], cell[:]))
            dve.wait_ge(s_table, 16)
            dve.tensor_copy(table_f[:], table[:]).then_inc(s_table_f, 1)
            dve.wait_ge(s_turned, 1)
            dve.tensor_copy(token_of[:, :SLOTS // P], pk[:, :SLOTS // P]).then_inc(s_token_of, 1)
            dve.memset(token_of[:, SLOTS // P:], 0).then_inc(s_token_of, 1)
            dve.wait_ge(s_token_of, 2)

        @block.gpsimd
        def _(pool):
            pool.wait_ge(s_zeroed, 16)
            pool.wait_ge(s_put_at, 1)
            for t in range(NT):
                for k in range(TOP):
                    pool.indirect_dma_start(tokens, bass.IndirectOffsetOnAxis(put_at[:, t, k:k + 1], 0),
                                            token_id[:, t:t + 1], None).then_inc(s_put, 16)


def experts(nc, h_in, w1, w2, b1, b2, ident_in, token_of, expert_out):
    rows = h_in.rearrange("b s d -> (b s) d")
    with ExitStack() as ctx:
        def sb(name, shape, dt=F32):
            return ctx.enter_context(nc.sbuf_tensor("e_" + name, shape, dt))

        sem = stage_semaphores(nc, ctx, "e_")

        HALF = CW // 2
        W2CUT = FT // 2
        raw1 = sb("raw1", [P, DT, F])
        raw2 = sb("raw2", [P, FT, D])
        w1_hi = sb("w1_hi", [P, DT, F], F32R)
        w1_lo = sb("w1_lo", [P, DT, F], F32R)
        w2_hi = sb("w2_hi", [P, FT, D], F32R)
        w2_lo = sb("w2_lo", [P, FT, D], F32R)
        b1_all = sb("b1_all", [P, E_N, FT])
        b1_col = sb("b1_col", [P, FT])
        b2_row = sb("b2_row", [P, D])
        ident = sb("ident", [P, P])
        index = sb("index", [P, 2, CT], I32)
        x = sb("x", [P, 2, CT, D])
        xt_hi = sb("xt_hi", [P, DT, CW], F32R)
        xt_lo = sb("xt_lo", [P, DT, CW], F32R)
        g = sb("g", [P, 2, CW])
        g_hi = sb("g_hi", [P, FT, CW], F32R)
        g_lo = sb("g_lo", [P, FT, CW], F32R)
        out = sb("out", [P, CT, D])
        pt = ctx.enter_context(nc.psum_tensor("e_pt", [P, 2, 512], F32))
        ph = ctx.enter_context(nc.psum_tensor("e_ph", [P, 2, 2, 512], F32))
        po = ctx.enter_context(nc.psum_tensor("e_po", [P, 2, 512], F32))
        s_const = sem("s_const")
        s_raw1 = sem("s_raw1")
        s_raw2 = sem("s_raw2")
        s_w1_hi = sem("s_w1_hi")
        s_w1_lo = sem("s_w1_lo")
        s_w2_hi = sem("s_w2_hi")
        s_w2_lo = sem("s_w2_lo")
        s_b1 = sem("s_b1")
        s_b2 = sem("s_b2")
        s_index = sem("s_index")
        s_x = [sem("s_x0"), sem("s_x1")]
        s_pt = sem("s_pt")
        s_xt_hi = sem("s_xt_hi")
        s_xt = sem("s_xt")
        s_ph = sem("s_ph")
        s_g = sem("s_g")
        s_g_hi = sem("s_g_hi")
        s_g_lo = sem("s_g_lo")
        s_po = sem("s_po")
        s_out = sem("s_out")
        s_store = sem("s_store")
        s_passed = sem("s_passed")
        s_passed_pool = sem("s_passed_pool")
        block = ctx.enter_context(nc.Block())

        def load(sp, e):
            first = isinstance(e, int)
            if not first:
                passed(sp, s_w1_lo, e, s_passed)
            sp.dma_start(raw1[:], w1[e]).then_inc(s_raw1, 16)
            if not first:
                passed(sp, s_w2_lo, 2 * e, s_passed)
            sp.dma_start(raw2[:], w2[e]).then_inc(s_raw2, 16)

        def load_b2(sp, e):
            passed(sp, s_out, e * (CE * CT) + 2, s_passed)
            sp.dma_start(b2_row[:], b2[bass.ds(e, 1), :].to_broadcast([P, D])).then_inc(s_b2, 16)

        def store(sp, e, c):
            passed(sp, s_out, (e * CE + c + 1) * CT + 2, s_passed)
            dst = expert_out[bass.ds(e * CAP + c * CW, CW), :].rearrange("(t p) d -> p t d", p=P)
            sp.dma_start(dst, out[:]).then_inc(s_store, 16)

        @block.sync
        def _(sp):
            sp.dma_start(ident[:], ident_in).then_inc(s_const, 16)
            sp.dma_start(b1_all[:], b1).then_inc(s_const, 16)
            load(sp, 0)
            load_b2(sp, 0)
            store(sp, 0, 0)
            with sp.Fori(1, E_N) as e:
                load(sp, e)
                store(sp, e - 1, 1)
                load_b2(sp, e)
                store(sp, e, 0)
            store(sp, E_N - 1, 1)
            sp.wait_ge(s_store, (CHUNKS + 1) * 16)

        @block.gpsimd
        def _(pool):
            def gather(n, c):
                passed(pool, s_index, n + 1, s_passed_pool)
                for s in range(CT):
                    pool.indirect_dma_start(x[:, c, s, :], None, rows,
                                            bass.IndirectOffsetOnAxis(index[:, c, s:s + 1], 0)).then_inc(s_x[c], 16)

            gather(0, 0)
            with pool.Fori(0, E_N) as e:
                pool.wait_ge(s_w1_hi, e + 1)
                pool.tensor_tensor(w1_lo[:], raw1[:], f32(w1_hi[:]), ALU.subtract).then_inc(s_w1_lo, 1)
                gather(e * CE + 1, 1)
                for half in range(2):
                    cut = slice(half * W2CUT, (half + 1) * W2CUT)
                    pool.wait_ge(s_w2_hi, e * 2 + half + 1)
                    pool.tensor_tensor(w2_lo[:, cut], raw2[:, cut], f32(w2_hi[:, cut]), ALU.subtract).then_inc(s_w2_lo, 1)
                gather(e * CE + 2, 0)

        @block.scalar
        def _(act):
            def transposed(n, c):
                for s in range(CT):
                    act.wait_ge(s_pt, n * CT + s + 1)
                    act.activation(xt_hi[:, :, s * P:(s + 1) * P],
                                   pt[:, (c * CT + s) % 2, :].rearrange("p (d t) -> p d t", d=DT),
                                   ACT.Copy).then_inc(s_xt_hi, 1)

            transposed(0, 0)
            with act.Fori(0, E_N) as e:
                act.wait_ge(s_raw1, (e + 1) * 16)
                act.activation(w1_hi[:], raw1[:], ACT.Copy).then_inc(s_w1_hi, 1)
                act.wait_ge(s_b1, e + 1)
                for c in range(CE):
                    for f in range(FT):
                        i = e * (CE * FT) + c * FT + f
                        act.wait_ge(s_ph, i + 1)
                        act.wait_ge(s_g_lo, i + 1)
                        act.activation(g[:, f % 2].rearrange("p (h t) -> p h t", h=2), ph[:, f % 2, :, :HALF], ACT.Gelu,
                                       bias=b1_col[:, f:f + 1]).then_inc(s_g, 1)
                        act.wait_ge(s_g, i + 3)
                        act.activation(g_hi[:, f, :], g[:, f % 2, :], ACT.Copy).then_inc(s_g_hi, 1)
                        if c == 0 and f in (1, 3):
                            cut = slice(f // 2 * W2CUT, (f // 2 + 1) * W2CUT)
                            act.wait_ge(s_raw2, (e + 1) * 16)
                            act.activation(w2_hi[:, cut], raw2[:, cut], ACT.Copy).then_inc(s_w2_hi, 1)
                    transposed(e * CE + c + 1, 1 - c)

        @block.vector
        def _(dve):
            def put_index(n, c):
                dve.tensor_copy(index[:, c, :], token_of[:, bass.ds(n * CT, CT)]).then_inc(s_index, 1)

            def transposed(n, c):
                for s in range(CT):
                    cut = (slice(None), slice(None), slice(s * P, (s + 1) * P))
                    dve.wait_ge(s_xt_hi, n * CT + s + 1)
                    dve.tensor_tensor(xt_lo[cut], pt[:, (c * CT + s) % 2, :].rearrange("p (d t) -> p d t", d=DT),
                                      f32(xt_hi[cut]), ALU.subtract).then_inc(s_xt, 1)

            for s, n in ((s_xt, 2), (s_g, 2), (s_g_lo, 2), (s_out, 2), (s_store, 16)):
                dve.sem_inc(s, n)
            put_index(0, 0)
            dve.wait_ge(s_const, 32)
            transposed(0, 0)
            with dve.Fori(0, E_N) as e:
                dve.tensor_copy(b1_col[:], b1_all[:, bass.ds(e, 1), :].rearrange("p o f -> p (o f)")).then_inc(s_b1, 1)
                for c in range(CE):
                    n = e * CE + c
                    put_index(n + 1, 1 - c)
                    for f in range(FT):
                        dve.wait_ge(s_g_hi, e * (CE * FT) + c * FT + f + 1)
                        dve.tensor_tensor(g_lo[:, f, :], g[:, f % 2, :], f32(g_hi[:, f, :]), ALU.subtract).then_inc(s_g_lo, 1)
                    transposed(n + 1, 1 - c)
                    dve.wait_ge(s_store, (n + 1) * 16)
                    if c == 0:
                        dve.wait_ge(s_b2, (e + 1) * 16)
                    for s in range(CT):
                        dve.wait_ge(s_po, n * CT + s + 1)
                        dve.tensor_tensor(out[:, s, :], po[:, (c * CT + s) % 2, :], b2_row[:], ALU.add).then_inc(s_out, 1)

        @block.tensor
        def _(pe):
            def transpose(n, c, e):
                pe.wait_ge(s_x[c], (e + 1) * (CT * 16))
                for s in range(CT):
                    pe.wait_ge(s_xt, n * CT + s + 1)
                    for d in range(DT):
                        mm = pe.transpose(pt[:, (c * CT + s) % 2, d * P:(d + 1) * P], x[:, c, s, d * P:(d + 1) * P], ident[:])
                    mm.then_inc(s_pt, 1)

            pe.wait_ge(s_const, 32)
            transpose(0, 0, 0)
            with pe.Fori(0, E_N) as e:
                pe.wait_ge(s_w1_lo, e + 1)
                for c in range(CE):
                    n = e * CE + c
                    pe.wait_ge(s_xt, (n + 1) * CT + 2)
                    for f in range(FT):
                        pe.wait_ge(s_g, n * FT + f + 1)
                        cut = slice(f * P, (f + 1) * P)
                        for half in range(2):
                            part = slice(half * HALF, (half + 1) * HALF)
                            for d in range(DT):
                                ops = ((w1_hi, xt_hi), (w1_hi, xt_lo), (w1_lo, xt_hi))
                                for p, (w, r) in enumerate(ops):
                                    mm = pe.matmul(ph[:, f % 2, half, :HALF], w[:, d, cut], r[:, d, part],
                                                   start=(d == 0 and p == 0), stop=(d == DT - 1 and p == 2))
                        mm.then_inc(s_ph, 1)
                    transpose(n + 1, 1 - c, e if c == 0 else e + 1)
                    if c == 0:
                        pe.wait_ge(s_w2_lo, 2 * e + 2)
                    for s in range(CT):
                        pe.wait_ge(s_out, n * CT + s + 1)
                        cut = slice(s * P, (s + 1) * P)
                        for f in range(FT):
                            if s == 0:
                                pe.wait_ge(s_g_lo, n * FT + f + 3)
                            ops = ((g_hi, w2_hi), (g_hi, w2_lo), (g_lo, w2_hi))
                            for p, (l, w) in enumerate(ops):
                                mm = pe.matmul(po[:, (c * CT + s) % 2, :], l[:, f, cut], w[:, f, :],
                                               start=(f == 0 and p == 0), stop=(f == FT - 1 and p == 2))
                        mm.then_inc(s_po, 1)


def combine(nc, expert_out, x_in, x_out, slot_of, weight):
    with ExitStack() as ctx:
        def sb(name, shape, dt=F32):
            return ctx.enter_context(nc.sbuf_tensor("c_" + name, shape, dt))

        sem = stage_semaphores(nc, ctx, "c_")

        index = sb("index", [P, 2, ST * TOP], I32)
        part = sb("part", [P, 2, ST, TOP, D])
        x = sb("x", [P, 2, ST, D])
        w = sb("w", [P, 2, ST * TOP])
        s_index = [sem("s_index0"), sem("s_index1")]
        s_part = [sem("s_part0"), sem("s_part1")]
        s_x = [sem("s_x0"), sem("s_x1")]
        s_w = sem("s_w")
        s_first = sem("s_first")
        s_sum = sem("s_sum")
        s_store = [sem("s_store0"), sem("s_store1")]
        s_passed = sem("s_passed")
        s_passed_pool = sem("s_passed_pool")
        block = ctx.enter_context(nc.Block())

        def store(sp, b, v):
            passed(sp, s_sum, b + 3, s_passed)
            sp.dma_start(x_out[b].rearrange("(t p) d -> p t d", p=P), x[:, v]).then_inc(s_store[v], 16)

        @block.sync
        def _(sp):
            with sp.Fori(0, B // 2) as bb:
                for v in range(2):
                    passed(sp, s_store[v], (bb + 1) * 16, s_passed)
                    sp.dma_start(x[:, v], x_in[bb * 2 + v].rearrange("(t p) d -> p t d", p=P)).then_inc(s_x[v], 16)
                for v in range(2):
                    store(sp, bb * 2 + v, v)
            for v in range(2):
                sp.wait_ge(s_store[v], (B // 2 + 1) * 16)

        @block.gpsimd
        def _(pool):
            with pool.Fori(0, B // 2) as bb:
                for v in range(2):
                    passed(pool, s_index[v], bb + 1, s_passed_pool)
                    for t in range(ST):
                        for k in range(TOP):
                            pool.indirect_dma_start(part[:, v, t, k, :], None, expert_out,
                                                    bass.IndirectOffsetOnAxis(index[:, v, t * TOP + k:t * TOP + k + 1], 0)
                                                    ).then_inc(s_part[v], 16)

        @block.vector
        def _(dve):
            def put_index(b, v):
                cut = bass.ds(b * ST, ST)
                dve.tensor_copy(index[:, v, :].rearrange("p (t k) -> p t k", k=TOP), slot_of[:, cut, :]).then_inc(s_index[v], 1)

            def body(bb, last):
                for v in range(2):
                    b = bb * 2 + v
                    dve.tensor_copy(w[:, v, :].rearrange("p (t k) -> p t k", k=TOP),
                                    weight[:, bass.ds(b * ST, ST), :]).then_inc(s_w, 1)
                    dve.wait_ge(s_w, b + 1)
                    dve.wait_ge(s_part[v], (bb + 1) * (ST * TOP * 16))
                    dve.wait_ge(s_x[v], (bb + 1) * 16)
                    for t in range(ST):
                        dve.scalar_tensor_tensor(x[:, v, t, :], part[:, v, t, 0, :], w[:, v, t * TOP:t * TOP + 1], x[:, v, t, :],
                                                 ALU.mult, ALU.add).then_inc(s_first, 1)
                    for t in range(ST):
                        dve.wait_ge(s_first, b * ST + t + 1)
                        ins = dve.scalar_tensor_tensor(x[:, v, t, :], part[:, v, t, 1, :], w[:, v, t * TOP + 1:t * TOP + 2],
                                                       x[:, v, t, :], ALU.mult, ALU.add)
                    ins.then_inc(s_sum, 1)
                    if not last:
                        dve.wait_ge(s_sum, b + 3)
                        put_index(b + 2, v)

            dve.sem_inc(s_sum, 2)
            dve.sem_inc(s_store[0], 16)
            dve.sem_inc(s_store[1], 16)
            put_index(0, 0)
            put_index(1, 1)
            with dve.Fori(0, B // 2 - 1) as bb:
                body(bb, False)
            body(B // 2 - 1, True)



def program(nc, x, ctx_t, out, bufs, attn, mlp, moe, g_xattn, g_ffn, consts):
    def column(g, layer):
        return g[:, layer:layer + 1].to_broadcast([P, 1])

    def row(v):
        return v.to_broadcast([P, D])

    def attend(layer, x_in, x_out, hmax):
        a = attn[layer]
        attention(nc, layer, x_in, x_out, bufs["h"], hmax, ctx_t, [a["Wq"], a["Wk"], a["Wv"], a["Wo"]],
                  {"bq": a["bq"], "bk": a["bk"]}, {"bv": row(a["bv"]), "bo": row(a["bo"])},
                  column(g_xattn, layer), consts)

    attend(0, x, bufs["x1"], bufs["hmax"])
    gated_mlp(nc, bufs["h"], bufs["hmax"], bufs["x1"], bufs["x2"], (mlp["w_gate"], mlp["w_up"], mlp["w_down"]),
              column(g_ffn, 0), consts["ident"], bufs)
    attend(1, bufs["x2"], bufs["x1"], None)
    mixture(nc, bufs["h"], bufs["x1"], out, moe["router_w"], moe["router_b"].to_broadcast([P, E_N]),
            moe["w1"], moe["w2"], moe["b1"], moe["b2"], column(g_ffn, 1), consts, bufs)




def heads_inside(a):
    return a.reshape(*a.shape[:-1], G, HG, HD).swapaxes(-1, -2).reshape(a.shape)


def lay_w(w, interleave):
    wt = w.T
    if interleave:
        wt = heads_inside(wt)
    return np.ascontiguousarray(wt.reshape(DT, P, D).transpose(1, 0, 2))


def lay_bias(v):
    return np.ascontiguousarray(heads_inside(v).reshape(G, P).T)


def constants():
    token = np.arange(NT)[None, :, None] * P + np.arange(P)[:, None, None]
    p, c = np.arange(P)[:, None], np.arange(P)[None, :]
    half = HD // 2
    inv_freq = np.float32(1.0) / np.float32(10000.0) ** (np.arange(half, dtype=np.float32) / np.float32(half))
    angle = inv_freq.astype(np.float32)[:, None] * np.arange(S, dtype=np.float32)[None, :]
    cos, sin = np.cos(angle), np.sin(angle)
    return {
        "ident": np.eye(P, dtype=np.float32),
        "masks": np.stack([np.where(c <= p, 0.0, NEG), np.where(c >= p, 0.0, NEG)], 1).astype(np.float32),
        "cos": np.repeat(np.concatenate([cos, cos]), HG, 0),
        "sin": np.repeat(np.concatenate([-sin, sin]), HG, 0),
        "before": np.triu(np.ones((P, P), np.float32), 1),
        "expert": np.ascontiguousarray(np.broadcast_to(np.arange(E_N, dtype=np.float32), (P, NT, E_N))),
        "spare": (SLOTS + np.arange(TOP)[None, None, :] * T + token).astype(np.float32),
        "token_id": token[:, :, 0].astype(np.int32),
    }


def kernel(**inputs):
    import concourse.bacc as bacc
    from concourse.bass_utils import run_bass_kernel_spmd

    a = {k: np.asarray(v) for k, v in inputs.items()}
    ctx = a["ctx_1024"]
    ctx_t = np.concatenate([ctx, ctx[:1]]).transpose(0, 2, 1).reshape(B + 1, DT, P, S).transpose(0, 2, 1, 3)
    arrays = {"x": a["x"], "ctx_t": ctx_t, "g_xattn": a["g_xattn"][None], "g_ffn": a["g_ffn"][None]}
    for layer in range(2):
        at = f"L{layer}_xattn_"
        for n in ("Wq", "Wk", "Wv", "Wo"):
            arrays[at + n] = lay_w(a[at + n], n in ("Wq", "Wk"))
        for n in ("bq", "bk"):
            arrays[at + n] = lay_bias(a[at + n])
        for n in ("bv", "bo"):
            arrays[at + n] = a[at + n][None]
    for n in ("w_gate", "w_up", "w_down"):
        arrays[n] = a["L0_ffn_" + n]
    arrays["router_w"] = a["L1_ffn_router_w"].reshape(DT, P, E_N).transpose(1, 0, 2)
    arrays["router_b"] = a["L1_ffn_router_b"][None]
    arrays["w1"] = a["L1_ffn_w1"].reshape(E_N, DT, P, F).transpose(0, 2, 1, 3)
    arrays["w2"] = a["L1_ffn_w2"].reshape(E_N, FT, P, D).transpose(0, 2, 1, 3)
    arrays["b1"] = a["L1_ffn_b1"].reshape(E_N, FT, P).transpose(2, 0, 1)
    arrays["b2"] = a["L1_ffn_b2"]
    consts = constants()
    arrays.update(consts)
    arrays = {"in_" + k: np.ascontiguousarray(v) for k, v in arrays.items()}

    nc = bacc.Bacc("TRN2", target_bir_lowering=False, num_devices=1)
    t = {k[3:]: nc.dram_tensor(k, v.shape, mybir.dt.from_np(v.dtype), kind="ExternalInput").ap()
         for k, v in arrays.items()}
    out = nc.dram_tensor("out", (B, S, D), F32, kind="ExternalOutput").ap()

    def scratch(name, shape, dt=F32):
        return nc.dram_tensor(name, shape, dt, kind="Internal").ap()

    bufs = {
        "x1": scratch("x1", (B, S, D)), "x2": scratch("x2", (B, S, D)), "h": scratch("h", (B, S, D)),
        "hmax": scratch("hmax", (P, 1)),
        "raw": [scratch(n, (NQ, P, 4, S)) for n in ("gate_raw", "up_raw")],
        "down": scratch("down_split", (2, P, IT, D)),
        "tokens": scratch("tokens", (SLOTS + T * TOP, 1), I32), "expert_out": scratch("expert_out", (SLOTS, D)),
    }
    attn = [{n: t[f"L{layer}_xattn_{n}"] for n in ("Wq", "bq", "Wk", "bk", "Wv", "bv", "Wo", "bo")} for layer in range(2)]
    program(nc, t["x"], t["ctx_t"], out, bufs, attn, t, t, t["g_xattn"], t["g_ffn"], {k: t[k] for k in consts})
    r = run_bass_kernel_spmd(nc, [arrays], core_ids=[0])
    return r.results[0]["out"]
```

```python
from contextlib import ExitStack

import numpy as np
import concourse.bass as bass
from concourse import mybir

F32 = mybir.dt.float32
F32R = mybir.dt.float32r
BF16 = mybir.dt.bfloat16
I16 = mybir.dt.int16
U16 = mybir.dt.uint16
I32 = mybir.dt.int32
U32 = mybir.dt.uint32
ALU = mybir.AluOpType
ACT = mybir.ActivationFunctionType
AX = mybir.AxisListType

P = 128
B, S, D = 8, 512, 512
T = B * S
NT = T // P
DT = D // P
ST = S // P
H, HD = 16, 32
HG = P // HD
G = H // HG
EPS = 1e-5
WINDOW = 256
NEG = -1.0e30


def passed(eng, sem, value, seen):
    eng.wait_ge(sem, value)
    eng.sem_inc(seen, 1)


def stage_semaphores(nc, ctx, tag):
    made = []
    ctx.callback(nc.all_engine_barrier)
    ctx.callback(nc.clear_and_free_semaphores, made)

    def sem(name):
        made.append(nc.alloc_semaphore(tag + name))
        return made[-1]

    return sem


def f32(ap):
    return ap.bitcast(F32)




def attention(nc, layer, x_in, x_out, h_out, hmax_out, ctx_t, w_in, cols, rows, gate, consts):
    rope = masked = layer == 1
    tag = f"a{layer}_"
    SCALE = float(HD) ** -0.5
    span = WINDOW // P
    keys_of = [(max(0, q - span), q + 1) if masked else (0, ST) for q in range(ST)]
    queries_of = [(k, min(ST, k + span + 1)) if masked else (0, ST) for k in range(ST)]

    with ExitStack() as ctx:
        def sb(name, shape, dt=F32):
            return ctx.enter_context(nc.sbuf_tensor(tag + name, shape, dt))

        def ps(name, shape, dt=F32):
            return ctx.enter_context(nc.psum_tensor(tag + name, shape, dt))

        sem = stage_semaphores(nc, ctx, tag)

        w_hi = sb("w_hi", [P, 3, DT, D], F32R)
        w_lo = sb("w_lo", [P, 3, DT, D], F32R)
        wo = sb("wo", [P, DT, D])
        ctx_raw = sb("ctx_raw", [P, DT, S])
        ctx_hi = sb("ctx_hi", [P, DT, S], F32R)
        ctx_lo = sb("ctx_lo", [P, DT, S], F32R)
        x_tile = sb("x_tile", [P, ST, D])
        h_new = x_tile
        ht_hi = sb("ht_hi", [P, DT, S], F32R)
        ht_lo = sb("ht_lo", [P, DT, S], F32R)
        qk_hi = sb("qk_hi", [P, 2, S], F32R)
        qk_lo = sb("qk_lo", [P, 2, S], F32R)
        NR = 3 * HD + 1
        q_stack = sb("q_stack", [P, 2, HG, S], F32R)
        k_stack = sb("k_stack", [P, 2, HG, S], F32R)
        v_sb = sb("v_sb", [P, ST, D])
        probs = sb("probs", [P, 2, HG, S])
        negmax = sb("negmax", [P, HG * ST])
        negmax_t = sb("negmax_t", [HG * ST, P], F32R)
        sums = sb("sums", [P, S])
        recip = sb("recip", [P, S])
        att = sb("att", [P, G, S])
        ones = sb("ones", [P, HD])
        ident = sb("ident", [P, P])
        b_col = {"q": sb("bq_col", [P, DT]), "k": sb("bk_col", [P, DT])}
        bv_row = sb("bv_row", [P, D])
        bo_row = sb("bo_row", [P, D])
        gate_col = sb("gate_col", [P, 1])
        tanh_g = sb("tanh_g", [P, 1])
        bn = sb("bn", [P, ST, 6])
        mv = sb("mv", [P, ST, 2])
        ve = sb("ve", [P, ST])
        rstd = sb("rstd", [P, ST])
        halfneg = sb("halfneg", [P, 1])
        x_new = sb("x_new", [P, ST, D])
        bn_o = sb("bn_o", [P, ST, 6])
        mv_o = sb("mv_o", [P, ST, 2])
        ve_o = sb("ve_o", [P, ST])
        rstd_o = sb("rstd_o", [P, ST])
        nmr_o = sb("nmr_o", [P, ST])
        hmax = sb("hmax", [P, NT])
        hmax_all = sb("hmax_all", [P, 1])
        if masked:
            ident_b = sb("ident_b", [P, P], BF16)
            masks = sb("masks", [P, 2, P], BF16)
            masks_in = sb("masks_in", [P, 2, P])
            cos_t = sb("cos_t", [P, S])
            sin_t = sb("sin_t", [P, S])
            lin = sb("lin", [P, S])
            lin_cos = sb("lin_cos", [P, S])
            swap_sin = sb("swap_sin", [P, S])

        pj = ps("pj", [P, 2, 512])
        pa = ps("pa", [P, 2, 512])
        pst = ps("pst", [P, 2, 512])
        po = ps("po", [P, 512])
        psm = ps("psm", [P, 512])

        s_w = [sem("s_w0"), sem("s_w1"), sem("s_w2")]
        s_const = sem("s_const")
        s_w_hi = sem("s_w_hi")
        s_w_lo = sem("s_w_lo")
        s_setup = sem("s_setup")
        s_tanh = sem("s_tanh")
        s_x_in = sem("s_x_in")
        s_ctx_in = sem("s_ctx_in")
        s_ctx_hi = sem("s_ctx_hi")
        s_ctx_lo = sem("s_ctx_lo")
        s_bn = sem("s_bn")
        s_mv = sem("s_mv")
        s_ve = sem("s_ve")
        s_rstd = sem("s_rstd")
        s_hn = sem("s_hn")
        s_pj = sem("s_pj")
        s_pj_out = sem("s_pj_out")
        s_o = sem("s_o")
        s_o_out = sem("s_o_out")
        s_ht_hi = sem("s_ht_hi")
        s_qk_hi = sem("s_qk_hi")
        s_qk_lo = sem("s_qk_lo")
        s_stack = {"q": [sem("s_qst0"), sem("s_qst1")], "k": [sem("s_kst0"), sem("s_kst1")]}
        s_pa = sem("s_pa")
        s_max = sem("s_max")
        s_nm_p = sem("s_nm_p")
        s_nm_t = sem("s_nm_t")
        s_mrow = [sem("s_mrow0"), sem("s_mrow1")]
        s_st = sem("s_st")
        s_exp = sem("s_exp")
        s_pv = sem("s_pv")
        s_sums = sem("s_sums")
        s_po_out = sem("s_po_out")
        s_recip = sem("s_recip")
        s_norm = sem("s_norm")
        s_xres = sem("s_xres")
        s_xb = sem("s_xb")
        s_bn_o = sem("s_bn_o")
        s_mv_o = sem("s_mv_o")
        s_ve_o = sem("s_ve_o")
        s_rstd_o = sem("s_rstd_o")
        s_nmr_o = sem("s_nmr_o")
        s_h_new = sem("s_h_new")
        s_hmax = sem("s_hmax")
        s_store_x = sem("s_store_x")
        s_store_h = sem("s_store_h")
        s_swap = sem("s_swap")
        s_rope = sem("s_rope")
        s_cos = sem("s_cos")
        s_last = sem("s_last")
        s_passed = sem("s_passed")
        s_passed_sp = sem("s_passed_sp")
        block = ctx.enter_context(nc.Block())

        T0, QK_A, V0, QK_B, PJ = 0, ST, 2 * ST, 3 * ST, 4 * ST
        NQK = 2 * G
        NG = HG * ST
        NSC = G * NG
        STACK = 16 * 3
        MROW = 16
        NCONST = 16 * (7 + 3 * masked)
        M_STEPS = [range(0, 0), range(0, 4), range(4, 10), range(10, NG)]
        M_SLOTS = [[0, 0, 0, 0, 0], [0, 0, 0, 2, 4], [0, 1, 3, 4, 6], [0, 2, 4, 6, 6]]
        S_STEP = [(0, 2), (0, 2), (0, 3), (0, 3)] if rope else [(0, 3), (0, 3), (1, 0), (1, 0)]
        N_STEP = [(1, 0), (1, 1), (1, 2), (1, 3)]
        KEY_STEP = 3

        def kind_of(n):
            return "kq"[n % 2]

        def qk_tile(n):
            return (QK_A if n < ST else QK_B - ST) + n

        def stacked(b, g):
            return (b * (G // 2) + g // 2 + 1) * STACK

        raw_of = [probs[:, 0], probs[:, 1], ctx_raw[:]]

        def lo_written(b, n):
            return (s_qk_lo, b * NQK + n + 1) if rope else (s_pj_out, b * PJ + qk_tile(n) + 3)

        def next_group(b, g):
            return (b, g + 1) if g + 1 < G else (b + 1, 0)

        def projected_in(b, g):
            return (b, g + 2) if g + 2 < G else (b + 1, g + 2 - G)

        def normalise_heads(eng, b, g, t):
            cut = slice(t * P, (t + 1) * P)
            eng.wait_ge(s_recip, b * (G * ST) + g * ST + t + 2)
            eng.wait_ge(s_po_out, b * G + g + 2)
            eng.tensor_tensor(att[:, g, cut], att[:, g, cut], recip[:, cut], ALU.mult).then_inc(s_norm, 1)

        @block.sync
        def _(sp):
            for m in range(3):
                sp.dma_start(raw_of[m], w_in[m]).then_inc(s_w[m], 16)
            sp.dma_start(x_tile[:], x_in[0].rearrange("(t p) d -> p t d", p=P)).then_inc(s_x_in, 16)
            sp.dma_start(wo[:], w_in[3]).then_inc(s_const, 16)
            loads = [(ident[:], consts["ident"]), (b_col["q"][:], cols["bq"]), (b_col["k"][:], cols["bk"]),
                     (bv_row[:], rows["bv"]), (bo_row[:], rows["bo"]), (gate_col[:], gate)]
            if masked:
                loads += [(masks_in[:], consts["masks"]), (cos_t[:], consts["cos"]), (sin_t[:], consts["sin"])]
            for dst, src in loads:
                sp.dma_start(dst, src).then_inc(s_const, 16)
            sp.wait_ge(s_w_lo, 3)
            sp.dma_start(ctx_raw[:], ctx_t[0]).then_inc(s_ctx_in, 16)

            def to_stack(b, n, free):
                g = n // 2
                passed(sp, *lo_written(b, n), s_passed_sp)
                if free:
                    passed(sp, s_st, b * NSC + (g - 1) * NG, s_passed_sp)
                dst = {"q": q_stack, "k": k_stack}[kind_of(n)]
                srcs = {"q": (qk_hi, qk_hi, qk_lo), "k": (qk_hi, qk_lo, qk_hi)}[kind_of(n)]
                for row, src in enumerate(srcs):
                    sp.dma_start(f32(dst[HD * row:HD * row + HD, g % 2, :, :]),
                                 f32(src[:, n % 2, :])).then_inc(s_stack[kind_of(n)][g % 2], 16)

            def maximum_rows(b, g):
                passed(sp, s_nm_t, b * G + g + 1, s_passed_sp)
                row = f32(q_stack[3 * HD:NR, g % 2, :, :]).rearrange("r j (t q) -> r (j t) q", t=ST)
                sp.dma_start(row, f32(negmax_t[:])).then_inc(s_mrow[g % 2], 16)

            def load_ctx(b):
                passed(sp, s_ctx_lo, b, s_passed_sp)
                sp.dma_start(ctx_raw[:], ctx_t[b]).then_inc(s_ctx_in, 16)

            def whole(a, b):
                return a[b].rearrange("(t p) d -> p t d", p=P)

            def store(b):
                passed(sp, s_h_new, (b + 1) * ST, s_passed_sp)
                sp.dma_start(whole(x_out, b), x_new[:]).then_inc(s_store_x, 16)
                sp.dma_start(whole(h_out, b), h_new[:]).then_inc(s_store_h, 16)

            def load_residual(b):
                passed(sp, s_store_x, (b + 1) * 16, s_passed_sp)
                sp.dma_start(x_new[:], whole(x_in, b)).then_inc(s_xres, 16)

            load_ctx(1)
            for n in range(4):
                to_stack(0, n, False)
            maximum_rows(0, 0)

            def body(b, last):
                if not last:
                    if hmax_out is not None:
                        passed(sp, s_hmax, b * ST + 2, s_passed_sp)
                    passed(sp, s_pj, b * PJ + ST, s_passed_sp)
                    passed(sp, s_store_h, (b + 1) * 16, s_passed_sp)
                    sp.dma_start(x_tile[:], whole(x_in, b + 1)).then_inc(s_x_in, 16)
                for g in range(G):
                    bn_, gn = projected_in(b, g)
                    ahead = not (last and gn < 2)
                    if ahead:
                        to_stack(bn_, 2 * gn, True)
                    if not (last and g == G - 1):
                        maximum_rows(*next_group(b, g))
                    if ahead:
                        to_stack(bn_, 2 * gn + 1, True)
                    if g == 2 and not last:
                        load_ctx(b + 2)
                    if g == 1:
                        load_residual(b)
                store(b)

            with sp.Fori(0, B - 1) as b:
                body(b, False)
            body(B - 1, True)
            sp.wait_ge(s_store_x, (B + 1) * 16)
            sp.wait_ge(s_store_h, (B + 1) * 16)
            sp.wait_ge(s_ctx_in, (B + 1) * 16)
            if hmax_out is not None:
                sp.wait_ge(s_last, 1)
                sp.dma_start(hmax_out, hmax_all[:]).then_inc(s_last, 16)
                sp.wait_ge(s_last, 17)

        @block.scalar
        def _(act):
            def context(b):
                act.wait_ge(s_ctx_in, b * 16 + 16)
                act.activation(ctx_hi[:], ctx_raw[:], ACT.Copy).then_inc(s_ctx_hi, 1)

            def transposed(b, t):
                act.wait_ge(s_pj, b * PJ + T0 + t + 1)
                act.activation(ht_hi[:, :, t * P:(t + 1) * P],
                               pj[:, (T0 + t) % 2, :].rearrange("p (d t) -> p d t", d=DT),
                               ACT.Copy).then_inc(s_ht_hi, 1)

            def qk_to_hi(b, n, first=False):
                g, tile = n // 2, qk_tile(n)
                if not first:
                    before = stacked(b, g - 1) if g else stacked(b - 1, G - 1)
                    act.wait_ge(s_stack[kind_of(n)][(g - 1) % 2], before)
                if rope:
                    act.wait_ge(s_rope, b * NQK + n + 1)
                    act.activation(qk_hi[:, n % 2, :], lin_cos[:], ACT.Copy).then_inc(s_qk_hi, 1)
                else:
                    act.wait_ge(s_pj, b * PJ + tile + 1)
                    act.activation(qk_hi[:, n % 2, :], pj[:, tile % 2, :], ACT.Identity,
                                   bias=b_col[kind_of(n)][:, g:g + 1]).then_inc(s_qk_hi, 1)

            def exponentials(b, g, k):
                q0, q1 = queries_of[k]
                act.wait_ge(s_pv, b * G * ST + g * ST + k + 1)
                for j in range(HG):
                    n = (g * ST + k) * HG + j
                    act.wait_ge(s_st, b * NSC + n + 1)
                    act.activation(probs[:, k % 2, j, q0 * P:q1 * P], pst[:, n % 2, q0 * P:q1 * P],
                                   ACT.Exp, scale=SCALE).then_inc(s_exp, 1)

            def take_out(b, g):
                act.wait_ge(s_pv, b * G * ST + (g + 1) * ST + 2)
                act.wait_ge(s_recip, b * (G * ST) + g * ST + 1)
                act.activation(sums[:], psm[:], ACT.Copy).then_inc(s_sums, 1)
                act.activation(att[:, g, :], po[:], ACT.Copy).then_inc(s_po_out, 1)

            for m in range(3):
                act.wait_ge(s_w[m], 16)
                act.activation(w_hi[:, m], raw_of[m], ACT.Copy).then_inc(s_w_hi, 1)
            act.wait_ge(s_const, NCONST)
            act.activation(tanh_g[:], gate_col[:], ACT.Tanh).then_inc(s_tanh, 1)
            context(0)
            for t in range(ST):
                transposed(0, t)
            for n in range(4):
                qk_to_hi(0, n, first=n < 2)

            def body(b, last):
                for g in range(G):
                    bn_, gn = projected_in(b, g)
                    ahead = not (last and gn < 2)
                    for k in range(ST):
                        exponentials(b, g, k)
                        if g == 2 and k < 2 and not last:
                            transposed(b + 1, 2 * k)
                            transposed(b + 1, 2 * k + 1)
                        if k == KEY_STEP and ahead:
                            qk_to_hi(bn_, 2 * gn)
                    take_out(b, g)
                    if g == 1 and not last:
                        context(b + 1)
                    if ahead:
                        qk_to_hi(bn_, 2 * gn + 1)
                for t in range(ST):
                    act.wait_ge(s_nmr_o, b * ST + t + 1)
                    if t == 0:
                        act.wait_ge(s_store_h, (b + 1) * 16)
                    act.activation(h_new[:, t, :], x_new[:, t, :], ACT.Identity,
                                   bias=nmr_o[:, t:t + 1], scale=rstd_o[:, t:t + 1]).then_inc(s_h_new, 1)

            with act.Fori(0, B - 1) as b:
                body(b, False)
            body(B - 1, True)

        @block.gpsimd
        def _(pool):
            def context(b):
                pool.wait_ge(s_ctx_hi, b + 1)
                pool.tensor_tensor(ctx_lo[:], ctx_raw[:], f32(ctx_hi[:]), ALU.subtract).then_inc(s_ctx_lo, 1)

            def deviation(b, t):
                pool.wait_ge(s_ve, b * ST + t + 1)
                pool.tensor_tensor(rstd[:, t:t + 1], ve[:, t:t + 1], halfneg[:], ALU.pow).then_inc(s_rstd, 1)

            def turn(b, n):
                if rope:
                    pool.wait_ge(s_pj_out, b * PJ + qk_tile(n) + 3)
                    pool.tensor_tensor(lin_cos[:], lin[:], cos_t[:], ALU.mult).then_inc(s_cos, 1)

            def add_bias(b, t):
                pool.wait_ge(s_xres, (b + 1) * 16)
                pool.tensor_tensor(x_new[:, t, :], x_new[:, t, :], bo_row[:], ALU.add).then_inc(s_xb, 1)

            pool.wait_ge(s_setup, 3)
            context(0)
            for t in range(ST):
                deviation(0, t)
            for n in range(4):
                turn(0, n)
            pool.wait_ge(s_setup, 4 + 2 * masked)

            def body(b, last):
                for t in range(ST):
                    if not last:
                        deviation(b + 1, t)
                for g in range(G):
                    bn_, gn = projected_in(b, g)
                    if not (last and gn < 2):
                        turn(bn_, 2 * gn)
                        if g == 1 and not last:
                            context(b + 1)
                    for t in range(ST if g < G - 1 else 0):
                        normalise_heads(pool, b, g, t)
                    if not (last and gn < 2):
                        turn(bn_, 2 * gn + 1)
                    if g == 2:
                        for t in range(ST):
                            add_bias(b, t)
                for t in range(ST):
                    pool.wait_ge(s_ve_o, b * ST + t + 1)
                    pool.tensor_tensor(rstd_o[:, t:t + 1], ve_o[:, t:t + 1], halfneg[:],
                                       ALU.pow).then_inc(s_rstd_o, 1)

            with pool.Fori(0, B - 1) as b:
                body(b, False)
            body(B - 1, True)

        @block.vector
        def _(dve):
            dve.memset(ones[:], 1.0).then_inc(s_setup, 1)
            dve.memset(halfneg[:], -0.5).then_inc(s_setup, 1)
            dve.memset(f32(k_stack[3 * HD:NR]), 1.0).then_inc(s_setup, 1)
            for m in range(3):
                dve.wait_ge(s_w_hi, m + 1)
                dve.tensor_tensor(w_lo[:, m], raw_of[m], f32(w_hi[:, m]), ALU.subtract).then_inc(s_w_lo, 1)
            for s, n in ((s_pj_out, 2), (s_o_out, ST), (s_max, 2), (s_exp, 2), (s_pv, 2), (s_sums, 1), (s_po_out, 1),
                         (s_recip, 1), (s_norm, 1), (s_hmax, 2),
                         (s_store_x, 16), (s_store_h, 16)):
                dve.sem_inc(s, n)

            def stats(b, t):
                if t == 0:
                    dve.wait_ge(s_x_in, (b + 1) * 16)
                dve.bn_stats(bn[:, t, :], x_tile[:, t, :]).then_inc(s_bn, 1)
                passed(dve, s_bn, b * ST + t + 1, s_passed)
                dve.bn_aggr(mv[:, t, :], bn[:, t, :]).then_inc(s_mv, 1)
                dve.wait_ge(s_mv, b * ST + t + 1)
                dve.tensor_scalar(ve[:, t:t + 1], mv[:, t, 1:2], EPS, None, ALU.add).then_inc(s_ve, 1)

            def normalise(b, t):
                dve.wait_ge(s_rstd, b * ST + t + 1)
                dve.tensor_scalar(x_tile[:, t, :], x_tile[:, t, :], mv[:, t, 0:1], rstd[:, t:t + 1],
                                  ALU.subtract, ALU.mult).then_inc(s_hn, 1)

            def values(b, t):
                dve.wait_ge(s_pj, b * PJ + V0 + t + 1)
                dve.tensor_tensor(v_sb[:, t, :], pj[:, (V0 + t) % 2, :], bv_row[:], ALU.add).then_inc(s_pj_out, 1)

            def qk_to_lo(b, n):
                g, tile = n // 2, qk_tile(n)
                bias = b_col[kind_of(n)][:, g:g + 1]
                if rope:
                    top, low = slice(0, P // 2), slice(P // 2, P)
                    dve.wait_ge(s_pj, b * PJ + tile + 1)
                    dve.tensor_scalar(lin[:], pj[:, tile % 2, :], bias, None, ALU.add).then_inc(s_pj_out, 1)
                    dve.wait_ge(s_pj_out, b * PJ + tile + 3)
                    for dst, src in ((top, low), (low, top)):
                        dve.tensor_tensor(swap_sin[dst, :], lin[src, :], sin_t[src, :], ALU.mult).then_inc(s_swap, 1)
                    dve.wait_ge(s_swap, (b * NQK + n + 1) * 2)
                    dve.wait_ge(s_cos, b * NQK + n + 1)
                    dve.tensor_tensor(lin_cos[:], lin_cos[:], swap_sin[:], ALU.add).then_inc(s_rope, 1)
                    dve.wait_ge(s_qk_hi, b * NQK + n + 1)
                    dve.tensor_tensor(qk_lo[:, n % 2, :], lin_cos[:], f32(qk_hi[:, n % 2, :]),
                                      ALU.subtract).then_inc(s_qk_lo, 1)
                else:
                    dve.wait_ge(s_qk_hi, b * NQK + n + 1)
                    dve.scalar_tensor_tensor(qk_lo[:, n % 2, :], pj[:, tile % 2, :], bias,
                                             f32(qk_hi[:, n % 2, :]), ALU.add, ALU.subtract).then_inc(s_pj_out, 1)

            def ht_to_lo(b, t):
                dve.wait_ge(s_ht_hi, b * ST + t + 1)
                cut = (slice(None), slice(None), slice(t * P, (t + 1) * P))
                dve.tensor_tensor(ht_lo[cut], pj[:, (T0 + t) % 2, :].rearrange("p (d t) -> p d t", d=DT),
                                  f32(ht_hi[cut]), ALU.subtract).then_inc(s_pj_out, 1)

            def maxima(b, g, tiles):
                for i in tiles:
                    q, j = i // HG, i % HG
                    k0, k1 = keys_of[q]
                    dve.wait_ge(s_pa, b * NSC + g * NG + i + 1)
                    dve.tensor_reduce(negmax[:, j * ST + q:j * ST + q + 1], pa[:, i % 2, k0 * P:k1 * P],
                                      AX.X, ALU.max, negate=True).then_inc(s_max, 1)

            def maxima_to_rows(b, g, first=False):
                if not first:
                    before = b * 2 + (g - 1) // 2 + 1 if g else b * 2
                    dve.wait_ge(s_mrow[(g - 1) % 2], before * MROW)
                dve.wait_ge(s_nm_p, b * G + g + 1)
                dve.tensor_copy(negmax_t[:], pa[0:NG, 0, 0:P]).then_inc(s_nm_t, 1)

            def invert_sums(b, g, t):
                n = b * (G * ST) + g * ST + t
                cut = slice(t * P, (t + 1) * P)
                dve.wait_ge(s_norm, b * (G * ST) + g * ST + 1)
                dve.wait_ge(s_sums, b * G + g + 2)
                dve.reciprocal(recip[:, cut], sums[:, cut]).then_inc(s_recip, 1)

            def out_stats(b, t):
                n = b * ST + t + 1
                dve.wait_ge(s_o, n)
                dve.wait_ge(s_xb, n)
                dve.scalar_tensor_tensor(x_new[:, t, :], pj[:, t % 2, :], tanh_g[:], x_new[:, t, :],
                                         ALU.mult, ALU.add).then_inc(s_o_out, 1)
                dve.wait_ge(s_o_out, n + ST)
                dve.bn_stats(bn_o[:, t, :], x_new[:, t, :]).then_inc(s_bn_o, 1)
                passed(dve, s_bn_o, n, s_passed)
                dve.bn_aggr(mv_o[:, t, :], bn_o[:, t, :]).then_inc(s_mv_o, 1)
                dve.wait_ge(s_mv_o, n)
                dve.tensor_scalar(ve_o[:, t:t + 1], mv_o[:, t, 1:2], EPS, None, ALU.add).then_inc(s_ve_o, 1)

            def out_scale(b, t):
                dve.wait_ge(s_rstd_o, b * ST + t + 1)
                dve.scalar_tensor_tensor(nmr_o[:, t:t + 1], mv_o[:, t, 0:1], -1.0, rstd_o[:, t:t + 1],
                                         ALU.mult, ALU.mult).then_inc(s_nmr_o, 1)

            def out_max(b, t):
                if hmax_out is not None:
                    dve.wait_ge(s_h_new, b * ST + t + 1)
                    dve.tensor_reduce(hmax[:, bass.ds(b * ST + t, 1)], h_new[:, t, :], AX.X, ALU.max,
                                      apply_absolute_value=True).then_inc(s_hmax, 1)

            dve.wait_ge(s_tanh, 1)
            if masked:
                dve.tensor_copy(ident_b[:], ident[:]).then_inc(s_setup, 1)
                dve.tensor_copy(masks[:], masks_in[:]).then_inc(s_setup, 1)
            dve.tensor_scalar(bo_row[:], bo_row[:], tanh_g[:], None, ALU.mult).then_inc(s_setup, 1)
            for t in range(ST):
                stats(0, t)
            for t in range(ST):
                normalise(0, t)
            for t in range(ST):
                ht_to_lo(0, t)
            for n in range(4):
                qk_to_lo(0, n)
            maxima(0, 0, range(NG))
            maxima_to_rows(0, 0, first=True)

            def body(b, last):
                for t in range(ST):
                    values(b, t)
                for g in range(G):
                    bn_, gn = projected_in(b, g)
                    ahead = not (last and gn < 2)
                    for k in range(ST):
                        for t in range(ST if not last else 0):
                            if S_STEP[t] == (g, k):
                                stats(b + 1, t)
                            if N_STEP[t] == (g, k):
                                normalise(b + 1, t)
                        tiles = [] if last and g == G - 1 else list(M_STEPS[k])
                        maxima(*next_group(b, g), tiles)
                        if k == KEY_STEP and ahead:
                            qk_to_lo(bn_, 2 * gn)
                        if g == 2 and k < 2 and not last:
                            ht_to_lo(b + 1, 2 * k)
                            ht_to_lo(b + 1, 2 * k + 1)
                    if g < G - 1:
                        maxima_to_rows(b, g + 1)
                    for t in range(ST):
                        invert_sums(b, g, t)
                        if g == G - 1:
                            normalise_heads(dve, b, g, t)
                    if g == G - 1 and not last:
                        maxima_to_rows(b + 1, 0)
                    if ahead:
                        qk_to_lo(bn_, 2 * gn + 1)
                for t in range(ST):
                    out_stats(b, t)
                    out_scale(b, t)
                    if t >= 1:
                        out_max(b, t - 1)
                out_max(b, ST - 1)

            with dve.Fori(0, B - 1) as b:
                body(b, False)
            body(B - 1, True)
            if hmax_out is not None:
                dve.wait_ge(s_hmax, NT + 2)
                dve.tensor_reduce(hmax_all[:], hmax[:], AX.X, ALU.max).then_inc(s_last, 1)

        @block.tensor
        def _(pe):
            def open_tile(b, n):
                pe.wait_ge(s_pj_out, b * PJ + n + 1)
                return pj[:, n % 2, :]

            def three_passes(out, lhs, rhs):
                for d in range(DT):
                    (lh, ll), (rh, rl) = lhs(d), rhs(d)
                    for n, (l, r) in enumerate(((lh, rh), (lh, rl), (ll, rh))):
                        mm = pe.matmul(out, l, r, start=(d == 0 and n == 0), stop=(d == DT - 1 and n == 2))
                return mm

            def project_qk(b, n):
                kind, g = kind_of(n), n // 2
                m = {"q": 0, "k": 1}[kind]
                hi, lo = {"q": (ht_hi, ht_lo), "k": (ctx_hi, ctx_lo)}[kind]
                cut = slice(g * P, (g + 1) * P)
                three_passes(open_tile(b, qk_tile(n)), lambda d: (w_hi[:, m, d, cut], w_lo[:, m, d, cut]),
                             lambda d: (hi[:, d, :], lo[:, d, :])).then_inc(s_pj, 1)

            def project_v(b, t):
                cut = slice(t * P, (t + 1) * P)
                out = open_tile(b, V0 + t)
                if t < 2:
                    pe.wait_ge(s_o_out, b * ST + t + 3)
                three_passes(out, lambda d: (ctx_hi[:, d, cut], ctx_lo[:, d, cut]),
                             lambda d: (w_hi[:, 2, d, :], w_lo[:, 2, d, :])).then_inc(s_pj, 1)

            def transpose(b, t):
                out = open_tile(b, T0 + t)
                pe.wait_ge(s_hn, b * ST + t + 1)
                for d in range(DT):
                    mm = pe.transpose(out[:, d * P:(d + 1) * P], x_tile[:, t, d * P:(d + 1) * P], ident[:])
                mm.then_inc(s_pj, 1)

            def transpose_maxima(b, g):
                pe.wait_ge(s_max, b * NSC + (g + 1) * NG + 2)
                pe.transpose(pa[0:NG, 0, 0:P], negmax[:], ident[:]).then_inc(s_nm_p, 1)

            def score_max(b, g, i, first=False):
                q, j = i // HG, i % HG
                k0, k1 = keys_of[q]
                if i == 0:
                    for kind in "qk":
                        pe.wait_ge(s_stack[kind][g % 2], stacked(b, g))
                    if not first:
                        pe.wait_ge(s_nm_t, b * G + g)
                pe.wait_ge(s_max, b * NSC + g * NG + i + 1)
                out = pa[:, i % 2, :]
                mm = pe.matmul(out[:, k0 * P:k1 * P], q_stack[0:3 * HD, g % 2, j, q * P:(q + 1) * P],
                               k_stack[0:3 * HD, g % 2, j, k0 * P:k1 * P], start=True, stop=not masked)
                if masked:
                    far = q - span >= 0
                    mm = pe.matmul(out[:, q * P:(q + 1) * P], ident_b[:], masks[:, 0, :], start=False, stop=not far)
                    if far:
                        mm = pe.matmul(out[:, k0 * P:(k0 + 1) * P], ident_b[:], masks[:, 1, :],
                                       start=False, stop=True)
                mm.then_inc(s_pa, 1)

            def score(b, g, k, j):
                n = (g * ST + k) * HG + j
                q0, q1 = queries_of[k]
                pe.wait_ge(s_exp, b * NSC + n + 1)
                out = pst[:, n % 2, :]
                mm = pe.matmul(out[:, q0 * P:q1 * P], k_stack[0:NR, g % 2, j, k * P:(k + 1) * P],
                               q_stack[0:NR, g % 2, j, q0 * P:q1 * P], start=True, stop=not masked)
                if masked:
                    far = k + span < ST
                    mm = pe.matmul(out[:, k * P:(k + 1) * P], ident_b[:], masks[:, 1, :], start=False, stop=not far)
                    if far:
                        mm = pe.matmul(out[:, (q1 - 1) * P:q1 * P], ident_b[:], masks[:, 0, :],
                                       start=False, stop=True)
                mm.then_inc(s_st, 1)

            def value_products(b, g, k, with_ones):
                if not with_ones:
                    pe.wait_ge(s_exp, b * NSC + (g * ST + k + 1) * HG + 2)
                    if k == 0:
                        pe.wait_ge(s_sums, b * G + g + 1)
                        pe.wait_ge(s_po_out, b * G + g + 1)
                q0, q1 = queries_of[k]
                for j in range(HG):
                    h = g * HG + j
                    lhs = ones[:] if with_ones else v_sb[:, k, h * HD:(h + 1) * HD]
                    mm = pe.matmul((psm if with_ones else po)[HD * j:HD * j + HD, q0 * P:q1 * P], lhs,
                                   probs[:, k % 2, j, q0 * P:q1 * P], start=(k == 0), stop=(k == ST - 1),
                                   skip_group_check=masked)
                if with_ones:
                    mm.then_inc(s_pv, 1)

            pe.wait_ge(s_w_lo, 3)
            pe.wait_ge(s_const, NCONST)
            for t in range(ST):
                transpose(0, t)
            pe.wait_ge(s_ctx_lo, 1)
            pe.wait_ge(s_pj_out, ST + 2)
            for n in range(4):
                project_qk(0, n)
            SETUP = 4 + 2 * masked
            if masked:
                pe.wait_ge(s_setup, SETUP)
            for i in range(NG):
                score_max(0, 0, i, first=True)
            transpose_maxima(0, 0)
            pe.wait_ge(s_setup, SETUP)
            pe.wait_ge(s_pj_out, 2 * ST + 2)

            def body(b, last):
                for t in range(ST):
                    project_v(b, t)
                for g in range(G):
                    bn_, gn = projected_in(b, g)
                    ahead = not (last and gn < 2)
                    pe.wait_ge(s_mrow[g % 2], (b * 2 + g // 2 + 1) * MROW)
                    for k in range(ST):
                        if g == 0 and k == 1:
                            pe.wait_ge(s_pj_out, b * PJ + V0 + ST + 2)
                        ms = [] if last and g == G - 1 else list(M_STEPS[k])
                        for j in range(HG):
                            score(b, g, k, j)
                            if k and j in (1, 2):
                                value_products(b, g, k - 1, j == 2)
                            for i in ms[M_SLOTS[k][j]:M_SLOTS[k][j + 1]]:
                                score_max(*next_group(b, g), i)
                        if g == 2 and k < 2 and not last:
                            transpose(b + 1, 2 * k)
                            transpose(b + 1, 2 * k + 1)
                        if k == 2 and ahead:
                            if gn == 0:
                                pe.wait_ge(s_ctx_lo, b + 2)
                            project_qk(bn_, 2 * gn)
                    value_products(b, g, ST - 1, False)
                    value_products(b, g, ST - 1, True)
                    if not (last and g == G - 1):
                        transpose_maxima(*next_group(b, g))
                    if ahead:
                        if gn == 0:
                            pe.wait_ge(s_pj_out, bn_ * PJ + T0 + ST + 2)
                        project_qk(bn_, 2 * gn + 1)
                pe.wait_ge(s_pj_out, (b + 1) * PJ + (0 if last else QK_A + 4) + 2)
                for t in range(ST):
                    if t >= 2:
                        pe.wait_ge(s_o_out, b * ST + t + 3)
                    pe.wait_ge(s_norm, (b + 1) * (G * ST) - ST + t + 2)
                    for g in range(G):
                        mm = pe.matmul(pj[:, t % 2, :], att[:, g, t * P:(t + 1) * P], wo[:, g, :],
                                       start=(g == 0), stop=(g == G - 1))
                    mm.then_inc(s_o, 1)

            with pe.Fori(0, B - 1) as b:
                body(b, False)
            body(B - 1, True)


I = 1536
IT = I // P
QBLOCK = 32
QMAX_A = 2.0 ** 15 - 1.0
QMAX_W = 2.0 ** 3 - 1.0
SCALE_MIN = 1e-12
SIG_ONE = 65536.0
NQ = B * IT // 4


def gated_mlp(nc, h_in, hmax_in, x_in, x_out, weights, gate, ident_in, spill):
    with ExitStack() as whole:
        def keep(name, shape, dt=F32):
            return whole.enter_context(nc.sbuf_tensor("m_" + name, shape, dt))

        scale = {n: keep("scale_" + n, [P, 1]) for n in ("h", "gate", "up", "silu", "out")}
        inv = {n: keep("inv_" + n, [P, 1]) for n in ("h", "gate", "up", "silu", "out")}
        peak = keep("peak", [P, 2])
        peak_all = keep("peak_all", [P, 2])
        mix = keep("mix", [P, 4])

        def find_scale(dve, link, name, top, unit):
            if unit is None:
                link(dve.tensor_scalar(scale[name][:], top, 1.0 / QMAX_A, SCALE_MIN, ALU.mult, ALU.max))
                link(dve.reciprocal(inv[name][:], scale[name][:]))
            else:
                link(dve.tensor_scalar(mix[:, 1:2], top, unit, 1.0 / QMAX_A, ALU.mult, ALU.mult))
                link(dve.tensor_scalar(scale[name][:], mix[:, 1:2], SCALE_MIN, None, ALU.max))
                link(dve.reciprocal(mix[:, 2:3], scale[name][:]))
                link(dve.tensor_tensor(inv[name][:], mix[:, 2:3], unit, ALU.mult))

        with ExitStack() as ctx:
            w_hi = ctx.enter_context(nc.sbuf_tensor("m_w_hi", [P, 2, DT, I], F32R))
            w_lo = ctx.enter_context(nc.sbuf_tensor("m_w_lo", [P, 2, DT, I], F32R))
            ident = ctx.enter_context(nc.sbuf_tensor("m_ident", [P, P], F32))
            mlp_weights(nc, weights, ident_in, ident, w_hi, w_lo, spill)
            mlp_inner(nc, h_in, hmax_in, ident, w_hi, w_lo, spill, scale, inv, peak, peak_all, find_scale)
        silu_q = keep("silu_q", [P, NQ, 4 * S], I16)
        mlp_silu(nc, spill, silu_q, scale, inv, peak, peak_all, mix, find_scale)
        mlp_product(nc, spill, silu_q, scale, inv, peak, peak_all, mix, find_scale)
        mlp_down(nc, spill, silu_q, x_in, x_out, gate, scale, inv)


def mlp_weights(nc, weights, ident_in, ident, w_hi, w_lo, spill):
    with ExitStack() as ctx:
        def sb(name, shape, dt=F32):
            return ctx.enter_context(nc.sbuf_tensor("mw_" + name, shape, dt))

        sem = stage_semaphores(nc, ctx, "mw_")

        NU, RB = 9, 4
        NB = D // QBLOCK
        raw = sb("raw", [P, 3, D])
        amax = sb("amax", [P, 2, NB])
        step = sb("step", [P, 2, NB])
        rstep = sb("rstep", [P, 2, NB])
        wi = sb("wi", [P, 2, D], I16)
        wq = sb("wq", [P, 2, D])
        down_hi = sb("down_hi", [P, 2, DT, P], F32R)
        down_lo = sb("down_lo", [P, 2, DT, P], F32R)
        pt = ctx.enter_context(nc.psum_tensor("mw_pt", [P, 2, 512], F32))
        s_raw = [sem(f"s_raw{i}") for i in range(3)]
        s_ident = sem("s_ident")
        s_amax = sem("s_amax")
        s_step = sem("s_step")
        s_rstep = sem("s_rstep")
        s_wi = sem("s_wi")
        s_wq = sem("s_wq")
        s_pt = sem("s_pt")
        s_hi = sem("s_hi")
        s_lo = sem("s_lo")
        s_down = [sem("s_down0"), sem("s_down1")]
        s_passed = sem("s_passed")
        s_passed_act = sem("s_passed_act")
        units = [(m, c) for c in range(3) for m in range(3)]
        block = ctx.enter_context(nc.Block())

        def store(sp, b, n, c):
            passed(sp, s_lo, b * NU + n + 3, s_passed)
            for part, src in enumerate((down_hi, down_lo)):
                dst = spill["down"][part, :, 4 * c:4 * c + 4, bass.ds(b * P, P)]
                sp.dma_start(dst, f32(src[:, c % 2])).then_inc(s_down[c % 2], 16)

        def spread(a):
            return a.rearrange("p (k o) -> p k o", o=1).to_broadcast([P, NB, QBLOCK])

        def where(b, m, c):
            if m == 2:
                return down_hi[:, c % 2], down_lo[:, c % 2]
            cut = bass.ds(b * (3 * P) + c * P, P)
            return w_hi[:, m, :, cut], w_lo[:, m, :, cut]

        @block.sync
        def _(sp):
            sp.dma_start(ident[:], ident_in).then_inc(s_ident, 16)
            with sp.Fori(0, RB) as b:
                for n, (m, c) in enumerate(units):
                    passed(sp, s_wi, b * NU + n + 1, s_passed)
                    if m < 2:
                        src = weights[m][bass.ds(b * (3 * P) + c * P, P), :]
                    else:
                        src = weights[2][bass.ds(b * P, P), c * D:(c + 1) * D]
                    sp.dma_start(raw[:, n % 3, :], src).then_inc(s_raw[n % 3], 16)
                    if n == 5:
                        store(sp, b, 2, 0)
                store(sp, b, 5, 1)
                store(sp, b, 8, 2)
            sp.wait_ge(s_down[0], 16 * 2 * (2 * RB + 1))
            sp.wait_ge(s_down[1], 16 * 2 * (RB + 1))

        @block.vector
        def _(dve):
            dve.sem_inc(s_wi, 3)
            dve.sem_inc(s_lo, 2)
            dve.sem_inc(s_down[0], 32)
            dve.sem_inc(s_down[1], 32)
            with dve.Fori(0, RB) as b:
                def split(n):
                    m, c = units[n]
                    dve.wait_ge(s_hi, b * NU + n + 1)
                    hi, lo = where(b, m, c)
                    dve.tensor_tensor(lo, pt[:, n % 2, :].rearrange("p (d o) -> p d o", d=DT), f32(hi),
                                      ALU.subtract).then_inc(s_lo, 1)

                for n, (m, c) in enumerate(units):
                    u, i = n % 2, b * NU + n + 1
                    v = raw[:, n % 3, :].rearrange("p (k s) -> p k s", s=QBLOCK)
                    dve.wait_ge(s_raw[n % 3], (b * 3 + n // 3 + 1) * 16)
                    dve.tensor_reduce(amax[:, u, :], v, AX.X, ALU.max, apply_absolute_value=True).then_inc(s_amax, 1)
                    dve.wait_ge(s_amax, i)
                    dve.tensor_scalar(step[:, u, :], amax[:, u, :], 1.0 / QMAX_W, SCALE_MIN,
                                      ALU.mult, ALU.max).then_inc(s_step, 1)
                    dve.wait_ge(s_step, i)
                    dve.reciprocal(rstep[:, u, :], step[:, u, :]).then_inc(s_rstep, 1)
                    dve.wait_ge(s_rstep, i)
                    dve.tensor_tensor(wi[:, u, :].rearrange("p (k s) -> p k s", s=QBLOCK), v,
                                      spread(rstep[:, u, :]), ALU.mult).then_inc(s_wi, 1)
                    dve.wait_ge(s_wi, i + 3)
                    if n >= 2:
                        dve.wait_ge(s_pt, b * NU + n - 1)
                    dve.tensor_tensor(wq[:, u, :].rearrange("p (k s) -> p k s", s=QBLOCK),
                                      wi[:, u, :].rearrange("p (k s) -> p k s", s=QBLOCK),
                                      spread(step[:, u, :]), ALU.mult).then_inc(s_wq, 1)
                    if n >= 1:
                        split(n - 1)
                split(NU - 1)

        @block.tensor
        def _(pe):
            pe.wait_ge(s_ident, 16)
            with pe.Fori(0, RB) as b:
                for n in range(NU):
                    pe.wait_ge(s_wq, b * NU + n + 1)
                    pe.wait_ge(s_lo, b * NU + n + 1)
                    for d in range(DT):
                        mm = pe.transpose(pt[:, n % 2, d * P:(d + 1) * P], wq[:, n % 2, d * P:(d + 1) * P], ident[:])
                    mm.then_inc(s_pt, 1)

        @block.scalar
        def _(act):
            with act.Fori(0, RB) as b:
                for n, (m, c) in enumerate(units):
                    if m == 2:
                        before = b * 2 + c // 2 + 1 if c % 2 == 0 else b + 1
                        act.wait_ge(s_down[c % 2], before * 32)
                    passed(act, s_pt, b * NU + n + 1, s_passed_act)
                    hi, _ = where(b, m, c)
                    act.activation(hi, pt[:, n % 2, :].rearrange("p (d o) -> p d o", d=DT), ACT.Copy).then_inc(s_hi, 1)


def mlp_inner(nc, h_in, hmax_in, ident, w_hi, w_lo, spill, scale, inv, peak, peak_all, find_scale):
    with ExitStack() as ctx:
        def sb(name, shape, dt=F32):
            return ctx.enter_context(nc.sbuf_tensor("mi_" + name, shape, dt))

        sem = stage_semaphores(nc, ctx, "mi_")

        h_tile = sb("h_tile", [P, 2, D])
        h_int = sb("h_int", [P, 2, D], I16)
        h_q = sb("h_q", [P, 2, D])
        ht_hi = sb("ht_hi", [P, DT, S], F32R)
        ht_lo = sb("ht_lo", [P, DT, S], F32R)
        out = sb("out", [P, 2, 4, S])
        peaks = sb("peaks", [P, 2, B * IT])
        pt = ctx.enter_context(nc.psum_tensor("mi_pt", [P, 2, 512], F32))
        pm = ctx.enter_context(nc.psum_tensor("mi_pm", [P, 4, 512], F32))
        s_peak_in = sem("s_peak_in")
        s_all = sem("s_all")
        s_link = sem("s_link")
        s_h_in = [sem("s_h_in0"), sem("s_h_in1")]
        s_int = sem("s_int")
        s_q = sem("s_q")
        s_pt = sem("s_pt")
        s_hi = sem("s_hi")
        s_lo = sem("s_lo")
        s_pm = sem("s_pm")
        s_out = sem("s_out")
        s_peak = sem("s_peak")
        s_store = [sem("s_store0"), sem("s_store1")]
        s_passed = sem("s_passed")
        s_fin = sem("s_fin")
        NM = 2 * IT
        NC = NM // 4
        tiles = [(m, 4 * c + k) for c in range(IT // 4) for m in range(2) for k in range(4)]
        block = ctx.enter_context(nc.Block())

        def hi(act, b, t):
            act.wait_ge(s_pt, b * ST + t + 1)
            act.activation(ht_hi[:, :, t * P:(t + 1) * P], pt[:, t % 2, :].rearrange("p (d t) -> p d t", d=DT),
                           ACT.Copy).then_inc(s_hi, 1)

        def lo(dve, b, t):
            dve.wait_ge(s_hi, b * ST + t + 1)
            dve.tensor_tensor(ht_lo[:, :, t * P:(t + 1) * P], pt[:, t % 2, :].rearrange("p (d t) -> p d t", d=DT),
                              f32(ht_hi[:, :, t * P:(t + 1) * P]), ALU.subtract).then_inc(s_lo, 1)

        @block.sync
        def _(sp):
            sp.dma_start(peak[:, 0:1], hmax_in).then_inc(s_peak_in, 16)

            def load(b, t):
                passed(sp, s_int, b * ST + t + 1, s_passed)
                sp.dma_start(h_tile[:, t % 2, :], h_in[b, t * P:(t + 1) * P, :]).then_inc(s_h_in[t % 2], 16)

            with sp.Fori(0, B) as b:
                for t in range(ST):
                    load(b, t)
                for c in range(NC):
                    passed(sp, s_peak, b * NM + 4 * c + 4, s_passed)
                    m, i = tiles[4 * c]
                    sp.dma_start(spill["raw"][m][b * (IT // 4) + i // 4], out[:, c % 2]).then_inc(s_store[c % 2], 16)
            for u in range(2):
                sp.wait_ge(s_store[u], 16 * (B * NC // 2 + 1))

        @block.scalar
        def _(act):
            with act.Fori(0, B) as b:
                for t in range(ST):
                    act.wait_ge(s_int, b * ST + t + 3)
                    if t >= 2:
                        act.wait_ge(s_pt, b * ST + t - 1)
                    act.activation(h_q[:, t % 2, :], h_int[:, t % 2, :], ACT.Copy).then_inc(s_q, 1)
                    if t >= 1:
                        hi(act, b, t - 1)
                hi(act, b, ST - 1)
                for n in range(NM):
                    act.wait_ge(s_pm, b * NM + n + 1)
                    if n % 4 == 0:
                        act.wait_ge(s_store[n // 4 % 2], (b * (NC // 2) + n // 8 + 1) * 16)
                    act.activation(out[:, n // 4 % 2, n % 4, :], pm[:, n % 4, :], ACT.Copy).then_inc(s_out, 1)

        @block.gpsimd
        def _(pool):
            pool.wait_ge(s_peak_in, 16)
            pool.partition_all_reduce(peak_all[:, 0:1], peak[:, 0:1], P, bass.bass_isa.ReduceOp.max).then_inc(s_all, 1)
            pool.wait_ge(s_fin, 2)
            pool.partition_all_reduce(peak_all[:], peak[:], P, bass.bass_isa.ReduceOp.max).then_inc(s_all, 1)

        @block.vector
        def _(dve):
            chain = [0]

            def link(ins):
                chain[0] += 1
                ins.then_inc(s_link, 1)
                dve.wait_ge(s_link, chain[0])

            dve.sem_inc(s_int, 2)
            dve.sem_inc(s_lo, 2)
            dve.sem_inc(s_store[0], 16)
            dve.sem_inc(s_store[1], 16)
            dve.wait_ge(s_all, 1)
            find_scale(dve, link, "h", peak_all[:, 0:1], None)
            with dve.Fori(0, B) as b:
                for t in range(ST):
                    dve.wait_ge(s_h_in[t % 2], (b * (ST // 2) + t // 2 + 1) * 16)
                    if t >= 2:
                        dve.wait_ge(s_q, b * ST + t - 1)
                    dve.tensor_scalar(h_int[:, t % 2, :], h_tile[:, t % 2, :], inv["h"][:], None,
                                      ALU.mult).then_inc(s_int, 1)
                    if t >= 1:
                        lo(dve, b, t - 1)
                lo(dve, b, ST - 1)
                for n, (m, i) in enumerate(tiles):
                    dve.wait_ge(s_out, b * NM + n + 1)
                    dve.tensor_reduce(peaks[:, m, bass.ds(b * IT + i, 1)], out[:, n // 4 % 2, n % 4, :], AX.X, ALU.max,
                                      apply_absolute_value=True).then_inc(s_peak, 1)
            dve.wait_ge(s_peak, B * NM)
            for m in range(2):
                dve.tensor_reduce(peak[:, m:m + 1], peaks[:, m, :], AX.X, ALU.max).then_inc(s_fin, 1)
            dve.wait_ge(s_all, 2)
            find_scale(dve, link, "gate", peak_all[:, 0:1], scale["h"][:])
            find_scale(dve, link, "up", peak_all[:, 1:2], scale["h"][:])

        @block.tensor
        def _(pe):
            with pe.Fori(0, B) as b:
                for t in range(ST):
                    pe.wait_ge(s_q, b * ST + t + 1)
                    pe.wait_ge(s_lo, b * ST + t + 1)
                    for d in range(DT):
                        mm = pe.transpose(pt[:, t % 2, d * P:(d + 1) * P], h_q[:, t % 2, d * P:(d + 1) * P], ident[:])
                    mm.then_inc(s_pt, 1)
                pe.wait_ge(s_lo, b * ST + ST + 2)
                for n, (m, i) in enumerate(tiles):
                    if n >= 4:
                        pe.wait_ge(s_out, b * NM + n - 3)
                    cut = slice(i * P, (i + 1) * P)
                    for d in range(DT):
                        ops = ((w_hi, ht_hi), (w_hi, ht_lo), (w_lo, ht_hi))
                        for p, (w, h) in enumerate(ops):
                            mm = pe.matmul(pm[:, n % 4, :], w[:, m, d, cut], h[:, d, :],
                                           start=(d == 0 and p == 0), stop=(d == DT - 1 and p == 2))
                    mm.then_inc(s_pm, 1)


def sigmoid_u16(dve, sig, out):
    return dve.tensor_scalar(out, sig, SIG_ONE, SIG_ONE - 1.0, ALU.mult, ALU.min)


def mlp_silu(nc, spill, silu_q, scale, inv, peak, peak_all, mix, find_scale):
    with ExitStack() as ctx:
        def sb(name, shape, dt=F32):
            return ctx.enter_context(nc.sbuf_tensor("ms_" + name, shape, dt))

        sem = stage_semaphores(nc, ctx, "ms_")

        W = 4 * S
        raw = sb("raw", [P, 2, W])
        sig = sb("sig", [P, 2, W])
        sig_q = sb("sig_q", [P, 2, W], U16)
        gabs = sb("gabs", [P, 2, W], I16)
        prod = sb("prod", [P, W])
        quad_peak = sb("quad_peak", [P, 2])
        s_raw = [sem("s_raw0"), sem("s_raw1")]
        s_int = sem("s_int")
        s_sig = sem("s_sig")
        s_abs = sem("s_abs")
        s_sig_q = sem("s_sig_q")
        s_peak = sem("s_peak")
        s_all = sem("s_all")
        s_link = sem("s_link")
        s_passed = sem("s_passed")
        s_passed_act = sem("s_passed_act")
        s_passed_dve = sem("s_passed_dve")
        s_top = sem("s_top")
        LAST = NQ // 2 - 1
        block = ctx.enter_context(nc.Block())

        @block.sync
        def _(sp):
            with sp.Fori(0, NQ // 2) as i:
                for u in range(2):
                    passed(sp, s_int, i * 2 + u + 1, s_passed)
                    sp.dma_start(raw[:, u].rearrange("p (k t) -> p k t", k=4), spill["raw"][0][i * 2 + u]).then_inc(s_raw[u], 16)

        @block.scalar
        def _(act):
            with act.Fori(0, NQ // 2) as i:
                for u in range(2):
                    n = i * 2 + u
                    q = silu_q[:, bass.ds(n, 1), :].rearrange("p o w -> p (o w)")
                    act.wait_ge(s_sig_q, n + 1)
                    passed(act, s_int, n + 3, s_passed_act)
                    act.activation(sig[:, u], q, ACT.Sigmoid, scale=scale["gate"][:]).then_inc(s_sig, 1)
                    passed(act, s_peak, n + 1, s_passed_act)
                    act.activation(gabs[:, u], q, ACT.Abs).then_inc(s_abs, 1)

        @block.vector
        def _(dve):
            chain = [0]

            def link(ins):
                chain[0] += 1
                ins.then_inc(s_link, 1)
                dve.wait_ge(s_link, chain[0])

            def to_int(i, u, n):
                dve.wait_ge(s_raw[u], (i + 1) * 16)
                dve.tensor_scalar(silu_q[:, bass.ds(n, 1), :].rearrange("p o w -> p (o w)"), raw[:, u],
                                  inv["gate"][:], None, ALU.mult).then_inc(s_int, 1)

            def body(i, last):
                for u in range(2):
                    n = i * 2 + u
                    if not (last and u == 1):
                        to_int(i + u, 1 - u, n + 1)
                    dve.wait_ge(s_sig, n + 1)
                    sigmoid_u16(dve, sig[:, u], sig_q[:, u]).then_inc(s_sig_q, 1)
                    dve.wait_ge(s_sig_q, n + 3)
                    passed(dve, s_abs, n + 1, s_passed_dve)
                    dve.tensor_tensor_reduce(prod[:], gabs[:, u], sig_q[:, u], 1.0, 0.0, ALU.mult, ALU.max,
                                             quad_peak[:, u:u + 1]).then_inc(s_peak, 1)
                    dve.wait_ge(s_peak, n + 3)
                    dve.wait_ge(s_top, n + 1)
                    dve.tensor_tensor(peak[:, 0:1], peak[:, 0:1], quad_peak[:, u:u + 1], ALU.max).then_inc(s_top, 1)

            for s in (s_int, s_sig_q, s_peak):
                dve.sem_inc(s, 2)
            dve.memset(peak[:, 0:1], 0.0).then_inc(s_top, 1)
            to_int(0, 0, 0)
            with dve.Fori(0, LAST) as i:
                body(i, False)
            body(LAST, True)
            dve.wait_ge(s_all, 1)
            link(dve.tensor_scalar(mix[:, 0:1], scale["gate"][:], 1.0 / SIG_ONE, None, ALU.mult))
            find_scale(dve, link, "silu", peak_all[:, 0:1], mix[:, 0:1])

        @block.gpsimd
        def _(pool):
            pool.wait_ge(s_top, NQ + 1)
            pool.partition_all_reduce(peak_all[:, 0:1], peak[:, 0:1], P, bass.bass_isa.ReduceOp.max).then_inc(s_all, 1)


def mlp_product(nc, spill, silu_q, scale, inv, peak, peak_all, mix, find_scale):
    with ExitStack() as ctx:
        def sb(name, shape, dt=F32):
            return ctx.enter_context(nc.sbuf_tensor("mp_" + name, shape, dt))

        sem = stage_semaphores(nc, ctx, "mp_")

        W = 4 * S
        raw = sb("raw", [P, 2, W])
        sig = sb("sig", [P, 2, W])
        sig_q = sb("sig_q", [P, W], U16)
        silu = sb("silu", [P, W])
        uabs = sb("uabs", [P, 2, W], I16)
        sabs = sb("sabs", [P, 2, W], I16)
        prod = sb("prod", [P, W])
        quad_peak = sb("quad_peak", [P, 2])
        s_raw = [sem("s_raw0"), sem("s_raw1")]
        s_sig = sem("s_sig")
        s_sig_q = sem("s_sig_q")
        s_silu = sem("s_silu")
        s_int = sem("s_int")
        s_uabs = sem("s_uabs")
        s_sabs = sem("s_sabs")
        s_peak = sem("s_peak")
        s_all = sem("s_all")
        s_link = sem("s_link")
        s_passed = sem("s_passed")
        s_passed_act = sem("s_passed_act")
        s_passed_dve = sem("s_passed_dve")
        s_top = sem("s_top")
        LAST = NQ // 2 - 1
        block = ctx.enter_context(nc.Block())

        def quad(n):
            return silu_q[:, bass.ds(n, 1), :].rearrange("p o w -> p (o w)")

        @block.sync
        def _(sp):
            with sp.Fori(0, NQ // 2) as i:
                for u in range(2):
                    passed(sp, s_uabs, i * 2 + u + 1, s_passed)
                    sp.dma_start(raw[:, u].rearrange("p (k t) -> p k t", k=4), spill["raw"][1][i * 2 + u]).then_inc(s_raw[u], 16)

        @block.scalar
        def _(act):
            def sigmoid(u, n):
                passed(act, s_sig_q, n + 1, s_passed_act)
                act.activation(sig[:, u], quad(n), ACT.Sigmoid, scale=scale["gate"][:]).then_inc(s_sig, 1)

            def body(i, last):
                for u in range(2):
                    n = i * 2 + u
                    if not (last and u == 1):
                        sigmoid(1 - u, n + 1)
                    act.wait_ge(s_raw[u], (i + 1) * 16)
                    act.wait_ge(s_peak, n + 1)
                    act.activation(uabs[:, u], raw[:, u], ACT.Abs, scale=inv["up"][:]).then_inc(s_uabs, 1)
                    passed(act, s_int, n + 1, s_passed_act)
                    act.activation(sabs[:, u], quad(n), ACT.Abs).then_inc(s_sabs, 1)

            act.wait_ge(s_uabs, 2)
            sigmoid(0, 0)
            with act.Fori(0, LAST) as i:
                body(i, False)
            body(LAST, True)

        @block.vector
        def _(dve):
            chain = [0]

            def link(ins):
                chain[0] += 1
                ins.then_inc(s_link, 1)
                dve.wait_ge(s_link, chain[0])

            def measure(u, n):
                dve.wait_ge(s_uabs, n + 3)
                passed(dve, s_sabs, n + 1, s_passed_dve)
                dve.tensor_tensor_reduce(prod[:], sabs[:, u], uabs[:, u], 1.0, 0.0, ALU.mult, ALU.max,
                                         quad_peak[:, u:u + 1]).then_inc(s_peak, 1)
                dve.wait_ge(s_peak, n + 3)
                dve.wait_ge(s_top, n + 1)
                dve.tensor_tensor(peak[:, 0:1], peak[:, 0:1], quad_peak[:, u:u + 1], ALU.max).then_inc(s_top, 1)

            def to_silu(u, n):
                dve.wait_ge(s_sig, n + 1)
                sigmoid_u16(dve, sig[:, u], sig_q[:]).then_inc(s_sig_q, 1)
                dve.wait_ge(s_sig_q, n + 3)
                dve.tensor_tensor(silu[:], quad(n), sig_q[:], ALU.mult).then_inc(s_silu, 1)
                dve.wait_ge(s_silu, n + 1)
                dve.tensor_scalar(quad(n), silu[:], inv["silu"][:], None, ALU.mult).then_inc(s_int, 1)

            def body(i, last):
                for u in range(2):
                    n = i * 2 + u
                    if not (last and u == 1):
                        to_silu(1 - u, n + 1)
                    measure(u, n)

            for s in (s_sig_q, s_peak, s_uabs):
                dve.sem_inc(s, 2)
            dve.memset(peak[:, 0:1], 0.0).then_inc(s_top, 1)
            to_silu(0, 0)
            with dve.Fori(0, LAST) as i:
                body(i, False)
            body(LAST, True)
            dve.wait_ge(s_all, 1)
            link(dve.tensor_tensor(mix[:, 0:1], scale["silu"][:], scale["up"][:], ALU.mult))
            find_scale(dve, link, "out", peak_all[:, 0:1], mix[:, 0:1])

        @block.gpsimd
        def _(pool):
            pool.wait_ge(s_top, NQ + 1)
            pool.partition_all_reduce(peak_all[:, 0:1], peak[:, 0:1], P, bass.bass_isa.ReduceOp.max).then_inc(s_all, 1)


def mlp_down(nc, spill, silu_q, x_in, x_out, gate, scale, inv):
    with ExitStack() as ctx:
        def sb(name, shape, dt=F32):
            return ctx.enter_context(nc.sbuf_tensor("md_" + name, shape, dt))

        sem = stage_semaphores(nc, ctx, "md_")

        W = 2 * S
        NP = IT // 2
        wd = [sb("wd_hi", [P, IT, D], F32R), sb("wd_lo", [P, IT, D], F32R)]
        raw = sb("raw", [P, 2, W])
        up_q = sb("up_q", [P, W], I16)
        prod = sb("prod", [P, W])
        prod_q = sb("prod_q", [P, 2, W], I16)
        p_hi = sb("p_hi", [P, 2, 2, S], F32R)
        p_lo = sb("p_lo", [P, 2, 2, S], F32R)
        x_new = sb("x_new", [P, 2, D])
        gate_col = sb("gate_col", [P, 1])
        tanh_g = sb("tanh_g", [P, 1])
        factor = sb("factor", [P, 1])
        pd = ctx.enter_context(nc.psum_tensor("md_pd", [P, 2, ST, 512], F32))
        s_wd = sem("s_wd")
        s_gate = sem("s_gate")
        s_raw = [sem("s_raw0"), sem("s_raw1")]
        s_up = sem("s_up")
        s_prod = sem("s_prod")
        s_int = sem("s_int")
        s_hi = sem("s_hi")
        s_lo = sem("s_lo")
        s_used = sem("s_used")
        s_x = [sem("s_x0"), sem("s_x1")]
        s_new = sem("s_new")
        s_store = [sem("s_store0"), sem("s_store1")]
        s_tanh = sem("s_tanh")
        s_factor = sem("s_factor")
        s_passed = sem("s_passed")
        block = ctx.enter_context(nc.Block())

        def store(sp, b, t):
            passed(sp, s_new, b * ST + t + 1 + 2 * ST, s_passed)
            sp.dma_start(x_out[b, t * P:(t + 1) * P, :], x_new[:, t % 2, :]).then_inc(s_store[t % 2], 16)

        @block.sync
        def _(sp):
            for part in range(2):
                sp.dma_start(f32(wd[part][:]), spill["down"][part]).then_inc(s_wd, 16)
            sp.dma_start(gate_col[:], gate).then_inc(s_gate, 16)

            def load_x(b, t):
                passed(sp, s_store[t % 2], (b * 2 + t // 2 + 1) * 16, s_passed)
                sp.dma_start(x_new[:, t % 2, :], x_in[b, t * P:(t + 1) * P, :]).then_inc(s_x[t % 2], 16)

            def body(bb, first):
                for v in range(2):
                    b = bb * 2 + v
                    for c in range(NP):
                        passed(sp, s_up, b * NP + c + 1, s_passed)
                        sp.dma_start(raw[:, c % 2].rearrange("p (k t) -> p k t", k=2),
                                     spill["raw"][1][b * (NP // 2) + c // 2][:, 2 * (c % 2):2 * (c % 2) + 2, :]
                                     ).then_inc(s_raw[c % 2], 16)
                        if not (first and v == 0):
                            if 1 <= c <= ST:
                                load_x(b - 1, c - 1)
                            if 2 <= c <= ST + 1:
                                store(sp, b - 1, c - 2)

            body(0, True)
            with sp.Fori(1, B // 2) as bb:
                body(bb, False)
            for t in range(ST):
                load_x(B - 1, t)
                if t >= 1:
                    store(sp, B - 1, t - 1)
            store(sp, B - 1, ST - 1)
            for u in range(2):
                sp.wait_ge(s_store[u], 16 * (B * 2 + 1))

        @block.scalar
        def _(act):
            act.wait_ge(s_gate, 16)
            act.activation(tanh_g[:], gate_col[:], ACT.Tanh).then_inc(s_tanh, 1)
            with act.Fori(0, B // 2) as bb:
                for v in range(2):
                    for c in range(NP):
                        n = bb * (2 * NP) + v * NP + c
                        act.wait_ge(s_int, n + 1)
                        act.wait_ge(s_used, n + 1)
                        act.activation(p_hi[:, c % 2].rearrange("p k t -> p (k t)"), prod_q[:, c % 2], ACT.Copy).then_inc(s_hi, 1)

        @block.vector
        def _(dve):
            dve.sem_inc(s_up, 2)
            dve.sem_inc(s_used, 2)
            dve.sem_inc(s_new, 2 * ST)
            dve.sem_inc(s_store[0], 16)
            dve.sem_inc(s_store[1], 16)
            dve.wait_ge(s_tanh, 1)
            dve.tensor_tensor(factor[:], tanh_g[:], scale["out"][:], ALU.mult).then_inc(s_factor, 1)
            dve.wait_ge(s_factor, 1)

            def to_lo(b, c):
                dve.wait_ge(s_hi, b * NP + c + 1)
                dve.tensor_tensor(p_lo[:, c % 2].rearrange("p k t -> p (k t)"), prod_q[:, c % 2],
                                  f32(p_hi[:, c % 2]).rearrange("p k t -> p (k t)"), ALU.subtract).then_inc(s_lo, 1)

            def take_out(b, v, t):
                dve.wait_ge(s_x[t % 2], (b * 2 + t // 2 + 1) * 16)
                dve.wait_ge(s_used, (b + 1) * NP + 2)
                dve.scalar_tensor_tensor(x_new[:, t % 2, :], pd[:, v, t, :], factor[:], x_new[:, t % 2, :],
                                         ALU.mult, ALU.add).then_inc(s_new, 1)

            def body(bb, first):
                for v in range(2):
                    b = bb * 2 + v
                    for c in range(NP):
                        i = b * NP + c + 1
                        quad = b * (NP // 2) + c // 2
                        q = silu_q[:, bass.ds(quad, 1), (c % 2) * W:(c % 2 + 1) * W].rearrange("p o w -> p (o w)")
                        dve.wait_ge(s_raw[c % 2], (quad + 1) * 16)
                        dve.tensor_scalar(up_q[:], raw[:, c % 2], inv["up"][:], None, ALU.mult).then_inc(s_up, 1)
                        dve.wait_ge(s_up, i + 2)
                        dve.tensor_tensor(prod[:], q, up_q[:], ALU.mult).then_inc(s_prod, 1)
                        dve.wait_ge(s_prod, i)
                        dve.tensor_scalar(prod_q[:, c % 2], prod[:], inv["out"][:], None, ALU.mult).then_inc(s_int, 1)
                        if c >= 1:
                            to_lo(b, c - 1)
                        if 1 <= c <= ST and not (first and v == 0):
                            take_out(b - 1, 1 - v, c - 1)
                    to_lo(b, NP - 1)

            body(0, True)
            with dve.Fori(1, B // 2) as bb:
                body(bb, False)
            for t in range(ST):
                take_out(B - 1, 1, t)

        @block.tensor
        def _(pe):
            pe.wait_ge(s_wd, 32)
            with pe.Fori(0, B // 2) as bb:
                for v in range(2):
                    for c in range(NP):
                        pe.wait_ge(s_lo, bb * (2 * NP) + v * NP + c + 1)
                        if c == 0:
                            pe.wait_ge(s_new, bb * (2 * ST) + (v + 1) * ST)
                        for t in range(ST):
                            cut = slice(t * P, (t + 1) * P)
                            for k in range(2):
                                i = 2 * c + k
                                ops = ((p_hi, 0), (p_hi, 1), (p_lo, 0))
                                for p, (lhs, part) in enumerate(ops):
                                    mm = pe.matmul(pd[:, v, t, :], lhs[:, c % 2, k, cut], wd[part][:, i, :],
                                                   start=(i == 0 and p == 0), stop=(i == IT - 1 and p == 2))
                        mm.then_inc(s_used, 1)


E_N = 8
TOP = 2
F = 1024
FT = F // P
CAP = max(1, -(-5 * T * TOP // (4 * E_N)))
SLOTS = E_N * CAP
CT = 5
CW = CT * P
CHUNKS = SLOTS // CW
CE = CHUNKS // E_N
WEIGHT_MIN = 1e-9


def mixture(nc, h_in, x_in, x_out, router_w, router_b, w1, w2, b1, b2, gate, consts, spill):
    with ExitStack() as whole:
        def keep(name, shape, dt=F32):
            return whole.enter_context(nc.sbuf_tensor("x_" + name, shape, dt))

        token_of = keep("token_of", [P, SLOTS // P + CT], I32)
        slot_of = keep("slot_of", [P, NT, TOP], I32)
        weight = keep("weight", [P, NT, TOP])
        route(nc, h_in, router_w, router_b, gate, consts, spill["tokens"], token_of, slot_of, weight)
        experts(nc, h_in, w1, w2, b1, b2, consts["ident"], token_of, spill["expert_out"])
        combine(nc, spill["expert_out"], x_in, x_out, slot_of, weight)


def route(nc, h_in, router_w, router_b, gate, consts, tokens, token_of, slot_of, weight):
    with ExitStack() as ctx:
        def sb(name, shape, dt=F32):
            return ctx.enter_context(nc.sbuf_tensor("r_" + name, shape, dt))

        def ps(name, shape):
            return ctx.enter_context(nc.psum_tensor("r_" + name, shape, F32))

        sem = stage_semaphores(nc, ctx, "r_")

        h = sb("h", [P, 2, ST, D])
        h_t = sb("h_t", [P, 2, D])
        rw = sb("rw", [P, DT, E_N])
        rb = sb("rb", [P, E_N])
        ident = sb("ident", [P, P])
        before = sb("before", [P, P])
        ones = sb("ones", [P, P])
        expert = sb("expert", [P, NT, E_N])
        spare = sb("spare", [P, NT, TOP])
        token_id = sb("token_id", [P, NT], I32)
        gate_col = sb("gate_col", [P, 1])
        tanh_g = sb("tanh_g", [P, 1])
        zeros = sb("zeros", [P, (SLOTS + T * TOP) // P], I32)
        prob = sb("prob", [P, NT, E_N])
        row = sb("row", [P, NT])
        top_p = sb("top_p", [P, NT, 8])
        top_i = sb("top_i", [P, NT, 8], U32)
        top_e = sb("top_e", [P, NT, TOP])
        hot = [sb("hot0", [P, NT, E_N]), sb("hot1", [P, NT, E_N])]
        taken = sb("taken", [P, NT, E_N])
        base = [sb("base0", [P, NT, E_N]), sb("base1", [P, NT, E_N])]
        rank = sb("rank", [P, NT, TOP])
        kept = sb("kept", [P, NT, TOP])
        cell = sb("cell", [P, NT, TOP])
        put_at = sb("put_at", [P, NT, TOP], I32)
        table = sb("table", [SLOTS // P, P], I32)
        table_f = sb("table_f", [SLOTS // P, P])
        pt = ps("pt", [P, 2, 512])
        pl = ps("pl", [P, 2, 512])
        pr = ps("pr", [P, 2, 512])
        pk = ps("pk", [P, 512])
        s_const = sem("s_const")
        s_h = [sem("s_h0"), sem("s_h1")]
        s_pt = sem("s_pt")
        s_ht = sem("s_ht")
        s_logit = sem("s_logit")
        s_prob = sem("s_prob")
        s_link = sem("s_link")
        s_exp_in = sem("s_exp_in")
        s_exp = sem("s_exp")
        s_tanh = sem("s_tanh")
        s_taken = sem("s_taken")
        s_count = sem("s_count")
        s_put_at = sem("s_put_at")
        s_zero = sem("s_zero")
        s_zeroed = sem("s_zeroed")
        s_put = sem("s_put")
        s_table = sem("s_table")
        s_table_f = sem("s_table_f")
        s_turned = sem("s_turned")
        s_token_of = sem("s_token_of")
        s_passed = sem("s_passed")
        s_passed_dve = sem("s_passed_dve")
        NCONST = 8 * 16
        block = ctx.enter_context(nc.Block())

        def over_experts(a):
            return a.rearrange("p (t o) -> p t o", o=1).to_broadcast([P, NT, E_N])

        @block.sync
        def _(sp):
            for dst, src in ((ident, consts["ident"]), (before, consts["before"]), (expert, consts["expert"]),
                             (spare, consts["spare"]), (token_id, consts["token_id"]), (rw, router_w),
                             (rb, router_b), (gate_col, gate)):
                sp.dma_start(dst[:], src).then_inc(s_const, 16)
            sp.wait_ge(s_zero, 1)
            sp.dma_start(tokens.rearrange("(p n) o -> p (n o)", p=P), zeros[:]).then_inc(s_zeroed, 16)
            with sp.Fori(0, B // 2) as bb:
                for v in range(2):
                    passed(sp, s_pt, (bb * 2 + v + 1) * ST, s_passed)
                    sp.dma_start(h[:, v], h_in[bb * 2 + v].rearrange("(t p) d -> p t d", p=P)).then_inc(s_h[v], 16)
            sp.wait_ge(s_put, TOP * NT * 16)
            sp.dma_start(table[:], tokens[0:SLOTS].rearrange("(n p) o -> n (p o)", p=P)).then_inc(s_table, 16)

        @block.scalar
        def _(act):
            act.wait_ge(s_const, NCONST)
            act.activation(tanh_g[:], gate_col[:], ACT.Tanh).then_inc(s_tanh, 1)
            with act.Fori(0, B // 2) as bb:
                for n in range(2 * ST):
                    i = bb * (2 * ST) + n
                    act.wait_ge(s_pt, i + 1 + 2 * ST)
                    act.wait_ge(s_logit, i + 1)
                    act.activation(h_t[:, n % 2, :], pt[:, n % 2, :], ACT.Copy).then_inc(s_ht, 1)
            act.wait_ge(s_exp_in, 1)
            act.activation(prob[:], prob[:], ACT.Exp).then_inc(s_exp, 1)

        @block.tensor
        def _(pe):
            def logits(bb, n):
                i = bb * (2 * ST) + n
                v, t = n // ST, n % ST
                if t == 0:
                    pe.wait_ge(s_prob, bb * 2 + v + 1)
                pe.wait_ge(s_ht, i + 3)
                for d in range(DT):
                    mm = pe.matmul(pl[:, v, t * E_N:(t + 1) * E_N], h_t[:, n % 2, d * P:(d + 1) * P], rw[:, d, :],
                                   start=(d == 0), stop=(d == DT - 1))
                mm.then_inc(s_logit, 1)

            pe.wait_ge(s_const, NCONST)
            with pe.Fori(0, B // 2) as bb:
                for n in range(2 * ST):
                    v, t = n // ST, n % ST
                    if t == 0:
                        pe.wait_ge(s_h[v], (bb + 1) * 16)
                    pe.wait_ge(s_ht, bb * (2 * ST) + n + 1)
                    for d in range(DT):
                        mm = pe.transpose(pt[:, n % 2, d * P:(d + 1) * P], h[:, v, t, d * P:(d + 1) * P], ident[:])
                    mm.then_inc(s_pt, 1)
                    if n >= 1:
                        logits(bb, n - 1)
                logits(bb, 2 * ST - 1)
            pe.wait_ge(s_taken, 1)
            flat = taken[:].rearrange("p t e -> p (t e)")
            pe.matmul(pr[:, 0, :NT * E_N], before[:], flat, start=True, stop=True).then_inc(s_count, 1)
            pe.matmul(pr[:, 1, :NT * E_N], ones[:], flat, start=True, stop=True).then_inc(s_count, 1)
            pe.wait_ge(s_table_f, 1)
            pe.transpose(pk[:, :SLOTS // P], table_f[:], ident[:SLOTS // P, :SLOTS // P]).then_inc(s_turned, 1)

        @block.vector
        def _(dve):
            chain = [0]

            def link(ins):
                chain[0] += 1
                ins.then_inc(s_link, 1)
                dve.wait_ge(s_link, chain[0])

            dve.sem_inc(s_pt, 2 * ST)
            dve.sem_inc(s_ht, 2)
            dve.sem_inc(s_logit, 2)
            dve.sem_inc(s_prob, 2)
            dve.memset(zeros[:], 0).then_inc(s_zero, 1)
            link(dve.memset(ones[:], 1.0))
            dve.wait_ge(s_tanh, 1)
            with dve.Fori(0, B // 2) as bb:
                for v in range(2):
                    b = bb * 2 + v
                    dve.wait_ge(s_logit, (b + 1) * ST + 2)
                    dve.tensor_tensor(prob[:, bass.ds(b * ST, ST), :],
                                      pl[:, v, :ST * E_N].rearrange("p (t e) -> p t e", e=E_N),
                                      rb[:].rearrange("p (o e) -> p o e", o=1).to_broadcast([P, ST, E_N]),
                                      ALU.add).then_inc(s_prob, 1)
            dve.wait_ge(s_prob, B + 2)
            link(dve.tensor_reduce(row[:], prob[:], AX.X, ALU.max))
            dve.tensor_tensor(prob[:], prob[:], over_experts(row[:]), ALU.subtract).then_inc(s_exp_in, 1)
            dve.wait_ge(s_exp, 1)
            link(dve.tensor_reduce(row[:], prob[:], AX.X, ALU.add))
            link(dve.reciprocal(row[:], row[:]))
            link(dve.tensor_tensor(prob[:], prob[:], over_experts(row[:]), ALU.mult))
            for t in range(NT):
                ins = dve.max(top_p[:, t, :], prob[:, t, :])
            link(ins)
            for t in range(NT):
                ins = dve.max_index(top_i[:, t, :], top_p[:, t, :], prob[:, t, :])
            link(ins)
            link(dve.tensor_copy(top_e[:], top_i[:, :, 0:TOP]))
            for k in range(TOP):
                ins = dve.tensor_tensor(hot[k][:], expert[:], top_e[:, :, k:k + 1].to_broadcast([P, NT, E_N]),
                                        ALU.is_equal)
            link(ins)
            dve.tensor_tensor(taken[:], hot[0][:], hot[1][:], ALU.add).then_inc(s_taken, 1)
            link(dve.tensor_tensor(row[:], top_p[:, :, 0], top_p[:, :, 1], ALU.add))
            link(dve.tensor_scalar(row[:], row[:], WEIGHT_MIN, None, ALU.max))
            link(dve.reciprocal(row[:], row[:]))
            link(dve.tensor_scalar(row[:], row[:], tanh_g[:], None, ALU.mult))
            link(dve.tensor_tensor(weight[:], top_p[:, :, 0:TOP],
                                   row[:].rearrange("p (t o) -> p t o", o=1).to_broadcast([P, NT, TOP]), ALU.mult))
            dve.wait_ge(s_count, 2)
            link(dve.memset(base[0][:, 0:1, :], 0.0))
            link(dve.tensor_copy(base[0][:, 1:, :].rearrange("p t e -> p (t e)"), pr[:, 1, :(NT - 1) * E_N]))
            reach, u = 1, 0
            while reach < NT:
                old, new = base[u], base[1 - u]
                dve.tensor_copy(new[:, :reach, :], old[:, :reach, :])
                link(dve.tensor_tensor(new[:, reach:, :], old[:, reach:, :], old[:, :NT - reach, :], ALU.add))
                reach, u = 2 * reach, 1 - u
            ranks, spent = base[u], base[1 - u]
            link(dve.tensor_tensor(ranks[:].rearrange("p t e -> p (t e)"), ranks[:].rearrange("p t e -> p (t e)"),
                                   pr[:, 0, :NT * E_N], ALU.add))
            for k in range(TOP):
                link(dve.tensor_tensor(spent[:], hot[k][:], ranks[:], ALU.mult))
                link(dve.tensor_reduce(rank[:, :, k], spent[:], AX.X, ALU.add))
            link(dve.tensor_scalar(kept[:], rank[:], float(CAP), None, ALU.is_lt))
            link(dve.tensor_tensor(weight[:], weight[:], kept[:], ALU.mult))
            link(dve.scalar_tensor_tensor(cell[:], top_e[:], float(CAP), rank[:], ALU.mult, ALU.add))
            link(dve.tensor_tensor(cell[:], cell[:], spare[:], ALU.subtract))
            link(dve.tensor_tensor(cell[:], cell[:], kept[:], ALU.mult))
            link(dve.tensor_tensor(cell[:], cell[:], spare[:], ALU.add))
            dve.tensor_copy(put_at[:], cell[:]).then_inc(s_put_at, 1)
            link(dve.tensor_scalar(rank[:], rank[:], float(CAP - 1), None, ALU.min))
            dve.wait_ge(s_put_at, 1)
            link(dve.scalar_tensor_tensor(cell[:], top_e[:], float(CAP), rank[:], ALU.mult, ALU.add))
            link(dve.tensor_copy(slot_of[:], cell[:]))
            dve.wait_ge(s_table, 16)
            dve.tensor_copy(table_f[:], table[:]).then_inc(s_table_f, 1)
            dve.wait_ge(s_turned, 1)
            dve.tensor_copy(token_of[:, :SLOTS // P], pk[:, :SLOTS // P]).then_inc(s_token_of, 1)
            dve.memset(token_of[:, SLOTS // P:], 0).then_inc(s_token_of, 1)
            dve.wait_ge(s_token_of, 2)

        @block.gpsimd
        def _(pool):
            pool.wait_ge(s_zeroed, 16)
            pool.wait_ge(s_put_at, 1)
            for t in range(NT):
                for k in range(TOP):
                    pool.indirect_dma_start(tokens, bass.IndirectOffsetOnAxis(put_at[:, t, k:k + 1], 0),
                                            token_id[:, t:t + 1], None).then_inc(s_put, 16)


def experts(nc, h_in, w1, w2, b1, b2, ident_in, token_of, expert_out):
    rows = h_in.rearrange("b s d -> (b s) d")
    with ExitStack() as ctx:
        def sb(name, shape, dt=F32):
            return ctx.enter_context(nc.sbuf_tensor("e_" + name, shape, dt))

        sem = stage_semaphores(nc, ctx, "e_")

        HALF = CW // 2
        W2CUT = FT // 2
        raw1 = sb("raw1", [P, DT, F])
        raw2 = sb("raw2", [P, FT, D])
        w1_hi = sb("w1_hi", [P, DT, F], F32R)
        w1_lo = sb("w1_lo", [P, DT, F], F32R)
        w2_hi = sb("w2_hi", [P, FT, D], F32R)
        w2_lo = sb("w2_lo", [P, FT, D], F32R)
        b1_all = sb("b1_all", [P, E_N, FT])
        b1_col = sb("b1_col", [P, FT])
        b2_row = sb("b2_row", [P, D])
        ident = sb("ident", [P, P])
        index = sb("index", [P, 2, CT], I32)
        x = sb("x", [P, 2, CT, D])
        xt_hi = sb("xt_hi", [P, DT, CW], F32R)
        xt_lo = sb("xt_lo", [P, DT, CW], F32R)
        g = sb("g", [P, 2, CW])
        g_hi = sb("g_hi", [P, FT, CW], F32R)
        g_lo = sb("g_lo", [P, FT, CW], F32R)
        out = sb("out", [P, CT, D])
        pt = ctx.enter_context(nc.psum_tensor("e_pt", [P, 2, 512], F32))
        ph = ctx.enter_context(nc.psum_tensor("e_ph", [P, 2, 2, 512], F32))
        po = ctx.enter_context(nc.psum_tensor("e_po", [P, 2, 512], F32))
        s_const = sem("s_const")
        s_raw1 = sem("s_raw1")
        s_raw2 = sem("s_raw2")
        s_w1_hi = sem("s_w1_hi")
        s_w1_lo = sem("s_w1_lo")
        s_w2_hi = sem("s_w2_hi")
        s_w2_lo = sem("s_w2_lo")
        s_b1 = sem("s_b1")
        s_b2 = sem("s_b2")
        s_index = sem("s_index")
        s_x = [sem("s_x0"), sem("s_x1")]
        s_pt = sem("s_pt")
        s_xt_hi = sem("s_xt_hi")
        s_xt = sem("s_xt")
        s_ph = sem("s_ph")
        s_g = sem("s_g")
        s_g_hi = sem("s_g_hi")
        s_g_lo = sem("s_g_lo")
        s_po = sem("s_po")
        s_out = sem("s_out")
        s_store = sem("s_store")
        s_passed = sem("s_passed")
        s_passed_pool = sem("s_passed_pool")
        block = ctx.enter_context(nc.Block())

        def load(sp, e):
            first = isinstance(e, int)
            if not first:
                passed(sp, s_w1_lo, e, s_passed)
            sp.dma_start(raw1[:], w1[e]).then_inc(s_raw1, 16)
            if not first:
                passed(sp, s_w2_lo, 2 * e, s_passed)
            sp.dma_start(raw2[:], w2[e]).then_inc(s_raw2, 16)

        def load_b2(sp, e):
            passed(sp, s_out, e * (CE * CT) + 2, s_passed)
            sp.dma_start(b2_row[:], b2[bass.ds(e, 1), :].to_broadcast([P, D])).then_inc(s_b2, 16)

        def store(sp, e, c):
            passed(sp, s_out, (e * CE + c + 1) * CT + 2, s_passed)
            dst = expert_out[bass.ds(e * CAP + c * CW, CW), :].rearrange("(t p) d -> p t d", p=P)
            sp.dma_start(dst, out[:]).then_inc(s_store, 16)

        @block.sync
        def _(sp):
            sp.dma_start(ident[:], ident_in).then_inc(s_const, 16)
            sp.dma_start(b1_all[:], b1).then_inc(s_const, 16)
            load(sp, 0)
            load_b2(sp, 0)
            store(sp, 0, 0)
            with sp.Fori(1, E_N) as e:
                load(sp, e)
                store(sp, e - 1, 1)
                load_b2(sp, e)
                store(sp, e, 0)
            store(sp, E_N - 1, 1)
            sp.wait_ge(s_store, (CHUNKS + 1) * 16)

        @block.gpsimd
        def _(pool):
            def gather(n, c):
                passed(pool, s_index, n + 1, s_passed_pool)
                for s in range(CT):
                    pool.indirect_dma_start(x[:, c, s, :], None, rows,
                                            bass.IndirectOffsetOnAxis(index[:, c, s:s + 1], 0)).then_inc(s_x[c], 16)

            gather(0, 0)
            with pool.Fori(0, E_N) as e:
                pool.wait_ge(s_w1_hi, e + 1)
                pool.tensor_tensor(w1_lo[:], raw1[:], f32(w1_hi[:]), ALU.subtract).then_inc(s_w1_lo, 1)
                gather(e * CE + 1, 1)
                for half in range(2):
                    cut = slice(half * W2CUT, (half + 1) * W2CUT)
                    pool.wait_ge(s_w2_hi, e * 2 + half + 1)
                    pool.tensor_tensor(w2_lo[:, cut], raw2[:, cut], f32(w2_hi[:, cut]), ALU.subtract).then_inc(s_w2_lo, 1)
                gather(e * CE + 2, 0)

        @block.scalar
        def _(act):
            def transposed(n, c):
                for s in range(CT):
                    act.wait_ge(s_pt, n * CT + s + 1)
                    act.activation(xt_hi[:, :, s * P:(s + 1) * P],
                                   pt[:, (c * CT + s) % 2, :].rearrange("p (d t) -> p d t", d=DT),
                                   ACT.Copy).then_inc(s_xt_hi, 1)

            transposed(0, 0)
            with act.Fori(0, E_N) as e:
                act.wait_ge(s_raw1, (e + 1) * 16)
                act.activation(w1_hi[:], raw1[:], ACT.Copy).then_inc(s_w1_hi, 1)
                act.wait_ge(s_b1, e + 1)
                for c in range(CE):
                    for f in range(FT):
                        i = e * (CE * FT) + c * FT + f
                        act.wait_ge(s_ph, i + 1)
                        act.wait_ge(s_g_lo, i + 1)
                        act.activation(g[:, f % 2].rearrange("p (h t) -> p h t", h=2), ph[:, f % 2, :, :HALF], ACT.Gelu,
                                       bias=b1_col[:, f:f + 1]).then_inc(s_g, 1)
                        act.wait_ge(s_g, i + 3)
                        act.activation(g_hi[:, f, :], g[:, f % 2, :], ACT.Copy).then_inc(s_g_hi, 1)
                        if c == 0 and f in (1, 3):
                            cut = slice(f // 2 * W2CUT, (f // 2 + 1) * W2CUT)
                            act.wait_ge(s_raw2, (e + 1) * 16)
                            act.activation(w2_hi[:, cut], raw2[:, cut], ACT.Copy).then_inc(s_w2_hi, 1)
                    transposed(e * CE + c + 1, 1 - c)

        @block.vector
        def _(dve):
            def put_index(n, c):
                dve.tensor_copy(index[:, c, :], token_of[:, bass.ds(n * CT, CT)]).then_inc(s_index, 1)

            def transposed(n, c):
                for s in range(CT):
                    cut = (slice(None), slice(None), slice(s * P, (s + 1) * P))
                    dve.wait_ge(s_xt_hi, n * CT + s + 1)
                    dve.tensor_tensor(xt_lo[cut], pt[:, (c * CT + s) % 2, :].rearrange("p (d t) -> p d t", d=DT),
                                      f32(xt_hi[cut]), ALU.subtract).then_inc(s_xt, 1)

            for s, n in ((s_xt, 2), (s_g, 2), (s_g_lo, 2), (s_out, 2), (s_store, 16)):
                dve.sem_inc(s, n)
            put_index(0, 0)
            dve.wait_ge(s_const, 32)
            transposed(0, 0)
            with dve.Fori(0, E_N) as e:
                dve.tensor_copy(b1_col[:], b1_all[:, bass.ds(e, 1), :].rearrange("p o f -> p (o f)")).then_inc(s_b1, 1)
                for c in range(CE):
                    n = e * CE + c
                    put_index(n + 1, 1 - c)
                    for f in range(FT):
                        dve.wait_ge(s_g_hi, e * (CE * FT) + c * FT + f + 1)
                        dve.tensor_tensor(g_lo[:, f, :], g[:, f % 2, :], f32(g_hi[:, f, :]), ALU.subtract).then_inc(s_g_lo, 1)
                    transposed(n + 1, 1 - c)
                    dve.wait_ge(s_store, (n + 1) * 16)
                    if c == 0:
                        dve.wait_ge(s_b2, (e + 1) * 16)
                    for s in range(CT):
                        dve.wait_ge(s_po, n * CT + s + 1)
                        dve.tensor_tensor(out[:, s, :], po[:, (c * CT + s) % 2, :], b2_row[:], ALU.add).then_inc(s_out, 1)

        @block.tensor
        def _(pe):
            def transpose(n, c, e):
                pe.wait_ge(s_x[c], (e + 1) * (CT * 16))
                for s in range(CT):
                    pe.wait_ge(s_xt, n * CT + s + 1)
                    for d in range(DT):
                        mm = pe.transpose(pt[:, (c * CT + s) % 2, d * P:(d + 1) * P], x[:, c, s, d * P:(d + 1) * P], ident[:])
                    mm.then_inc(s_pt, 1)

            pe.wait_ge(s_const, 32)
            transpose(0, 0, 0)
            with pe.Fori(0, E_N) as e:
                pe.wait_ge(s_w1_lo, e + 1)
                for c in range(CE):
                    n = e * CE + c
                    pe.wait_ge(s_xt, (n + 1) * CT + 2)
                    for f in range(FT):
                        pe.wait_ge(s_g, n * FT + f + 1)
                        cut = slice(f * P, (f + 1) * P)
                        for half in range(2):
                            part = slice(half * HALF, (half + 1) * HALF)
                            for d in range(DT):
                                ops = ((w1_hi, xt_hi), (w1_hi, xt_lo), (w1_lo, xt_hi))
                                for p, (w, r) in enumerate(ops):
                                    mm = pe.matmul(ph[:, f % 2, half, :HALF], w[:, d, cut], r[:, d, part],
                                                   start=(d == 0 and p == 0), stop=(d == DT - 1 and p == 2))
                        mm.then_inc(s_ph, 1)
                    transpose(n + 1, 1 - c, e if c == 0 else e + 1)
                    if c == 0:
                        pe.wait_ge(s_w2_lo, 2 * e + 2)
                    for s in range(CT):
                        pe.wait_ge(s_out, n * CT + s + 1)
                        cut = slice(s * P, (s + 1) * P)
                        for f in range(FT):
                            if s == 0:
                                pe.wait_ge(s_g_lo, n * FT + f + 3)
                            ops = ((g_hi, w2_hi), (g_hi, w2_lo), (g_lo, w2_hi))
                            for p, (l, w) in enumerate(ops):
                                mm = pe.matmul(po[:, (c * CT + s) % 2, :], l[:, f, cut], w[:, f, :],
                                               start=(f == 0 and p == 0), stop=(f == FT - 1 and p == 2))
                        mm.then_inc(s_po, 1)


def combine(nc, expert_out, x_in, x_out, slot_of, weight):
    with ExitStack() as ctx:
        def sb(name, shape, dt=F32):
            return ctx.enter_context(nc.sbuf_tensor("c_" + name, shape, dt))

        sem = stage_semaphores(nc, ctx, "c_")

        index = sb("index", [P, 2, ST * TOP], I32)
        part = sb("part", [P, 2, ST, TOP, D])
        x = sb("x", [P, 2, ST, D])
        w = sb("w", [P, 2, ST * TOP])
        s_index = [sem("s_index0"), sem("s_index1")]
        s_part = [sem("s_part0"), sem("s_part1")]
        s_x = [sem("s_x0"), sem("s_x1")]
        s_w = sem("s_w")
        s_first = sem("s_first")
        s_sum = sem("s_sum")
        s_store = [sem("s_store0"), sem("s_store1")]
        s_passed = sem("s_passed")
        s_passed_pool = sem("s_passed_pool")
        block = ctx.enter_context(nc.Block())

        def store(sp, b, v):
            passed(sp, s_sum, b + 3, s_passed)
            sp.dma_start(x_out[b].rearrange("(t p) d -> p t d", p=P), x[:, v]).then_inc(s_store[v], 16)

        @block.sync
        def _(sp):
            with sp.Fori(0, B // 2) as bb:
                for v in range(2):
                    passed(sp, s_store[v], (bb + 1) * 16, s_passed)
                    sp.dma_start(x[:, v], x_in[bb * 2 + v].rearrange("(t p) d -> p t d", p=P)).then_inc(s_x[v], 16)
                for v in range(2):
                    store(sp, bb * 2 + v, v)
            for v in range(2):
                sp.wait_ge(s_store[v], (B // 2 + 1) * 16)

        @block.gpsimd
        def _(pool):
            with pool.Fori(0, B // 2) as bb:
                for v in range(2):
                    passed(pool, s_index[v], bb + 1, s_passed_pool)
                    for t in range(ST):
                        for k in range(TOP):
                            pool.indirect_dma_start(part[:, v, t, k, :], None, expert_out,
                                                    bass.IndirectOffsetOnAxis(index[:, v, t * TOP + k:t * TOP + k + 1], 0)
                                                    ).then_inc(s_part[v], 16)

        @block.vector
        def _(dve):
            def put_index(b, v):
                cut = bass.ds(b * ST, ST)
                dve.tensor_copy(index[:, v, :].rearrange("p (t k) -> p t k", k=TOP), slot_of[:, cut, :]).then_inc(s_index[v], 1)

            def body(bb, last):
                for v in range(2):
                    b = bb * 2 + v
                    dve.tensor_copy(w[:, v, :].rearrange("p (t k) -> p t k", k=TOP),
                                    weight[:, bass.ds(b * ST, ST), :]).then_inc(s_w, 1)
                    dve.wait_ge(s_w, b + 1)
                    dve.wait_ge(s_part[v], (bb + 1) * (ST * TOP * 16))
                    dve.wait_ge(s_x[v], (bb + 1) * 16)
                    for t in range(ST):
                        dve.scalar_tensor_tensor(x[:, v, t, :], part[:, v, t, 0, :], w[:, v, t * TOP:t * TOP + 1], x[:, v, t, :],
                                                 ALU.mult, ALU.add).then_inc(s_first, 1)
                    for t in range(ST):
                        dve.wait_ge(s_first, b * ST + t + 1)
                        ins = dve.scalar_tensor_tensor(x[:, v, t, :], part[:, v, t, 1, :], w[:, v, t * TOP + 1:t * TOP + 2],
                                                       x[:, v, t, :], ALU.mult, ALU.add)
                    ins.then_inc(s_sum, 1)
                    if not last:
                        dve.wait_ge(s_sum, b + 3)
                        put_index(b + 2, v)

            dve.sem_inc(s_sum, 2)
            dve.sem_inc(s_store[0], 16)
            dve.sem_inc(s_store[1], 16)
            put_index(0, 0)
            put_index(1, 1)
            with dve.Fori(0, B // 2 - 1) as bb:
                body(bb, False)
            body(B // 2 - 1, True)



def program(nc, x, ctx_t, out, bufs, attn, mlp, moe, g_xattn, g_ffn, consts):
    def column(g, layer):
        return g[:, layer:layer + 1].to_broadcast([P, 1])

    def row(v):
        return v.to_broadcast([P, D])

    def attend(layer, x_in, x_out, hmax):
        a = attn[layer]
        attention(nc, layer, x_in, x_out, bufs["h"], hmax, ctx_t, [a["Wq"], a["Wk"], a["Wv"], a["Wo"]],
                  {"bq": a["bq"], "bk": a["bk"]}, {"bv": row(a["bv"]), "bo": row(a["bo"])},
                  column(g_xattn, layer), consts)

    attend(0, x, bufs["x1"], bufs["hmax"])
    gated_mlp(nc, bufs["h"], bufs["hmax"], bufs["x1"], bufs["x2"], (mlp["w_gate"], mlp["w_up"], mlp["w_down"]),
              column(g_ffn, 0), consts["ident"], bufs)
    attend(1, bufs["x2"], bufs["x1"], None)
    mixture(nc, bufs["h"], bufs["x1"], out, moe["router_w"], moe["router_b"].to_broadcast([P, E_N]),
            moe["w1"], moe["w2"], moe["b1"], moe["b2"], column(g_ffn, 1), consts, bufs)




def heads_inside(a):
    return a.reshape(*a.shape[:-1], G, HG, HD).swapaxes(-1, -2).reshape(a.shape)


def lay_w(w, interleave):
    wt = w.T
    if interleave:
        wt = heads_inside(wt)
    return np.ascontiguousarray(wt.reshape(DT, P, D).transpose(1, 0, 2))


def lay_bias(v):
    return np.ascontiguousarray(heads_inside(v).reshape(G, P).T)


def constants():
    token = np.arange(NT)[None, :, None] * P + np.arange(P)[:, None, None]
    p, c = np.arange(P)[:, None], np.arange(P)[None, :]
    half = HD // 2
    inv_freq = np.float32(1.0) / np.float32(10000.0) ** (np.arange(half, dtype=np.float32) / np.float32(half))
    angle = inv_freq.astype(np.float32)[:, None] * np.arange(S, dtype=np.float32)[None, :]
    cos, sin = np.cos(angle), np.sin(angle)
    return {
        "ident": np.eye(P, dtype=np.float32),
        "masks": np.stack([np.where(c <= p, 0.0, NEG), np.where(c >= p, 0.0, NEG)], 1).astype(np.float32),
        "cos": np.repeat(np.concatenate([cos, cos]), HG, 0),
        "sin": np.repeat(np.concatenate([sin, -sin]), HG, 0),
        "before": np.triu(np.ones((P, P), np.float32), 1),
        "expert": np.ascontiguousarray(np.broadcast_to(np.arange(E_N, dtype=np.float32), (P, NT, E_N))),
        "spare": (SLOTS + np.arange(TOP)[None, None, :] * T + token).astype(np.float32),
        "token_id": token[:, :, 0].astype(np.int32),
    }


def kernel(**inputs):
    import concourse.bacc as bacc
    from concourse.bass_utils import run_bass_kernel_spmd

    a = {k: np.asarray(v) for k, v in inputs.items()}
    ctx = a["ctx_1024"]
    ctx_t = np.concatenate([ctx, ctx[:1]]).transpose(0, 2, 1).reshape(B + 1, DT, P, S).transpose(0, 2, 1, 3)
    arrays = {"x": a["x"], "ctx_t": ctx_t, "g_xattn": a["g_xattn"][None], "g_ffn": a["g_ffn"][None]}
    for layer in range(2):
        at = f"L{layer}_xattn_"
        for n in ("Wq", "Wk", "Wv", "Wo"):
            arrays[at + n] = lay_w(a[at + n], n in ("Wq", "Wk"))
        for n in ("bq", "bk"):
            arrays[at + n] = lay_bias(a[at + n])
        for n in ("bv", "bo"):
            arrays[at + n] = a[at + n][None]
    for n in ("w_gate", "w_up", "w_down"):
        arrays[n] = a["L0_ffn_" + n]
    arrays["router_w"] = a["L1_ffn_router_w"].reshape(DT, P, E_N).transpose(1, 0, 2)
    arrays["router_b"] = a["L1_ffn_router_b"][None]
    arrays["w1"] = a["L1_ffn_w1"].reshape(E_N, DT, P, F).transpose(0, 2, 1, 3)
    arrays["w2"] = a["L1_ffn_w2"].reshape(E_N, FT, P, D).transpose(0, 2, 1, 3)
    arrays["b1"] = a["L1_ffn_b1"].reshape(E_N, FT, P).transpose(2, 0, 1)
    arrays["b2"] = a["L1_ffn_b2"]
    consts = constants()
    arrays.update(consts)
    arrays = {"in_" + k: np.ascontiguousarray(v) for k, v in arrays.items()}

    nc = bacc.Bacc("TRN2", target_bir_lowering=False, num_devices=1)
    t = {k[3:]: nc.dram_tensor(k, v.shape, mybir.dt.from_np(v.dtype), kind="ExternalInput").ap()
         for k, v in arrays.items()}
    out = nc.dram_tensor("out", (B, S, D), F32, kind="ExternalOutput").ap()

    def scratch(name, shape, dt=F32):
        return nc.dram_tensor(name, shape, dt, kind="Internal").ap()

    bufs = {
        "x1": scratch("x1", (B, S, D)), "x2": scratch("x2", (B, S, D)), "h": scratch("h", (B, S, D)),
        "hmax": scratch("hmax", (P, 1)),
        "raw": [scratch(n, (NQ, P, 4, S)) for n in ("gate_raw", "up_raw")],
        "down": scratch("down_split", (2, P, IT, D)),
        "tokens": scratch("tokens", (SLOTS + T * TOP, 1), I32), "expert_out": scratch("expert_out", (SLOTS, D)),
    }
    attn = [{n: t[f"L{layer}_xattn_{n}"] for n in ("Wq", "bq", "Wk", "bk", "Wv", "bv", "Wo", "bo")} for layer in range(2)]
    program(nc, t["x"], t["ctx_t"], out, bufs, attn, t, t, t["g_xattn"], t["g_ffn"], {k: t[k] for k in consts})
    r = run_bass_kernel_spmd(nc, [arrays], core_ids=[0])
    return r.results[0]["out"]
```

```python
from contextlib import ExitStack

import numpy as np
import concourse.bass as bass
from concourse import mybir

F32 = mybir.dt.float32
F32R = mybir.dt.float32r
BF16 = mybir.dt.bfloat16
I16 = mybir.dt.int16
U16 = mybir.dt.uint16
I32 = mybir.dt.int32
U32 = mybir.dt.uint32
ALU = mybir.AluOpType
ACT = mybir.ActivationFunctionType
AX = mybir.AxisListType

P = 128
B, S, D = 8, 512, 512
T = B * S
NT = T // P
DT = D // P
ST = S // P
H, HD = 16, 32
HG = P // HD
G = H // HG
EPS = 1e-5
WINDOW = 256
NEG = -1.0e30


def passed(eng, sem, value, seen):
    eng.wait_ge(sem, value)
    eng.sem_inc(seen, 1)


def stage_semaphores(nc, ctx, tag):
    made = []
    ctx.callback(nc.all_engine_barrier)
    ctx.callback(nc.clear_and_free_semaphores, made)

    def sem(name):
        made.append(nc.alloc_semaphore(tag + name))
        return made[-1]

    return sem


def f32(ap):
    return ap.bitcast(F32)




def attention(nc, layer, x_in, x_out, h_out, hmax_out, ctx_t, w_in, cols, rows, gate, consts):
    rope = masked = layer == 1
    tag = f"a{layer}_"
    SCALE = float(HD) ** -0.5
    span = WINDOW // P
    keys_of = [(max(0, q - span), q + 1) if masked else (0, ST) for q in range(ST)]
    queries_of = [(k, min(ST, k + span + 1)) if masked else (0, ST) for k in range(ST)]

    with ExitStack() as ctx:
        def sb(name, shape, dt=F32):
            return ctx.enter_context(nc.sbuf_tensor(tag + name, shape, dt))

        def ps(name, shape, dt=F32):
            return ctx.enter_context(nc.psum_tensor(tag + name, shape, dt))

        sem = stage_semaphores(nc, ctx, tag)

        w_hi = sb("w_hi", [P, 3, DT, D], F32R)
        w_lo = sb("w_lo", [P, 3, DT, D], F32R)
        wo = sb("wo", [P, DT, D])
        ctx_raw = sb("ctx_raw", [P, DT, S])
        ctx_hi = sb("ctx_hi", [P, DT, S], F32R)
        ctx_lo = sb("ctx_lo", [P, DT, S], F32R)
        x_tile = sb("x_tile", [P, ST, D])
        h_new = x_tile
        ht_hi = sb("ht_hi", [P, DT, S], F32R)
        ht_lo = sb("ht_lo", [P, DT, S], F32R)
        qk_hi = sb("qk_hi", [P, 2, S], F32R)
        qk_lo = sb("qk_lo", [P, 2, S], F32R)
        NR = 3 * HD + 1
        q_stack = sb("q_stack", [P, 2, HG, S], F32R)
        k_stack = sb("k_stack", [P, 2, HG, S], F32R)
        v_sb = sb("v_sb", [P, ST, D])
        probs = sb("probs", [P, 2, HG, S])
        negmax = sb("negmax", [P, HG * ST])
        negmax_t = sb("negmax_t", [HG * ST, P], F32R)
        sums = sb("sums", [P, S])
        recip = sb("recip", [P, S])
        att = sb("att", [P, G, S])
        ones = sb("ones", [P, HD])
        ident = sb("ident", [P, P])
        b_col = {"q": sb("bq_col", [P, DT]), "k": sb("bk_col", [P, DT])}
        bv_row = sb("bv_row", [P, D])
        bo_row = sb("bo_row", [P, D])
        gate_col = sb("gate_col", [P, 1])
        tanh_g = sb("tanh_g", [P, 1])
        bn = sb("bn", [P, ST, 6])
        mv = sb("mv", [P, ST, 2])
        ve = sb("ve", [P, ST])
        rstd = sb("rstd", [P, ST])
        halfneg = sb("halfneg", [P, 1])
        x_new = sb("x_new", [P, ST, D])
        bn_o = sb("bn_o", [P, ST, 6])
        mv_o = sb("mv_o", [P, ST, 2])
        ve_o = sb("ve_o", [P, ST])
        rstd_o = sb("rstd_o", [P, ST])
        nmr_o = sb("nmr_o", [P, ST])
        hmax = sb("hmax", [P, NT])
        hmax_all = sb("hmax_all", [P, 1])
        if masked:
            ident_b = sb("ident_b", [P, P], BF16)
            masks = sb("masks", [P, 2, P], BF16)
            masks_in = sb("masks_in", [P, 2, P])
            cos_t = sb("cos_t", [P, S])
            sin_t = sb("sin_t", [P, S])
            lin = sb("lin", [P, S])
            lin_cos = sb("lin_cos", [P, S])
            swap_sin = sb("swap_sin", [P, S])

        pj = ps("pj", [P, 2, 512])
        pa = ps("pa", [P, 2, 512])
        pst = ps("pst", [P, 2, 512])
        po = ps("po", [P, 512])
        psm = ps("psm", [P, 512])

        s_w = [sem("s_w0"), sem("s_w1"), sem("s_w2")]
        s_const = sem("s_const")
        s_w_hi = sem("s_w_hi")
        s_w_lo = sem("s_w_lo")
        s_setup = sem("s_setup")
        s_tanh = sem("s_tanh")
        s_x_in = sem("s_x_in")
        s_ctx_in = sem("s_ctx_in")
        s_ctx_hi = sem("s_ctx_hi")
        s_ctx_lo = sem("s_ctx_lo")
        s_bn = sem("s_bn")
        s_mv = sem("s_mv")
        s_ve = sem("s_ve")
        s_rstd = sem("s_rstd")
        s_hn = sem("s_hn")
        s_pj = sem("s_pj")
        s_pj_out = sem("s_pj_out")
        s_o = sem("s_o")
        s_o_out = sem("s_o_out")
        s_ht_hi = sem("s_ht_hi")
        s_qk_hi = sem("s_qk_hi")
        s_qk_lo = sem("s_qk_lo")
        s_stack = {"q": [sem("s_qst0"), sem("s_qst1")], "k": [sem("s_kst0"), sem("s_kst1")]}
        s_pa = sem("s_pa")
        s_max = sem("s_max")
        s_nm_p = sem("s_nm_p")
        s_nm_t = sem("s_nm_t")
        s_mrow = [sem("s_mrow0"), sem("s_mrow1")]
        s_st = sem("s_st")
        s_exp = sem("s_exp")
        s_pv = sem("s_pv")
        s_sums = sem("s_sums")
        s_po_out = sem("s_po_out")
        s_recip = sem("s_recip")
        s_norm = sem("s_norm")
        s_xres = sem("s_xres")
        s_xb = sem("s_xb")
        s_bn_o = sem("s_bn_o")
        s_mv_o = sem("s_mv_o")
        s_ve_o = sem("s_ve_o")
        s_rstd_o = sem("s_rstd_o")
        s_nmr_o = sem("s_nmr_o")
        s_h_new = sem("s_h_new")
        s_hmax = sem("s_hmax")
        s_store_x = sem("s_store_x")
        s_store_h = sem("s_store_h")
        s_swap = sem("s_swap")
        s_rope = sem("s_rope")
        s_cos = sem("s_cos")
        s_last = sem("s_last")
        s_passed = sem("s_passed")
        s_passed_sp = sem("s_passed_sp")
        block = ctx.enter_context(nc.Block())

        T0, QK_A, V0, QK_B, PJ = 0, ST, 2 * ST, 3 * ST, 4 * ST
        NQK = 2 * G
        NG = HG * ST
        NSC = G * NG
        STACK = 16 * 3
        MROW = 16
        NCONST = 16 * (7 + 3 * masked)
        M_STEPS = [range(0, 0), range(0, 4), range(4, 9 + rope), range(9 + rope, NG)]
        M_SLOTS = [[0, 0, 0, 0, 0], [0, 0, 0, 2, 4], [0, 1, 3, 4, 6] if rope else [0, 1, 2, 3, 5],
                   [0, 2, 4, 6, 6] if rope else [0, 2, 4, 6, 7]]
        S_STEP = [(0, 2), (0, 2), (0, 3), (0, 3)] if rope else [(0, 3), (0, 3), (1, 0), (1, 0)]
        N_STEP = [(1, 0), (1, 1), (1, 2), (1, 3)]
        KEY_STEP = 3

        def kind_of(n):
            return "kq"[n % 2]

        def qk_tile(n):
            return (QK_A if n < ST else QK_B - ST) + n

        def stacked(b, g):
            return (b * (G // 2) + g // 2 + 1) * STACK

        raw_of = [probs[:, 0], probs[:, 1], ctx_raw[:]]

        def lo_written(b, n):
            return (s_qk_lo, b * NQK + n + 1) if rope else (s_pj_out, b * PJ + qk_tile(n) + 3)

        def next_group(b, g):
            return (b, g + 1) if g + 1 < G else (b + 1, 0)

        def projected_in(b, g):
            return (b, g + 2) if g + 2 < G else (b + 1, g + 2 - G)

        def normalise_heads(eng, b, g, t):
            cut = slice(t * P, (t + 1) * P)
            eng.wait_ge(s_recip, b * (G * ST) + g * ST + t + 2)
            eng.wait_ge(s_po_out, b * G + g + 2)
            eng.tensor_tensor(att[:, g, cut], att[:, g, cut], recip[:, cut], ALU.mult).then_inc(s_norm, 1)

        @block.sync
        def _(sp):
            for m in range(3):
                sp.dma_start(raw_of[m], w_in[m]).then_inc(s_w[m], 16)
            sp.dma_start(x_tile[:], x_in[0].rearrange("(t p) d -> p t d", p=P)).then_inc(s_x_in, 16)
            sp.dma_start(wo[:], w_in[3]).then_inc(s_const, 16)
            loads = [(ident[:], consts["ident"]), (b_col["q"][:], cols["bq"]), (b_col["k"][:], cols["bk"]),
                     (bv_row[:], rows["bv"]), (bo_row[:], rows["bo"]), (gate_col[:], gate)]
            if masked:
                loads += [(masks_in[:], consts["masks"]), (cos_t[:], consts["cos"]), (sin_t[:], consts["sin"])]
            for dst, src in loads:
                sp.dma_start(dst, src).then_inc(s_const, 16)
            sp.wait_ge(s_w_lo, 3)
            sp.dma_start(ctx_raw[:], ctx_t[0]).then_inc(s_ctx_in, 16)

            def to_stack(b, n, free):
                g = n // 2
                passed(sp, *lo_written(b, n), s_passed_sp)
                if free:
                    passed(sp, s_st, b * NSC + (g - 1) * NG, s_passed_sp)
                dst = {"q": q_stack, "k": k_stack}[kind_of(n)]
                srcs = {"q": (qk_hi, qk_hi, qk_lo), "k": (qk_hi, qk_lo, qk_hi)}[kind_of(n)]
                for row, src in enumerate(srcs):
                    sp.dma_start(f32(dst[HD * row:HD * row + HD, g % 2, :, :]),
                                 f32(src[:, n % 2, :])).then_inc(s_stack[kind_of(n)][g % 2], 16)

            def maximum_rows(b, g):
                passed(sp, s_nm_t, b * G + g + 1, s_passed_sp)
                row = f32(q_stack[3 * HD:NR, g % 2, :, :]).rearrange("r j (t q) -> r (j t) q", t=ST)
                sp.dma_start(row, f32(negmax_t[:])).then_inc(s_mrow[g % 2], 16)

            def load_ctx(b):
                passed(sp, s_ctx_lo, b, s_passed_sp)
                sp.dma_start(ctx_raw[:], ctx_t[b]).then_inc(s_ctx_in, 16)

            def whole(a, b):
                return a[b].rearrange("(t p) d -> p t d", p=P)

            def store(b):
                passed(sp, s_h_new, (b + 1) * ST, s_passed_sp)
                sp.dma_start(whole(x_out, b), x_new[:]).then_inc(s_store_x, 16)
                sp.dma_start(whole(h_out, b), h_new[:]).then_inc(s_store_h, 16)

            def load_residual(b):
                passed(sp, s_store_x, (b + 1) * 16, s_passed_sp)
                sp.dma_start(x_new[:], whole(x_in, b)).then_inc(s_xres, 16)

            load_ctx(1)
            for n in range(4):
                to_stack(0, n, False)
            maximum_rows(0, 0)

            def body(b, last):
                if not last:
                    if hmax_out is not None:
                        passed(sp, s_hmax, b * ST + 2, s_passed_sp)
                    passed(sp, s_pj, b * PJ + ST, s_passed_sp)
                    passed(sp, s_store_h, (b + 1) * 16, s_passed_sp)
                    sp.dma_start(x_tile[:], whole(x_in, b + 1)).then_inc(s_x_in, 16)
                for g in range(G):
                    bn_, gn = projected_in(b, g)
                    ahead = not (last and gn < 2)
                    if ahead:
                        to_stack(bn_, 2 * gn, True)
                    if not (last and g == G - 1):
                        maximum_rows(*next_group(b, g))
                    if ahead:
                        to_stack(bn_, 2 * gn + 1, True)
                    if g == 2 and not last:
                        load_ctx(b + 2)
                    if g == 1:
                        load_residual(b)
                store(b)

            with sp.Fori(0, B - 1) as b:
                body(b, False)
            body(B - 1, True)
            sp.wait_ge(s_store_x, (B + 1) * 16)
            sp.wait_ge(s_store_h, (B + 1) * 16)
            sp.wait_ge(s_ctx_in, (B + 1) * 16)
            if hmax_out is not None:
                sp.wait_ge(s_last, 1)
                sp.dma_start(hmax_out, hmax_all[:]).then_inc(s_last, 16)
                sp.wait_ge(s_last, 17)

        @block.scalar
        def _(act):
            def context(b):
                act.wait_ge(s_ctx_in, b * 16 + 16)
                act.activation(ctx_hi[:], ctx_raw[:], ACT.Copy).then_inc(s_ctx_hi, 1)

            def transposed(b, t):
                act.wait_ge(s_pj, b * PJ + T0 + t + 1)
                act.activation(ht_hi[:, :, t * P:(t + 1) * P],
                               pj[:, (T0 + t) % 2, :].rearrange("p (d t) -> p d t", d=DT),
                               ACT.Copy).then_inc(s_ht_hi, 1)

            def qk_to_hi(b, n, first=False):
                g, tile = n // 2, qk_tile(n)
                if not first:
                    before = stacked(b, g - 1) if g else stacked(b - 1, G - 1)
                    act.wait_ge(s_stack[kind_of(n)][(g - 1) % 2], before)
                if rope:
                    act.wait_ge(s_rope, b * NQK + n + 1)
                    act.activation(qk_hi[:, n % 2, :], lin_cos[:], ACT.Copy).then_inc(s_qk_hi, 1)
                else:
                    act.wait_ge(s_pj, b * PJ + tile + 1)
                    act.activation(qk_hi[:, n % 2, :], pj[:, tile % 2, :], ACT.Identity,
                                   bias=b_col[kind_of(n)][:, g:g + 1]).then_inc(s_qk_hi, 1)

            def exponentials(b, g, k):
                q0, q1 = queries_of[k]
                act.wait_ge(s_pv, b * G * ST + g * ST + k + 1)
                for j in range(HG):
                    n = (g * ST + k) * HG + j
                    act.wait_ge(s_st, b * NSC + n + 1)
                    act.activation(probs[:, k % 2, j, q0 * P:q1 * P], pst[:, n % 2, q0 * P:q1 * P],
                                   ACT.Exp, scale=SCALE).then_inc(s_exp, 1)

            def take_out(b, g):
                act.wait_ge(s_pv, b * G * ST + (g + 1) * ST + 2)
                act.wait_ge(s_recip, b * (G * ST) + g * ST + 1)
                act.activation(sums[:], psm[:], ACT.Copy).then_inc(s_sums, 1)
                act.activation(att[:, g, :], po[:], ACT.Copy).then_inc(s_po_out, 1)

            for m in range(3):
                act.wait_ge(s_w[m], 16)
                act.activation(w_hi[:, m], raw_of[m], ACT.Copy).then_inc(s_w_hi, 1)
            act.wait_ge(s_const, NCONST)
            act.activation(tanh_g[:], gate_col[:], ACT.Tanh).then_inc(s_tanh, 1)
            context(0)
            for t in range(ST):
                transposed(0, t)
            for n in range(4):
                qk_to_hi(0, n, first=n < 2)

            def body(b, last):
                for g in range(G):
                    bn_, gn = projected_in(b, g)
                    ahead = not (last and gn < 2)
                    for k in range(ST):
                        exponentials(b, g, k)
                        if g == 2 and k < 2 and not last:
                            transposed(b + 1, 2 * k)
                            transposed(b + 1, 2 * k + 1)
                        if k == KEY_STEP and ahead:
                            qk_to_hi(bn_, 2 * gn)
                    take_out(b, g)
                    if g == 1 and not last:
                        context(b + 1)
                    if ahead:
                        qk_to_hi(bn_, 2 * gn + 1)
                for t in range(ST):
                    act.wait_ge(s_nmr_o, b * ST + t + 1)
                    if t == 0:
                        act.wait_ge(s_store_h, (b + 1) * 16)
                    act.activation(h_new[:, t, :], x_new[:, t, :], ACT.Identity,
                                   bias=nmr_o[:, t:t + 1], scale=rstd_o[:, t:t + 1]).then_inc(s_h_new, 1)

            with act.Fori(0, B - 1) as b:
                body(b, False)
            body(B - 1, True)

        @block.gpsimd
        def _(pool):
            def context(b):
                pool.wait_ge(s_ctx_hi, b + 1)
                pool.tensor_tensor(ctx_lo[:], ctx_raw[:], f32(ctx_hi[:]), ALU.subtract).then_inc(s_ctx_lo, 1)

            def deviation(b, t):
                pool.wait_ge(s_ve, b * ST + t + 1)
                pool.tensor_tensor(rstd[:, t:t + 1], ve[:, t:t + 1], halfneg[:], ALU.pow).then_inc(s_rstd, 1)

            def turn(b, n):
                if rope:
                    pool.wait_ge(s_pj_out, b * PJ + qk_tile(n) + 3)
                    pool.tensor_tensor(lin_cos[:], lin[:], cos_t[:], ALU.mult).then_inc(s_cos, 1)

            def add_bias(b, t):
                pool.wait_ge(s_xres, (b + 1) * 16)
                pool.tensor_tensor(x_new[:, t, :], x_new[:, t, :], bo_row[:], ALU.add).then_inc(s_xb, 1)

            pool.wait_ge(s_setup, 3)
            context(0)
            for t in range(ST):
                deviation(0, t)
            for n in range(4):
                turn(0, n)
            pool.wait_ge(s_setup, 4 + 2 * masked)

            def body(b, last):
                for t in range(ST):
                    if not last:
                        deviation(b + 1, t)
                for g in range(G):
                    bn_, gn = projected_in(b, g)
                    if not (last and gn < 2):
                        turn(bn_, 2 * gn)
                        if g == 1 and not last:
                            context(b + 1)
                    for t in range(ST if g < G - 1 else 0):
                        normalise_heads(pool, b, g, t)
                    if not (last and gn < 2):
                        turn(bn_, 2 * gn + 1)
                    if g == 2:
                        for t in range(ST):
                            add_bias(b, t)
                for t in range(ST):
                    pool.wait_ge(s_ve_o, b * ST + t + 1)
                    pool.tensor_tensor(rstd_o[:, t:t + 1], ve_o[:, t:t + 1], halfneg[:],
                                       ALU.pow).then_inc(s_rstd_o, 1)

            with pool.Fori(0, B - 1) as b:
                body(b, False)
            body(B - 1, True)

        @block.vector
        def _(dve):
            dve.memset(ones[:], 1.0).then_inc(s_setup, 1)
            dve.memset(halfneg[:], -0.5).then_inc(s_setup, 1)
            dve.memset(f32(k_stack[3 * HD:NR]), 1.0).then_inc(s_setup, 1)
            for m in range(3):
                dve.wait_ge(s_w_hi, m + 1)
                dve.tensor_tensor(w_lo[:, m], raw_of[m], f32(w_hi[:, m]), ALU.subtract).then_inc(s_w_lo, 1)
            for s, n in ((s_pj_out, 2), (s_o_out, ST), (s_max, 2), (s_exp, 2), (s_pv, 2), (s_sums, 1), (s_po_out, 1),
                         (s_recip, 1), (s_norm, 1), (s_hmax, 2),
                         (s_store_x, 16), (s_store_h, 16)):
                dve.sem_inc(s, n)

            def stats(b, t):
                if t == 0:
                    dve.wait_ge(s_x_in, (b + 1) * 16)
                dve.bn_stats(bn[:, t, :], x_tile[:, t, :]).then_inc(s_bn, 1)
                passed(dve, s_bn, b * ST + t + 1, s_passed)
                dve.bn_aggr(mv[:, t, :], bn[:, t, :]).then_inc(s_mv, 1)
                dve.wait_ge(s_mv, b * ST + t + 1)
                dve.tensor_scalar(ve[:, t:t + 1], mv[:, t, 1:2], EPS, None, ALU.add).then_inc(s_ve, 1)

            def normalise(b, t):
                dve.wait_ge(s_rstd, b * ST + t + 1)
                dve.tensor_scalar(x_tile[:, t, :], x_tile[:, t, :], mv[:, t, 0:1], rstd[:, t:t + 1],
                                  ALU.subtract, ALU.mult).then_inc(s_hn, 1)

            def values(b, t):
                dve.wait_ge(s_pj, b * PJ + V0 + t + 1)
                dve.tensor_tensor(v_sb[:, t, :], pj[:, (V0 + t) % 2, :], bv_row[:], ALU.add).then_inc(s_pj_out, 1)

            def qk_to_lo(b, n):
                g, tile = n // 2, qk_tile(n)
                bias = b_col[kind_of(n)][:, g:g + 1]
                if rope:
                    top, low = slice(0, P // 2), slice(P // 2, P)
                    dve.wait_ge(s_pj, b * PJ + tile + 1)
                    dve.tensor_scalar(lin[:], pj[:, tile % 2, :], bias, None, ALU.add).then_inc(s_pj_out, 1)
                    dve.wait_ge(s_pj_out, b * PJ + tile + 3)
                    for dst, src in ((top, low), (low, top)):
                        dve.tensor_tensor(swap_sin[dst, :], lin[src, :], sin_t[src, :], ALU.mult).then_inc(s_swap, 1)
                    dve.wait_ge(s_swap, (b * NQK + n + 1) * 2)
                    dve.wait_ge(s_cos, b * NQK + n + 1)
                    dve.tensor_tensor(lin_cos[:], lin_cos[:], swap_sin[:], ALU.add).then_inc(s_rope, 1)
                    dve.wait_ge(s_qk_hi, b * NQK + n + 1)
                    dve.tensor_tensor(qk_lo[:, n % 2, :], lin_cos[:], f32(qk_hi[:, n % 2, :]),
                                      ALU.subtract).then_inc(s_qk_lo, 1)
                else:
                    dve.wait_ge(s_qk_hi, b * NQK + n + 1)
                    dve.scalar_tensor_tensor(qk_lo[:, n % 2, :], pj[:, tile % 2, :], bias,
                                             f32(qk_hi[:, n % 2, :]), ALU.add, ALU.subtract).then_inc(s_pj_out, 1)

            def ht_to_lo(b, t):
                dve.wait_ge(s_ht_hi, b * ST + t + 1)
                cut = (slice(None), slice(None), slice(t * P, (t + 1) * P))
                dve.tensor_tensor(ht_lo[cut], pj[:, (T0 + t) % 2, :].rearrange("p (d t) -> p d t", d=DT),
                                  f32(ht_hi[cut]), ALU.subtract).then_inc(s_pj_out, 1)

            def maxima(b, g, tiles):
                for i in tiles:
                    q, j = i // HG, i % HG
                    k0, k1 = keys_of[q]
                    dve.wait_ge(s_pa, b * NSC + g * NG + i + 1)
                    dve.tensor_reduce(negmax[:, j * ST + q:j * ST + q + 1], pa[:, i % 2, k0 * P:k1 * P],
                                      AX.X, ALU.max, negate=True).then_inc(s_max, 1)

            def maxima_to_rows(b, g, first=False):
                if not first:
                    before = b * 2 + (g - 1) // 2 + 1 if g else b * 2
                    dve.wait_ge(s_mrow[(g - 1) % 2], before * MROW)
                dve.wait_ge(s_nm_p, b * G + g + 1)
                dve.tensor_copy(negmax_t[:], pa[0:NG, 0, 0:P]).then_inc(s_nm_t, 1)

            def invert_sums(b, g, t):
                cut = slice(t * P, (t + 1) * P)
                dve.wait_ge(s_norm, b * (G * ST) + g * ST + 1)
                dve.wait_ge(s_sums, b * G + g + 2)
                dve.reciprocal(recip[:, cut], sums[:, cut]).then_inc(s_recip, 1)

            def out_stats(b, t):
                n = b * ST + t + 1
                dve.wait_ge(s_o, n)
                dve.wait_ge(s_xb, n)
                dve.scalar_tensor_tensor(x_new[:, t, :], pj[:, t % 2, :], tanh_g[:], x_new[:, t, :],
                                         ALU.mult, ALU.add).then_inc(s_o_out, 1)
                dve.wait_ge(s_o_out, n + ST)
                dve.bn_stats(bn_o[:, t, :], x_new[:, t, :]).then_inc(s_bn_o, 1)
                passed(dve, s_bn_o, n, s_passed)
                dve.bn_aggr(mv_o[:, t, :], bn_o[:, t, :]).then_inc(s_mv_o, 1)
                dve.wait_ge(s_mv_o, n)
                dve.tensor_scalar(ve_o[:, t:t + 1], mv_o[:, t, 1:2], EPS, None, ALU.add).then_inc(s_ve_o, 1)

            def out_scale(b, t):
                dve.wait_ge(s_rstd_o, b * ST + t + 1)
                dve.scalar_tensor_tensor(nmr_o[:, t:t + 1], mv_o[:, t, 0:1], -1.0, rstd_o[:, t:t + 1],
                                         ALU.mult, ALU.mult).then_inc(s_nmr_o, 1)

            def out_max(b, t):
                if hmax_out is not None:
                    dve.wait_ge(s_h_new, b * ST + t + 1)
                    dve.tensor_reduce(hmax[:, bass.ds(b * ST + t, 1)], h_new[:, t, :], AX.X, ALU.max,
                                      apply_absolute_value=True).then_inc(s_hmax, 1)

            dve.wait_ge(s_tanh, 1)
            if masked:
                dve.tensor_copy(ident_b[:], ident[:]).then_inc(s_setup, 1)
                dve.tensor_copy(masks[:], masks_in[:]).then_inc(s_setup, 1)
            dve.tensor_scalar(bo_row[:], bo_row[:], tanh_g[:], None, ALU.mult).then_inc(s_setup, 1)
            for t in range(ST):
                stats(0, t)
            for t in range(ST):
                normalise(0, t)
            for t in range(ST):
                ht_to_lo(0, t)
            for n in range(4):
                qk_to_lo(0, n)
            maxima(0, 0, range(NG))
            maxima_to_rows(0, 0, first=True)

            def body(b, last):
                for t in range(ST):
                    values(b, t)
                for g in range(G):
                    bn_, gn = projected_in(b, g)
                    ahead = not (last and gn < 2)
                    for k in range(ST):
                        for t in range(ST if not last else 0):
                            if S_STEP[t] == (g, k):
                                stats(b + 1, t)
                            if N_STEP[t] == (g, k):
                                normalise(b + 1, t)
                        tiles = [] if last and g == G - 1 else list(M_STEPS[k])
                        maxima(*next_group(b, g), tiles)
                        if k == KEY_STEP and ahead:
                            qk_to_lo(bn_, 2 * gn)
                        if g == 2 and k < 2 and not last:
                            ht_to_lo(b + 1, 2 * k)
                            ht_to_lo(b + 1, 2 * k + 1)
                    if g < G - 1:
                        maxima_to_rows(b, g + 1)
                    for t in range(ST):
                        invert_sums(b, g, t)
                        if g == G - 1:
                            normalise_heads(dve, b, g, t)
                    if g == G - 1 and not last:
                        maxima_to_rows(b + 1, 0)
                    if ahead:
                        qk_to_lo(bn_, 2 * gn + 1)
                for t in range(ST):
                    out_stats(b, t)
                    out_scale(b, t)
                    if t >= 1:
                        out_max(b, t - 1)
                out_max(b, ST - 1)

            with dve.Fori(0, B - 1) as b:
                body(b, False)
            body(B - 1, True)
            if hmax_out is not None:
                dve.wait_ge(s_hmax, NT + 2)
                dve.tensor_reduce(hmax_all[:], hmax[:], AX.X, ALU.max).then_inc(s_last, 1)

        @block.tensor
        def _(pe):
            def open_tile(b, n):
                pe.wait_ge(s_pj_out, b * PJ + n + 1)
                return pj[:, n % 2, :]

            def three_passes(out, lhs, rhs):
                for d in range(DT):
                    (lh, ll), (rh, rl) = lhs(d), rhs(d)
                    for n, (l, r) in enumerate(((lh, rh), (lh, rl), (ll, rh))):
                        mm = pe.matmul(out, l, r, start=(d == 0 and n == 0), stop=(d == DT - 1 and n == 2))
                return mm

            def project_qk(b, n):
                kind, g = kind_of(n), n // 2
                m = {"q": 0, "k": 1}[kind]
                hi, lo = {"q": (ht_hi, ht_lo), "k": (ctx_hi, ctx_lo)}[kind]
                cut = slice(g * P, (g + 1) * P)
                three_passes(open_tile(b, qk_tile(n)), lambda d: (w_hi[:, m, d, cut], w_lo[:, m, d, cut]),
                             lambda d: (hi[:, d, :], lo[:, d, :])).then_inc(s_pj, 1)

            def project_v(b, t):
                cut = slice(t * P, (t + 1) * P)
                out = open_tile(b, V0 + t)
                if t < 2:
                    pe.wait_ge(s_o_out, b * ST + t + 3)
                three_passes(out, lambda d: (ctx_hi[:, d, cut], ctx_lo[:, d, cut]),
                             lambda d: (w_hi[:, 2, d, :], w_lo[:, 2, d, :])).then_inc(s_pj, 1)

            def transpose(b, t):
                out = open_tile(b, T0 + t)
                pe.wait_ge(s_hn, b * ST + t + 1)
                for d in range(DT):
                    mm = pe.transpose(out[:, d * P:(d + 1) * P], x_tile[:, t, d * P:(d + 1) * P], ident[:])
                mm.then_inc(s_pj, 1)

            def transpose_maxima(b, g):
                pe.wait_ge(s_max, b * NSC + (g + 1) * NG + 2)
                pe.transpose(pa[0:NG, 0, 0:P], negmax[:], ident[:]).then_inc(s_nm_p, 1)

            def score_max(b, g, i, first=False):
                q, j = i // HG, i % HG
                k0, k1 = keys_of[q]
                if i == 0:
                    for kind in "qk":
                        pe.wait_ge(s_stack[kind][g % 2], stacked(b, g))
                    if not first:
                        pe.wait_ge(s_nm_t, b * G + g)
                pe.wait_ge(s_max, b * NSC + g * NG + i + 1)
                out = pa[:, i % 2, :]
                mm = pe.matmul(out[:, k0 * P:k1 * P], q_stack[0:3 * HD, g % 2, j, q * P:(q + 1) * P],
                               k_stack[0:3 * HD, g % 2, j, k0 * P:k1 * P], start=True, stop=not masked)
                if masked:
                    far = q - span >= 0
                    mm = pe.matmul(out[:, q * P:(q + 1) * P], ident_b[:], masks[:, 0, :], start=False, stop=not far)
                    if far:
                        mm = pe.matmul(out[:, k0 * P:(k0 + 1) * P], ident_b[:], masks[:, 1, :],
                                       start=False, stop=True)
                mm.then_inc(s_pa, 1)

            def score(b, g, k, j):
                n = (g * ST + k) * HG + j
                q0, q1 = queries_of[k]
                pe.wait_ge(s_exp, b * NSC + n + 1)
                out = pst[:, n % 2, :]
                mm = pe.matmul(out[:, q0 * P:q1 * P], k_stack[0:NR, g % 2, j, k * P:(k + 1) * P],
                               q_stack[0:NR, g % 2, j, q0 * P:q1 * P], start=True, stop=not masked)
                if masked:
                    far = k + span < ST
                    mm = pe.matmul(out[:, k * P:(k + 1) * P], ident_b[:], masks[:, 1, :], start=False, stop=not far)
                    if far:
                        mm = pe.matmul(out[:, (q1 - 1) * P:q1 * P], ident_b[:], masks[:, 0, :],
                                       start=False, stop=True)
                mm.then_inc(s_st, 1)

            def value_products(b, g, k, with_ones):
                if not with_ones:
                    pe.wait_ge(s_exp, b * NSC + (g * ST + k + 1) * HG + 2)
                    if k == 0:
                        pe.wait_ge(s_sums, b * G + g + 1)
                        pe.wait_ge(s_po_out, b * G + g + 1)
                q0, q1 = queries_of[k]
                for j in range(HG):
                    h = g * HG + j
                    lhs = ones[:] if with_ones else v_sb[:, k, h * HD:(h + 1) * HD]
                    mm = pe.matmul((psm if with_ones else po)[HD * j:HD * j + HD, q0 * P:q1 * P], lhs,
                                   probs[:, k % 2, j, q0 * P:q1 * P], start=(k == 0), stop=(k == ST - 1),
                                   skip_group_check=masked)
                if with_ones:
                    mm.then_inc(s_pv, 1)

            pe.wait_ge(s_w_lo, 3)
            pe.wait_ge(s_const, NCONST)
            for t in range(ST):
                transpose(0, t)
            pe.wait_ge(s_ctx_lo, 1)
            pe.wait_ge(s_pj_out, ST + 2)
            for n in range(4):
                project_qk(0, n)
            SETUP = 4 + 2 * masked
            if masked:
                pe.wait_ge(s_setup, SETUP)
            for i in range(NG):
                score_max(0, 0, i, first=True)
            transpose_maxima(0, 0)
            pe.wait_ge(s_setup, SETUP)
            pe.wait_ge(s_pj_out, 2 * ST + 2)

            def body(b, last):
                for t in range(ST):
                    project_v(b, t)
                for g in range(G):
                    bn_, gn = projected_in(b, g)
                    ahead = not (last and gn < 2)
                    pe.wait_ge(s_mrow[g % 2], (b * 2 + g // 2 + 1) * MROW)
                    for k in range(ST):
                        if g == 0 and k == 1:
                            pe.wait_ge(s_pj_out, b * PJ + V0 + ST + 2)
                        ms = [] if last and g == G - 1 else list(M_STEPS[k])
                        for j in range(HG):
                            score(b, g, k, j)
                            if k and j in (1, 2):
                                value_products(b, g, k - 1, j == 2)
                            for i in ms[M_SLOTS[k][j]:M_SLOTS[k][j + 1]]:
                                score_max(*next_group(b, g), i)
                        if g == 2 and k < 2 and not last:
                            transpose(b + 1, 2 * k)
                            transpose(b + 1, 2 * k + 1)
                        if k == 2 and ahead:
                            if gn == 0:
                                pe.wait_ge(s_ctx_lo, b + 2)
                            project_qk(bn_, 2 * gn)
                    value_products(b, g, ST - 1, False)
                    value_products(b, g, ST - 1, True)
                    if not (last and g == G - 1):
                        transpose_maxima(*next_group(b, g))
                    if ahead:
                        if gn == 0:
                            pe.wait_ge(s_pj_out, bn_ * PJ + T0 + ST + 2)
                        project_qk(bn_, 2 * gn + 1)
                pe.wait_ge(s_pj_out, (b + 1) * PJ + (0 if last else QK_A + 4) + 2)
                for t in range(ST):
                    if t >= 2:
                        pe.wait_ge(s_o_out, b * ST + t + 3)
                    pe.wait_ge(s_norm, (b + 1) * (G * ST) - ST + t + 2)
                    for g in range(G):
                        mm = pe.matmul(pj[:, t % 2, :], att[:, g, t * P:(t + 1) * P], wo[:, g, :],
                                       start=(g == 0), stop=(g == G - 1))
                    mm.then_inc(s_o, 1)

            with pe.Fori(0, B - 1) as b:
                body(b, False)
            body(B - 1, True)


I = 1536
IT = I // P
QBLOCK = 32
QMAX_A = 2.0 ** 15 - 1.0
QMAX_W = 2.0 ** 3 - 1.0
SCALE_MIN = 1e-12
SIG_ONE = 65536.0
NQ = B * IT // 4


def gated_mlp(nc, h_in, hmax_in, x_in, x_out, weights, gate, ident_in, spill):
    with ExitStack() as whole:
        def keep(name, shape, dt=F32):
            return whole.enter_context(nc.sbuf_tensor("m_" + name, shape, dt))

        scale = {n: keep("scale_" + n, [P, 1]) for n in ("h", "gate", "up", "silu", "out")}
        inv = {n: keep("inv_" + n, [P, 1]) for n in ("h", "gate", "up", "silu", "out")}
        peak = keep("peak", [P, 2])
        peak_all = keep("peak_all", [P, 2])
        mix = keep("mix", [P, 4])

        def find_scale(dve, link, name, top, unit):
            if unit is None:
                link(dve.tensor_scalar(scale[name][:], top, 1.0 / QMAX_A, SCALE_MIN, ALU.mult, ALU.max))
                link(dve.reciprocal(inv[name][:], scale[name][:]))
            else:
                link(dve.tensor_scalar(mix[:, 1:2], top, unit, 1.0 / QMAX_A, ALU.mult, ALU.mult))
                link(dve.tensor_scalar(scale[name][:], mix[:, 1:2], SCALE_MIN, None, ALU.max))
                link(dve.reciprocal(mix[:, 2:3], scale[name][:]))
                link(dve.tensor_tensor(inv[name][:], mix[:, 2:3], unit, ALU.mult))

        tools = (scale, inv, peak, peak_all, mix, find_scale)
        ident = keep("ident", [P, P])
        silu_q = None
        with ExitStack() as ctx:
            gate_w, up_w = [[nc.sbuf_tensor(f"m_{m}_{n}", [P, DT, I], F32R) for n in ("hi", "lo")] for m in ("gate", "up")]
            up_w = [ctx.enter_context(w) for w in up_w]
            with ExitStack() as first:
                gate_w = [first.enter_context(w) for w in gate_w]
                mlp_weights(nc, weights, ident_in, ident, gate_w, up_w, spill)
                mlp_inner(nc, 0, h_in, hmax_in, ident, gate_w, spill, None, *tools)
            silu_q = ctx.enter_context(nc.sbuf_tensor("m_silu_q", [P, NQ, 4 * S], I16))
            mlp_inner(nc, 1, h_in, hmax_in, ident, up_w, spill, silu_q, *tools)
            mlp_product(nc, spill, silu_q, *tools)
            mlp_down(nc, spill, silu_q, up_w, x_in, x_out, gate, scale, inv)


def mlp_weights(nc, weights, ident_in, ident, gate_w, up_w, spill):
    with ExitStack() as ctx:
        def sb(name, shape, dt=F32):
            return ctx.enter_context(nc.sbuf_tensor("mw_" + name, shape, dt))

        sem = stage_semaphores(nc, ctx, "mw_")

        NU, RB = 9, 4
        NB = D // QBLOCK
        raw = sb("raw", [P, 3, D])
        amax = sb("amax", [P, 2, NB])
        step = sb("step", [P, 2, NB])
        rstep = sb("rstep", [P, 2, NB])
        wi = sb("wi", [P, 2, D], I16)
        wq = sb("wq", [P, 2, D])
        down_hi = sb("down_hi", [P, 2, DT, P], F32R)
        down_lo = sb("down_lo", [P, 2, DT, P], F32R)
        pt = ctx.enter_context(nc.psum_tensor("mw_pt", [P, 2, 512], F32))
        s_raw = [sem(f"s_raw{i}") for i in range(3)]
        s_ident = sem("s_ident")
        s_amax = sem("s_amax")
        s_step = sem("s_step")
        s_rstep = sem("s_rstep")
        s_wi = sem("s_wi")
        s_wq = sem("s_wq")
        s_pt = sem("s_pt")
        s_hi = sem("s_hi")
        s_lo = sem("s_lo")
        s_down = [sem("s_down0"), sem("s_down1")]
        s_passed = sem("s_passed")
        s_passed_act = sem("s_passed_act")
        units = [(m, c) for c in range(3) for m in (2, 0, 1)]
        block = ctx.enter_context(nc.Block())

        def store(sp, b, n, c):
            passed(sp, s_lo, b * NU + n + 3, s_passed)
            for part, src in enumerate((down_hi, down_lo)):
                dst = spill["down"][part, :, 4 * c:4 * c + 4, bass.ds(b * P, P)]
                sp.dma_start(dst, f32(src[:, c % 2])).then_inc(s_down[c % 2], 16)

        def spread(a):
            return a.rearrange("p (k o) -> p k o", o=1).to_broadcast([P, NB, QBLOCK])

        def where(b, m, c):
            if m == 2:
                return down_hi[:, c % 2], down_lo[:, c % 2]
            cut = bass.ds(b * (3 * P) + c * P, P)
            return tuple(w[:, :, cut] for w in (gate_w, up_w)[m])

        @block.sync
        def _(sp):
            sp.dma_start(ident[:], ident_in).then_inc(s_ident, 16)
            with sp.Fori(0, RB) as b:
                for n, (m, c) in enumerate(units):
                    passed(sp, s_wi, b * NU + n + 1, s_passed)
                    if m < 2:
                        src = weights[m][bass.ds(b * (3 * P) + c * P, P), :]
                    else:
                        src = weights[2][bass.ds(b * P, P), c * D:(c + 1) * D]
                    sp.dma_start(raw[:, n % 3, :], src).then_inc(s_raw[n % 3], 16)
                    if n % 3 == 2:
                        store(sp, b, n - 2, n // 3)
            sp.wait_ge(s_down[0], 16 * 2 * (2 * RB + 1))
            sp.wait_ge(s_down[1], 16 * 2 * (RB + 1))

        @block.vector
        def _(dve):
            dve.sem_inc(s_wi, 3)
            dve.sem_inc(s_lo, 2)
            dve.sem_inc(s_down[0], 32)
            dve.sem_inc(s_down[1], 32)
            with dve.Fori(0, RB) as b:
                def split(n):
                    m, c = units[n]
                    dve.wait_ge(s_hi, b * NU + n + 1)
                    hi, lo = where(b, m, c)
                    dve.tensor_tensor(lo, pt[:, n % 2, :].rearrange("p (d o) -> p d o", d=DT), f32(hi),
                                      ALU.subtract).then_inc(s_lo, 1)

                for n, (m, c) in enumerate(units):
                    u, i = n % 2, b * NU + n + 1
                    v = raw[:, n % 3, :].rearrange("p (k s) -> p k s", s=QBLOCK)
                    dve.wait_ge(s_raw[n % 3], (b * 3 + n // 3 + 1) * 16)
                    dve.tensor_reduce(amax[:, u, :], v, AX.X, ALU.max, apply_absolute_value=True).then_inc(s_amax, 1)
                    dve.wait_ge(s_amax, i)
                    dve.tensor_scalar(step[:, u, :], amax[:, u, :], 1.0 / QMAX_W, SCALE_MIN,
                                      ALU.mult, ALU.max).then_inc(s_step, 1)
                    dve.wait_ge(s_step, i)
                    dve.reciprocal(rstep[:, u, :], step[:, u, :]).then_inc(s_rstep, 1)
                    dve.wait_ge(s_rstep, i)
                    dve.tensor_tensor(wi[:, u, :].rearrange("p (k s) -> p k s", s=QBLOCK), v,
                                      spread(rstep[:, u, :]), ALU.mult).then_inc(s_wi, 1)
                    dve.wait_ge(s_wi, i + 3)
                    if n >= 2:
                        dve.wait_ge(s_pt, b * NU + n - 1)
                    dve.tensor_tensor(wq[:, u, :].rearrange("p (k s) -> p k s", s=QBLOCK),
                                      wi[:, u, :].rearrange("p (k s) -> p k s", s=QBLOCK),
                                      spread(step[:, u, :]), ALU.mult).then_inc(s_wq, 1)
                    if n >= 1:
                        split(n - 1)
                split(NU - 1)

        @block.tensor
        def _(pe):
            pe.wait_ge(s_ident, 16)
            with pe.Fori(0, RB) as b:
                for n in range(NU):
                    pe.wait_ge(s_wq, b * NU + n + 1)
                    pe.wait_ge(s_lo, b * NU + n + 1)
                    for d in range(DT):
                        mm = pe.transpose(pt[:, n % 2, d * P:(d + 1) * P], wq[:, n % 2, d * P:(d + 1) * P], ident[:])
                    mm.then_inc(s_pt, 1)

        @block.scalar
        def _(act):
            with act.Fori(0, RB) as b:
                for n, (m, c) in enumerate(units):
                    if m == 2:
                        before = b * 2 + c // 2 + 1 if c % 2 == 0 else b + 1
                        act.wait_ge(s_down[c % 2], before * 32)
                    passed(act, s_pt, b * NU + n + 1, s_passed_act)
                    hi, _ = where(b, m, c)
                    act.activation(hi, pt[:, n % 2, :].rearrange("p (d o) -> p d o", d=DT), ACT.Copy).then_inc(s_hi, 1)


def sigmoid_u16(dve, sig, out):
    return dve.tensor_scalar(out, sig, SIG_ONE, SIG_ONE - 1.0, ALU.mult, ALU.min)


def mlp_inner(nc, m, h_in, hmax_in, ident, weights, spill, silu_q, scale, inv, peak, peak_all, mix, find_scale):
    with ExitStack() as ctx:
        def sb(name, shape, dt=F32):
            return ctx.enter_context(nc.sbuf_tensor(f"mi{m}_" + name, shape, dt))

        sem = stage_semaphores(nc, ctx, f"mi{m}_")

        W = 2 * S
        HALF_B = B // 2
        name = ("gate", "up")[m]
        w_hi, w_lo = weights
        h_tile = sb("h_tile", [P, 2, D])
        h_int = sb("h_int", [P, 2, D], I16)
        h_q = h_tile
        ht_hi = sb("ht_hi", [P, 2, DT, S], F32R)
        ht_lo = sb("ht_lo", [P, 2, DT, S], F32R)
        out = sb("out", [P, 2, 2, S])
        peaks = sb("peaks", [P, B * IT])
        if m == 1:
            raw = sb("raw", [P, 2, W])
            sig = sb("sig", [P, W])
            sig_q = sb("sig_q", [P, W], U16)
            gabs = sb("gabs", [P, W], I16)
            pair_peak = sb("pair_peak", [P, 2])
        pt = ctx.enter_context(nc.psum_tensor(f"mi{m}_pt", [P, 2, 512], F32))
        pm = ctx.enter_context(nc.psum_tensor(f"mi{m}_pm", [P, 4, 512], F32))
        s_peak_in = sem("s_peak_in")
        s_all = sem("s_all")
        s_link = sem("s_link")
        s_h_in = [sem("s_h_in0"), sem("s_h_in1")]
        s_int = sem("s_int")
        s_q = sem("s_q")
        s_pt = sem("s_pt")
        s_hi = sem("s_hi")
        s_lo = sem("s_lo")
        s_pm = sem("s_pm")
        s_out = sem("s_out")
        s_peak = sem("s_peak")
        s_store = [sem("s_store0"), sem("s_store1")]
        s_passed = sem("s_passed")
        s_passed_act = sem("s_passed_act")
        s_passed_dve = sem("s_passed_dve")
        s_fin = sem("s_fin")
        s_raw = [sem("s_raw0"), sem("s_raw1")]
        s_gate_int = [sem("s_gate_int0"), sem("s_gate_int1")]
        s_sig = sem("s_sig")
        s_sig_q = sem("s_sig_q")
        s_abs = sem("s_abs")
        s_pair = sem("s_pair")
        s_top = sem("s_top")
        s_silu = sem("s_silu")
        s_silu_int = sem("s_silu_int")
        block = ctx.enter_context(nc.Block())

        LOAD = [0, 1, 5, 7]
        QUANT, WIDEN, TURN, SPLIT = ([2 * t + d for t in range(ST)] for d in (2, 3, 4, 5))

        def first_half(eng, body):
            with eng.Fori(0, HALF_B // 2) as bb:
                for v in range(2):
                    body(bb * 2 + v, v, True, 0)

        def second_half(eng, body):
            for b in range(HALF_B, B):
                body(b, b % 2, b < B - 1, 1)

        def step_pair(b, n):
            first_quad = 2 * (b - HALF_B if isinstance(b, int) else b) * (IT // 4)
            return first_quad + n // 2, n % 2

        def cells(b, n):
            quad, half = step_pair(b, n)
            return silu_q[:, bass.ds(quad, 1), half * W:(half + 1) * W].rearrange("p o w -> p (o w)")

        def load_h(sp, b, t):
            passed(sp, s_pt, b * ST + t + 1, s_passed)
            sp.dma_start(h_tile[:, t % 2, :], h_in[b, t * P:(t + 1) * P, :]).then_inc(s_h_in[t % 2], 16)

        def load_gate(sp, b, n):
            passed(sp, s_pair, b * IT + n + 1, s_passed)
            quad, half = step_pair(b, n)
            sp.dma_start(raw[:, n % 2].rearrange("p (k t) -> p k t", k=2),
                         spill["raw"][0][quad][:, 2 * half:2 * half + 2, :]).then_inc(s_raw[n % 2], 16)

        @block.sync
        def _(sp):
            def body(b, v, more, half):
                for n in range(IT):
                    if more and n in LOAD:
                        load_h(sp, b + 1, LOAD.index(n))
                    if m == 1 and half == 0:
                        for i in ([0] if n == 0 else []) + ([n + 1] if n + 1 < IT else []):
                            load_gate(sp, b, i)
                    if n % 2 == 1:
                        p = n // 2
                        passed(sp, s_peak, b * IT + n + 1, s_passed)
                        sp.dma_start(spill["raw"][m][b * (IT // 4) + p // 2][:, 2 * (p % 2):2 * (p % 2) + 2, :],
                                     out[:, p % 2]).then_inc(s_store[p % 2], 16)

            if m == 0:
                sp.dma_start(peak[:, 0:1], hmax_in).then_inc(s_peak_in, 16)
            for t in range(ST):
                load_h(sp, 0, t)
            first_half(sp, body)
            second_half(sp, body)
            for u in range(2):
                sp.wait_ge(s_store[u], 16 * (B * IT // 4 + 1))

        @block.scalar
        def _(act):
            def widen(b, t):
                act.wait_ge(s_pt, b * ST + t + 1)
                act.wait_ge(s_int, b * ST + t + 3)
                act.activation(h_q[:, t % 2, :], h_int[:, t % 2, :], ACT.Copy).then_inc(s_q, 1)

            def hi(b, v, t):
                act.wait_ge(s_pt, b * ST + t + 3)
                act.activation(ht_hi[:, v, :, t * P:(t + 1) * P], pt[:, t % 2, :].rearrange("p (d t) -> p d t", d=DT),
                               ACT.Copy).then_inc(s_hi, 1)

            def silu_to_int(i):
                b, n = i // IT, i % IT
                passed(act, s_silu, i - HALF_B * IT + 1, s_passed_act)
                if i == HALF_B * IT:
                    act.wait_ge(s_fin, 1)
                act.activation(cells(b, n), raw[:, n % 2], ACT.Copy, scale=inv["silu"][:]).then_inc(s_silu_int, 1)

            def body(b, v, more, half):
                for n in range(IT):
                    if more and n in SPLIT:
                        hi(b + 1, 1 - v, SPLIT.index(n))
                    act.wait_ge(s_pm, b * IT + n + 1)
                    if n % 2 == 0:
                        act.wait_ge(s_store[n // 2 % 2], (b * (IT // 4) + n // 4 + 1) * 16)
                    act.activation(out[:, n // 2 % 2, n % 2, :], pm[:, n % 4, :], ACT.Copy).then_inc(s_out, 1)
                    if more and n in WIDEN:
                        widen(b + 1, WIDEN.index(n))
                    if m == 1:
                        i = b * IT + n
                        if half == 0 and n % 2 == 0:
                            passed(act, s_raw[0], (b * (IT // 2) + n // 2 + 1) * 16, s_passed_act)
                            act.activation(cells(b, n), raw[:, 0], ACT.Copy, scale=inv["gate"][:]).then_inc(s_gate_int[0], 1)
                        act.wait_ge(s_sig_q, i + 1)
                        if half == 0:
                            passed(act, s_gate_int[n % 2], b * (IT // 2) + n // 2 + 1, s_passed_act)
                        else:
                            passed(act, s_gate_int[1], HALF_B * IT // 2, s_passed_act)
                        act.activation(sig[:], cells(b, n), ACT.Sigmoid, scale=scale["gate"][:]).then_inc(s_sig, 1)
                        if half == 0:
                            passed(act, s_pair, i + 2, s_passed_act)
                            act.activation(gabs[:], cells(b, n), ACT.Abs).then_inc(s_abs, 1)
                        elif i > HALF_B * IT:
                            silu_to_int(i - 1)

            for t in range(ST):
                widen(0, t)
                if t >= 1:
                    hi(0, 0, t - 1)
            hi(0, 0, ST - 1)
            first_half(act, body)
            second_half(act, body)
            if m == 1:
                silu_to_int(B * IT - 1)

        @block.gpsimd
        def _(pool):
            def reduce_all():
                pool.partition_all_reduce(peak_all[:, 0:1], peak[:, 0:1], P, bass.bass_isa.ReduceOp.max).then_inc(s_all, 1)

            if m == 0:
                pool.wait_ge(s_peak_in, 16)
                reduce_all()
            else:
                pool.wait_ge(s_top, HALF_B * IT + 1)
                reduce_all()
            pool.wait_ge(s_fin, 1 + m)
            reduce_all()

        @block.vector
        def _(dve):
            chain = [0]

            def link(ins):
                chain[0] += 1
                ins.then_inc(s_link, 1)
                dve.wait_ge(s_link, chain[0])

            def quantise(b, t):
                dve.wait_ge(s_h_in[t % 2], (b * (ST // 2) + t // 2 + 1) * 16)
                dve.wait_ge(s_q, b * ST + t + 1)
                dve.tensor_scalar(h_int[:, t % 2, :], h_tile[:, t % 2, :], inv["h"][:], None,
                                  ALU.mult).then_inc(s_int, 1)

            def lo(b, v, t):
                dve.wait_ge(s_hi, b * ST + t + 1)
                dve.tensor_tensor(ht_lo[:, v, :, t * P:(t + 1) * P], pt[:, t % 2, :].rearrange("p (d t) -> p d t", d=DT),
                                  f32(ht_hi[:, v, :, t * P:(t + 1) * P]), ALU.subtract).then_inc(s_lo, 1)

            def body(b, v, more, half):
                for n in range(IT):
                    i = b * IT + n
                    if more and n in SPLIT:
                        lo(b + 1, 1 - v, SPLIT.index(n))
                    if more and n in QUANT:
                        quantise(b + 1, QUANT.index(n))
                    if m == 1:
                        dve.wait_ge(s_sig, i + 1)
                        dve.wait_ge(s_pair, HALF_B * IT + 2 if half else i + 2)
                        if half:
                            if i > HALF_B * IT:
                                dve.wait_ge(s_silu, i - HALF_B * IT)
                        sigmoid_u16(dve, sig[:], sig_q[:]).then_inc(s_sig_q, 1)
                    dve.wait_ge(s_out, i + 5)
                    dve.tensor_reduce(peaks[:, bass.ds(i, 1)], out[:, n // 2 % 2, n % 2, :], AX.X, ALU.max,
                                      apply_absolute_value=True).then_inc(s_peak, 1)
                    if m == 1 and half == 0 and n % 2 == 0:
                        dve.wait_ge(s_raw[1], (b * (IT // 2) + n // 2 + 1) * 16)
                        dve.tensor_scalar(cells(b, n + 1), raw[:, 1], inv["gate"][:], None, ALU.mult).then_inc(s_gate_int[1], 1)
                    if m == 1 and half == 0:
                        dve.wait_ge(s_sig_q, i + 2)
                        passed(dve, s_abs, i + 1, s_passed_dve)
                        dve.tensor_tensor_reduce(raw[:, n % 2], gabs[:], sig_q[:], 1.0, 0.0, ALU.mult, ALU.max,
                                                 pair_peak[:, n % 2:n % 2 + 1]).then_inc(s_pair, 1)
                        dve.wait_ge(s_pair, i + 3)
                        dve.wait_ge(s_top, i + 1)
                        dve.tensor_tensor(peak[:, 0:1], peak[:, 0:1], pair_peak[:, n % 2:n % 2 + 1], ALU.max).then_inc(s_top, 1)
                    if m == 1 and half == 1:
                        dve.wait_ge(s_sig_q, i + 2)
                        dve.wait_ge(s_silu_int, i - HALF_B * IT + 1)
                        dve.tensor_tensor(raw[:, n % 2], cells(b, n), sig_q[:], ALU.mult).then_inc(s_silu, 1)

            for s, n in ((s_int, 2), (s_q, 2), (s_pt, 2), (s_lo, 2), (s_out, 4), (s_store[0], 16), (s_store[1], 16),
                         (s_sig_q, 1), (s_pair, 2), (s_silu_int, 2)):
                dve.sem_inc(s, n)
            if m == 0:
                dve.wait_ge(s_all, 1)
                find_scale(dve, link, "h", peak_all[:, 0:1], None)
            else:
                dve.memset(peak[:, 0:1], 0.0).then_inc(s_top, 1)
            for t in range(ST):
                quantise(0, t)
                if t >= 1:
                    lo(0, 0, t - 1)
            lo(0, 0, ST - 1)
            first_half(dve, body)
            if m == 1:
                dve.wait_ge(s_all, 1)
                link(dve.tensor_scalar(mix[:, 0:1], scale["gate"][:], 1.0 / SIG_ONE, None, ALU.mult))
                find_scale(dve, link, "silu", peak_all[:, 0:1], mix[:, 0:1])
                dve.sem_inc(s_fin, 1)
            second_half(dve, body)
            dve.wait_ge(s_peak, B * IT)
            dve.tensor_reduce(peak[:, 0:1], peaks[:], AX.X, ALU.max).then_inc(s_fin, 1)
            dve.wait_ge(s_all, 2)
            find_scale(dve, link, name, peak_all[:, 0:1], scale["h"][:])

        @block.tensor
        def _(pe):
            def turn(b, t):
                pe.wait_ge(s_q, b * ST + t + 3)
                pe.wait_ge(s_lo, b * ST + t + 1)
                for d in range(DT):
                    mm = pe.transpose(pt[:, t % 2, d * P:(d + 1) * P], h_q[:, t % 2, d * P:(d + 1) * P], ident[:])
                mm.then_inc(s_pt, 1)

            def body(b, v, more, half):
                pe.wait_ge(s_lo, b * ST + ST + 2)
                for n in range(IT):
                    pe.wait_ge(s_out, b * IT + n + 1)
                    cut = slice(n * P, (n + 1) * P)
                    for d in range(DT):
                        ops = ((w_hi, ht_hi), (w_hi, ht_lo), (w_lo, ht_hi))
                        for p, (w, h) in enumerate(ops):
                            mm = pe.matmul(pm[:, n % 4, :], w[:, d, cut], h[:, v, d, :],
                                           start=(d == 0 and p == 0), stop=(d == DT - 1 and p == 2))
                    mm.then_inc(s_pm, 1)
                    if more and n in TURN:
                        turn(b + 1, TURN.index(n))

            for t in range(ST):
                turn(0, t)
            first_half(pe, body)
            second_half(pe, body)


def mlp_product(nc, spill, silu_q, scale, inv, peak, peak_all, mix, find_scale):
    with ExitStack() as ctx:
        def sb(name, shape, dt=F32):
            return ctx.enter_context(nc.sbuf_tensor("mp_" + name, shape, dt))

        sem = stage_semaphores(nc, ctx, "mp_")

        W = 2 * S
        NPAIR = 2 * NQ
        raw = sb("raw", [P, 2, W])
        uabs = sb("uabs", [P, 2, W], I16)
        sabs = sb("sabs", [P, 2, W], I16)
        prod = sb("prod", [P, W])
        pair_peak = sb("pair_peak", [P, 2])
        s_raw = [sem("s_raw0"), sem("s_raw1")]
        s_uabs = sem("s_uabs")
        s_sabs = sem("s_sabs")
        s_peak = sem("s_peak")
        s_top = sem("s_top")
        s_all = sem("s_all")
        s_link = sem("s_link")
        s_passed = sem("s_passed")
        s_passed_dve = sem("s_passed_dve")
        block = ctx.enter_context(nc.Block())

        @block.sync
        def _(sp):
            with sp.Fori(0, NQ) as i:
                for u in range(2):
                    passed(sp, s_uabs, i * 2 + u + 1, s_passed)
                    sp.dma_start(raw[:, u].rearrange("p (k t) -> p k t", k=2),
                                 spill["raw"][1][i][:, 2 * u:2 * u + 2, :]).then_inc(s_raw[u], 16)

        @block.scalar
        def _(act):
            with act.Fori(0, NQ) as i:
                for u in range(2):
                    n = i * 2 + u
                    act.wait_ge(s_raw[u], (i + 1) * 16)
                    act.wait_ge(s_peak, n + 1)
                    act.activation(uabs[:, u], raw[:, u], ACT.Abs, scale=inv["up"][:]).then_inc(s_uabs, 1)
                    act.activation(sabs[:, u], silu_q[:, bass.ds(i, 1), u * W:(u + 1) * W].rearrange("p o w -> p (o w)"),
                                   ACT.Abs).then_inc(s_sabs, 1)

        @block.vector
        def _(dve):
            chain = [0]

            def link(ins):
                chain[0] += 1
                ins.then_inc(s_link, 1)
                dve.wait_ge(s_link, chain[0])

            dve.sem_inc(s_uabs, 2)
            dve.sem_inc(s_peak, 2)
            dve.memset(peak[:, 0:1], 0.0).then_inc(s_top, 1)
            with dve.Fori(0, NQ) as i:
                for u in range(2):
                    n = i * 2 + u
                    dve.wait_ge(s_uabs, n + 3)
                    passed(dve, s_sabs, n + 1, s_passed_dve)
                    dve.tensor_tensor_reduce(prod[:], sabs[:, u], uabs[:, u], 1.0, 0.0, ALU.mult, ALU.max,
                                             pair_peak[:, u:u + 1]).then_inc(s_peak, 1)
                    dve.wait_ge(s_peak, n + 3)
                    dve.wait_ge(s_top, n + 1)
                    dve.tensor_tensor(peak[:, 0:1], peak[:, 0:1], pair_peak[:, u:u + 1], ALU.max).then_inc(s_top, 1)
            dve.wait_ge(s_all, 1)
            link(dve.tensor_tensor(mix[:, 0:1], scale["silu"][:], scale["up"][:], ALU.mult))
            find_scale(dve, link, "out", peak_all[:, 0:1], mix[:, 0:1])

        @block.gpsimd
        def _(pool):
            pool.wait_ge(s_top, NPAIR + 1)
            pool.partition_all_reduce(peak_all[:, 0:1], peak[:, 0:1], P, bass.bass_isa.ReduceOp.max).then_inc(s_all, 1)


def mlp_down(nc, spill, silu_q, up_w, x_in, x_out, gate, scale, inv):
    with ExitStack() as ctx:
        def sb(name, shape, dt=F32):
            return ctx.enter_context(nc.sbuf_tensor("md_" + name, shape, dt))

        sem = stage_semaphores(nc, ctx, "md_")

        W = 2 * S
        NP = IT // 2
        wd = [w[:].rearrange("p d i -> p (d i)").rearrange("p (i o) -> p i o", i=IT) for w in up_w]
        raw = sb("raw", [P, 2, W])
        up_q = sb("up_q", [P, W], I16)
        prod = sb("prod", [P, W])
        prod_q = sb("prod_q", [P, 2, W], I16)
        p_hi = sb("p_hi", [P, 2, 2, S], F32R)
        p_lo = sb("p_lo", [P, 2, 2, S], F32R)
        x_new = sb("x_new", [P, 2, D])
        gate_col = sb("gate_col", [P, 1])
        tanh_g = sb("tanh_g", [P, 1])
        factor = sb("factor", [P, 1])
        pd = ctx.enter_context(nc.psum_tensor("md_pd", [P, 2, ST, 512], F32))
        s_wd = sem("s_wd")
        s_gate = sem("s_gate")
        s_raw = [sem("s_raw0"), sem("s_raw1")]
        s_up = sem("s_up")
        s_prod = sem("s_prod")
        s_int = sem("s_int")
        s_hi = sem("s_hi")
        s_lo = sem("s_lo")
        s_used = sem("s_used")
        s_x = [sem("s_x0"), sem("s_x1")]
        s_new = sem("s_new")
        s_store = [sem("s_store0"), sem("s_store1")]
        s_tanh = sem("s_tanh")
        s_factor = sem("s_factor")
        s_passed = sem("s_passed")
        block = ctx.enter_context(nc.Block())

        def store(sp, b, t):
            passed(sp, s_new, b * ST + t + 1 + 2 * ST, s_passed)
            sp.dma_start(x_out[b, t * P:(t + 1) * P, :], x_new[:, t % 2, :]).then_inc(s_store[t % 2], 16)

        @block.sync
        def _(sp):
            for part in range(2):
                sp.dma_start(f32(wd[part]), spill["down"][part]).then_inc(s_wd, 16)
            sp.dma_start(gate_col[:], gate).then_inc(s_gate, 16)

            def load_x(b, t):
                passed(sp, s_store[t % 2], (b * 2 + t // 2 + 1) * 16, s_passed)
                sp.dma_start(x_new[:, t % 2, :], x_in[b, t * P:(t + 1) * P, :]).then_inc(s_x[t % 2], 16)

            def body(bb, first):
                for v in range(2):
                    b = bb * 2 + v
                    for c in range(NP):
                        passed(sp, s_up, b * NP + c + 1, s_passed)
                        sp.dma_start(raw[:, c % 2].rearrange("p (k t) -> p k t", k=2),
                                     spill["raw"][1][b * (NP // 2) + c // 2][:, 2 * (c % 2):2 * (c % 2) + 2, :]
                                     ).then_inc(s_raw[c % 2], 16)
                        if not (first and v == 0):
                            if 1 <= c <= ST:
                                load_x(b - 1, c - 1)
                            if 2 <= c <= ST + 1:
                                store(sp, b - 1, c - 2)

            body(0, True)
            with sp.Fori(1, B // 2) as bb:
                body(bb, False)
            for t in range(ST):
                load_x(B - 1, t)
                if t >= 1:
                    store(sp, B - 1, t - 1)
            store(sp, B - 1, ST - 1)
            for u in range(2):
                sp.wait_ge(s_store[u], 16 * (B * 2 + 1))

        @block.scalar
        def _(act):
            act.wait_ge(s_gate, 16)
            act.activation(tanh_g[:], gate_col[:], ACT.Tanh).then_inc(s_tanh, 1)
            with act.Fori(0, B // 2) as bb:
                for v in range(2):
                    for c in range(NP):
                        n = bb * (2 * NP) + v * NP + c
                        act.wait_ge(s_int, n + 1)
                        act.wait_ge(s_used, n + 1)
                        act.activation(p_hi[:, c % 2].rearrange("p k t -> p (k t)"), prod_q[:, c % 2], ACT.Copy).then_inc(s_hi, 1)

        @block.vector
        def _(dve):
            dve.sem_inc(s_up, 2)
            dve.sem_inc(s_used, 2)
            dve.sem_inc(s_new, 2 * ST)
            dve.sem_inc(s_store[0], 16)
            dve.sem_inc(s_store[1], 16)
            dve.wait_ge(s_tanh, 1)
            dve.tensor_tensor(factor[:], tanh_g[:], scale["out"][:], ALU.mult).then_inc(s_factor, 1)
            dve.wait_ge(s_factor, 1)

            def to_lo(b, c):
                dve.wait_ge(s_hi, b * NP + c + 1)
                dve.tensor_tensor(p_lo[:, c % 2].rearrange("p k t -> p (k t)"), prod_q[:, c % 2],
                                  f32(p_hi[:, c % 2]).rearrange("p k t -> p (k t)"), ALU.subtract).then_inc(s_lo, 1)

            def take_out(b, v, t):
                dve.wait_ge(s_x[t % 2], (b * 2 + t // 2 + 1) * 16)
                dve.wait_ge(s_used, (b + 1) * NP + 2)
                dve.scalar_tensor_tensor(x_new[:, t % 2, :], pd[:, v, t, :], factor[:], x_new[:, t % 2, :],
                                         ALU.mult, ALU.add).then_inc(s_new, 1)

            def body(bb, first):
                for v in range(2):
                    b = bb * 2 + v
                    for c in range(NP):
                        i = b * NP + c + 1
                        quad = b * (NP // 2) + c // 2
                        q = silu_q[:, bass.ds(quad, 1), (c % 2) * W:(c % 2 + 1) * W].rearrange("p o w -> p (o w)")
                        dve.wait_ge(s_raw[c % 2], (quad + 1) * 16)
                        dve.tensor_scalar(up_q[:], raw[:, c % 2], inv["up"][:], None, ALU.mult).then_inc(s_up, 1)
                        dve.wait_ge(s_up, i + 2)
                        dve.tensor_tensor(prod[:], q, up_q[:], ALU.mult).then_inc(s_prod, 1)
                        dve.wait_ge(s_prod, i)
                        dve.tensor_scalar(prod_q[:, c % 2], prod[:], inv["out"][:], None, ALU.mult).then_inc(s_int, 1)
                        if c >= 1:
                            to_lo(b, c - 1)
                        if 1 <= c <= ST and not (first and v == 0):
                            take_out(b - 1, 1 - v, c - 1)
                    to_lo(b, NP - 1)

            body(0, True)
            with dve.Fori(1, B // 2) as bb:
                body(bb, False)
            for t in range(ST):
                take_out(B - 1, 1, t)

        @block.tensor
        def _(pe):
            pe.wait_ge(s_wd, 32)
            with pe.Fori(0, B // 2) as bb:
                for v in range(2):
                    for c in range(NP):
                        pe.wait_ge(s_lo, bb * (2 * NP) + v * NP + c + 1)
                        if c == 0:
                            pe.wait_ge(s_new, bb * (2 * ST) + (v + 1) * ST)
                        for t in range(ST):
                            cut = slice(t * P, (t + 1) * P)
                            for k in range(2):
                                i = 2 * c + k
                                ops = ((p_hi, 0), (p_hi, 1), (p_lo, 0))
                                for p, (lhs, part) in enumerate(ops):
                                    mm = pe.matmul(pd[:, v, t, :], lhs[:, c % 2, k, cut], wd[part][:, i, :],
                                                   start=(i == 0 and p == 0), stop=(i == IT - 1 and p == 2))
                        mm.then_inc(s_used, 1)


E_N = 8
TOP = 2
F = 1024
FT = F // P
CAP = max(1, -(-5 * T * TOP // (4 * E_N)))
SLOTS = E_N * CAP
CT = 5
CW = CT * P
CHUNKS = SLOTS // CW
CE = CHUNKS // E_N
WEIGHT_MIN = 1e-9


def mixture(nc, h_in, x_in, x_out, router_w, router_b, w1, w2, b1, b2, gate, consts, spill):
    with ExitStack() as whole:
        def keep(name, shape, dt=F32):
            return whole.enter_context(nc.sbuf_tensor("x_" + name, shape, dt))

        token_of = keep("token_of", [P, SLOTS // P + CT], I32)
        slot_of = keep("slot_of", [P, NT, TOP], I32)
        weight = keep("weight", [P, NT, TOP])
        route(nc, h_in, router_w, router_b, gate, consts, spill["tokens"], token_of, slot_of, weight)
        experts(nc, h_in, w1, w2, b1, b2, consts["ident"], token_of, spill["expert_out"])
        combine(nc, spill["expert_out"], x_in, x_out, slot_of, weight)


def route(nc, h_in, router_w, router_b, gate, consts, tokens, token_of, slot_of, weight):
    with ExitStack() as ctx:
        def sb(name, shape, dt=F32):
            return ctx.enter_context(nc.sbuf_tensor("r_" + name, shape, dt))

        def ps(name, shape):
            return ctx.enter_context(nc.psum_tensor("r_" + name, shape, F32))

        sem = stage_semaphores(nc, ctx, "r_")

        h = sb("h", [P, 2, ST, D])
        h_t = sb("h_t", [P, 2, D])
        rw = sb("rw", [P, DT, E_N])
        rb = sb("rb", [P, E_N])
        ident = sb("ident", [P, P])
        before = sb("before", [P, P])
        ones = sb("ones", [P, P])
        expert = sb("expert", [P, NT, E_N])
        spare = sb("spare", [P, NT, TOP])
        token_id = sb("token_id", [P, NT], I32)
        gate_col = sb("gate_col", [P, 1])
        tanh_g = sb("tanh_g", [P, 1])
        zeros = sb("zeros", [P, (SLOTS + T * TOP) // P], I32)
        prob = sb("prob", [P, NT, E_N])
        row = sb("row", [P, NT])
        top_p = sb("top_p", [P, NT, 8])
        top_i = sb("top_i", [P, NT, 8], U32)
        top_e = sb("top_e", [P, NT, TOP])
        hot = [sb("hot0", [P, NT, E_N]), sb("hot1", [P, NT, E_N])]
        taken = sb("taken", [P, NT, E_N])
        base = [sb("base0", [P, NT, E_N]), sb("base1", [P, NT, E_N])]
        rank = sb("rank", [P, NT, TOP])
        kept = sb("kept", [P, NT, TOP])
        cell = sb("cell", [P, NT, TOP])
        put_at = sb("put_at", [P, NT, TOP], I32)
        table = sb("table", [SLOTS // P, P], I32)
        table_f = sb("table_f", [SLOTS // P, P])
        pt = ps("pt", [P, 2, 512])
        pl = ps("pl", [P, 2, 512])
        pr = ps("pr", [P, 2, 512])
        pk = ps("pk", [P, 512])
        s_const = sem("s_const")
        s_h = [sem("s_h0"), sem("s_h1")]
        s_pt = sem("s_pt")
        s_ht = sem("s_ht")
        s_logit = sem("s_logit")
        s_prob = sem("s_prob")
        s_link = sem("s_link")
        s_exp_in = sem("s_exp_in")
        s_exp = sem("s_exp")
        s_tanh = sem("s_tanh")
        s_taken = sem("s_taken")
        s_count = sem("s_count")
        s_put_at = sem("s_put_at")
        s_zero = sem("s_zero")
        s_zeroed = sem("s_zeroed")
        s_put = sem("s_put")
        s_table = sem("s_table")
        s_table_f = sem("s_table_f")
        s_turned = sem("s_turned")
        s_token_of = sem("s_token_of")
        s_passed = sem("s_passed")
        NCONST = 8 * 16
        block = ctx.enter_context(nc.Block())

        def over_experts(a):
            return a.rearrange("p (t o) -> p t o", o=1).to_broadcast([P, NT, E_N])

        @block.sync
        def _(sp):
            for dst, src in ((ident, consts["ident"]), (before, consts["before"]), (expert, consts["expert"]),
                             (spare, consts["spare"]), (token_id, consts["token_id"]), (rw, router_w),
                             (rb, router_b), (gate_col, gate)):
                sp.dma_start(dst[:], src).then_inc(s_const, 16)
            sp.wait_ge(s_zero, 1)
            sp.dma_start(tokens.rearrange("(p n) o -> p (n o)", p=P), zeros[:]).then_inc(s_zeroed, 16)
            with sp.Fori(0, B // 2) as bb:
                for v in range(2):
                    passed(sp, s_pt, (bb * 2 + v + 1) * ST, s_passed)
                    sp.dma_start(h[:, v], h_in[bb * 2 + v].rearrange("(t p) d -> p t d", p=P)).then_inc(s_h[v], 16)
            sp.wait_ge(s_put, TOP * NT * 16)
            sp.dma_start(table[:], tokens[0:SLOTS].rearrange("(n p) o -> n (p o)", p=P)).then_inc(s_table, 16)

        @block.scalar
        def _(act):
            act.wait_ge(s_const, NCONST)
            act.activation(tanh_g[:], gate_col[:], ACT.Tanh).then_inc(s_tanh, 1)
            with act.Fori(0, B // 2) as bb:
                for n in range(2 * ST):
                    i = bb * (2 * ST) + n
                    act.wait_ge(s_pt, i + 1 + 2 * ST)
                    act.wait_ge(s_logit, i + 1)
                    act.activation(h_t[:, n % 2, :], pt[:, n % 2, :], ACT.Copy).then_inc(s_ht, 1)
            act.wait_ge(s_exp_in, 1)
            act.activation(prob[:], prob[:], ACT.Exp).then_inc(s_exp, 1)

        @block.tensor
        def _(pe):
            def logits(bb, n):
                i = bb * (2 * ST) + n
                v, t = n // ST, n % ST
                if t == 0:
                    pe.wait_ge(s_prob, bb * 2 + v + 1)
                pe.wait_ge(s_ht, i + 3)
                for d in range(DT):
                    mm = pe.matmul(pl[:, v, t * E_N:(t + 1) * E_N], h_t[:, n % 2, d * P:(d + 1) * P], rw[:, d, :],
                                   start=(d == 0), stop=(d == DT - 1))
                mm.then_inc(s_logit, 1)

            pe.wait_ge(s_const, NCONST)
            with pe.Fori(0, B // 2) as bb:
                for n in range(2 * ST):
                    v, t = n // ST, n % ST
                    if t == 0:
                        pe.wait_ge(s_h[v], (bb + 1) * 16)
                    pe.wait_ge(s_ht, bb * (2 * ST) + n + 1)
                    for d in range(DT):
                        mm = pe.transpose(pt[:, n % 2, d * P:(d + 1) * P], h[:, v, t, d * P:(d + 1) * P], ident[:])
                    mm.then_inc(s_pt, 1)
                    if n >= 1:
                        logits(bb, n - 1)
                logits(bb, 2 * ST - 1)
            pe.wait_ge(s_taken, 1)
            flat = taken[:].rearrange("p t e -> p (t e)")
            pe.matmul(pr[:, 0, :NT * E_N], before[:], flat, start=True, stop=True).then_inc(s_count, 1)
            pe.matmul(pr[:, 1, :NT * E_N], ones[:], flat, start=True, stop=True).then_inc(s_count, 1)
            pe.wait_ge(s_table_f, 1)
            pe.transpose(pk[:, :SLOTS // P], table_f[:], ident[:SLOTS // P, :SLOTS // P]).then_inc(s_turned, 1)

        @block.vector
        def _(dve):
            chain = [0]

            def link(ins):
                chain[0] += 1
                ins.then_inc(s_link, 1)
                dve.wait_ge(s_link, chain[0])

            dve.sem_inc(s_pt, 2 * ST)
            dve.sem_inc(s_ht, 2)
            dve.sem_inc(s_logit, 2)
            dve.sem_inc(s_prob, 2)
            dve.memset(zeros[:], 0).then_inc(s_zero, 1)
            link(dve.memset(ones[:], 1.0))
            dve.wait_ge(s_tanh, 1)
            with dve.Fori(0, B // 2) as bb:
                for v in range(2):
                    b = bb * 2 + v
                    dve.wait_ge(s_logit, (b + 1) * ST + 2)
                    dve.tensor_tensor(prob[:, bass.ds(b * ST, ST), :],
                                      pl[:, v, :ST * E_N].rearrange("p (t e) -> p t e", e=E_N),
                                      rb[:].rearrange("p (o e) -> p o e", o=1).to_broadcast([P, ST, E_N]),
                                      ALU.add).then_inc(s_prob, 1)
            dve.wait_ge(s_prob, B + 2)
            link(dve.tensor_reduce(row[:], prob[:], AX.X, ALU.max))
            dve.tensor_tensor(prob[:], prob[:], over_experts(row[:]), ALU.subtract).then_inc(s_exp_in, 1)
            dve.wait_ge(s_exp, 1)
            link(dve.tensor_reduce(row[:], prob[:], AX.X, ALU.add))
            link(dve.reciprocal(row[:], row[:]))
            link(dve.tensor_tensor(prob[:], prob[:], over_experts(row[:]), ALU.mult))
            for t in range(NT):
                ins = dve.max(top_p[:, t, :], prob[:, t, :])
            link(ins)
            for t in range(NT):
                ins = dve.max_index(top_i[:, t, :], top_p[:, t, :], prob[:, t, :])
            link(ins)
            link(dve.tensor_copy(top_e[:], top_i[:, :, 0:TOP]))
            for k in range(TOP):
                ins = dve.tensor_tensor(hot[k][:], expert[:], top_e[:, :, k:k + 1].to_broadcast([P, NT, E_N]),
                                        ALU.is_equal)
            link(ins)
            dve.tensor_tensor(taken[:], hot[0][:], hot[1][:], ALU.add).then_inc(s_taken, 1)
            link(dve.tensor_tensor(row[:], top_p[:, :, 0], top_p[:, :, 1], ALU.add))
            link(dve.tensor_scalar(row[:], row[:], WEIGHT_MIN, None, ALU.max))
            link(dve.reciprocal(row[:], row[:]))
            link(dve.tensor_scalar(row[:], row[:], tanh_g[:], None, ALU.mult))
            link(dve.tensor_tensor(weight[:], top_p[:, :, 0:TOP],
                                   row[:].rearrange("p (t o) -> p t o", o=1).to_broadcast([P, NT, TOP]), ALU.mult))
            dve.wait_ge(s_count, 2)
            link(dve.memset(base[0][:, 0:1, :], 0.0))
            link(dve.tensor_copy(base[0][:, 1:, :].rearrange("p t e -> p (t e)"), pr[:, 1, :(NT - 1) * E_N]))
            reach, u = 1, 0
            while reach < NT:
                old, new = base[u], base[1 - u]
                dve.tensor_copy(new[:, :reach, :], old[:, :reach, :])
                link(dve.tensor_tensor(new[:, reach:, :], old[:, reach:, :], old[:, :NT - reach, :], ALU.add))
                reach, u = 2 * reach, 1 - u
            ranks, spent = base[u], base[1 - u]
            link(dve.tensor_tensor(ranks[:].rearrange("p t e -> p (t e)"), ranks[:].rearrange("p t e -> p (t e)"),
                                   pr[:, 0, :NT * E_N], ALU.add))
            for k in range(TOP):
                link(dve.tensor_tensor(spent[:], hot[k][:], ranks[:], ALU.mult))
                link(dve.tensor_reduce(rank[:, :, k], spent[:], AX.X, ALU.add))
            link(dve.tensor_scalar(kept[:], rank[:], float(CAP), None, ALU.is_lt))
            link(dve.tensor_tensor(weight[:], weight[:], kept[:], ALU.mult))
            link(dve.scalar_tensor_tensor(cell[:], top_e[:], float(CAP), rank[:], ALU.mult, ALU.add))
            link(dve.tensor_tensor(cell[:], cell[:], spare[:], ALU.subtract))
            link(dve.tensor_tensor(cell[:], cell[:], kept[:], ALU.mult))
            link(dve.tensor_tensor(cell[:], cell[:], spare[:], ALU.add))
            dve.tensor_copy(put_at[:], cell[:]).then_inc(s_put_at, 1)
            link(dve.tensor_scalar(rank[:], rank[:], float(CAP - 1), None, ALU.min))
            dve.wait_ge(s_put_at, 1)
            link(dve.scalar_tensor_tensor(cell[:], top_e[:], float(CAP), rank[:], ALU.mult, ALU.add))
            link(dve.tensor_copy(slot_of[:], cell[:]))
            dve.wait_ge(s_table, 16)
            dve.tensor_copy(table_f[:], table[:]).then_inc(s_table_f, 1)
            dve.wait_ge(s_turned, 1)
            dve.tensor_copy(token_of[:, :SLOTS // P], pk[:, :SLOTS // P]).then_inc(s_token_of, 1)
            dve.memset(token_of[:, SLOTS // P:], 0).then_inc(s_token_of, 1)
            dve.wait_ge(s_token_of, 2)

        @block.gpsimd
        def _(pool):
            pool.wait_ge(s_zeroed, 16)
            pool.wait_ge(s_put_at, 1)
            for t in range(NT):
                for k in range(TOP):
                    pool.indirect_dma_start(tokens, bass.IndirectOffsetOnAxis(put_at[:, t, k:k + 1], 0),
                                            token_id[:, t:t + 1], None).then_inc(s_put, 16)


def experts(nc, h_in, w1, w2, b1, b2, ident_in, token_of, expert_out):
    rows = h_in.rearrange("b s d -> (b s) d")
    with ExitStack() as ctx:
        def sb(name, shape, dt=F32):
            return ctx.enter_context(nc.sbuf_tensor("e_" + name, shape, dt))

        sem = stage_semaphores(nc, ctx, "e_")

        HALF = CW // 2
        W2CUT = FT // 2
        raw1 = sb("raw1", [P, DT, F])
        raw2 = sb("raw2", [P, FT, D])
        w1_hi = sb("w1_hi", [P, DT, F], F32R)
        w1_lo = sb("w1_lo", [P, DT, F], F32R)
        w2_hi = sb("w2_hi", [P, FT, D], F32R)
        w2_lo = sb("w2_lo", [P, FT, D], F32R)
        b1_all = sb("b1_all", [P, E_N, FT])
        b1_col = sb("b1_col", [P, FT])
        b2_row = sb("b2_row", [P, D])
        ident = sb("ident", [P, P])
        index = sb("index", [P, 2, CT], I32)
        x = sb("x", [P, 2, CT, D])
        xt_hi = sb("xt_hi", [P, DT, CW], F32R)
        xt_lo = sb("xt_lo", [P, DT, CW], F32R)
        g = sb("g", [P, 2, CW])
        g_hi = sb("g_hi", [P, FT, CW], F32R)
        g_lo = sb("g_lo", [P, FT, CW], F32R)
        out = sb("out", [P, CT, D])
        pt = ctx.enter_context(nc.psum_tensor("e_pt", [P, 2, 512], F32))
        ph = ctx.enter_context(nc.psum_tensor("e_ph", [P, 2, 2, 512], F32))
        po = ctx.enter_context(nc.psum_tensor("e_po", [P, 2, 512], F32))
        s_const = sem("s_const")
        s_raw1 = sem("s_raw1")
        s_raw2 = sem("s_raw2")
        s_w1_hi = sem("s_w1_hi")
        s_w1_lo = sem("s_w1_lo")
        s_w2_hi = sem("s_w2_hi")
        s_w2_lo = sem("s_w2_lo")
        s_b1 = sem("s_b1")
        s_b2 = sem("s_b2")
        s_index = sem("s_index")
        s_x = [sem("s_x0"), sem("s_x1")]
        s_pt = sem("s_pt")
        s_xt_hi = sem("s_xt_hi")
        s_xt = sem("s_xt")
        s_ph = sem("s_ph")
        s_g = sem("s_g")
        s_g_hi = sem("s_g_hi")
        s_g_lo = sem("s_g_lo")
        s_po = sem("s_po")
        s_out = sem("s_out")
        s_store = sem("s_store")
        s_passed = sem("s_passed")
        s_passed_pool = sem("s_passed_pool")
        block = ctx.enter_context(nc.Block())

        def load(sp, e):
            first = isinstance(e, int)
            if not first:
                passed(sp, s_w1_lo, e, s_passed)
            sp.dma_start(raw1[:], w1[e]).then_inc(s_raw1, 16)
            if not first:
                passed(sp, s_w2_lo, 2 * e, s_passed)
            sp.dma_start(raw2[:], w2[e]).then_inc(s_raw2, 16)

        def load_b2(sp, e):
            passed(sp, s_out, e * (CE * CT) + 2, s_passed)
            sp.dma_start(b2_row[:], b2[bass.ds(e, 1), :].to_broadcast([P, D])).then_inc(s_b2, 16)

        def store(sp, e, c):
            passed(sp, s_out, (e * CE + c + 1) * CT + 2, s_passed)
            dst = expert_out[bass.ds(e * CAP + c * CW, CW), :].rearrange("(t p) d -> p t d", p=P)
            sp.dma_start(dst, out[:]).then_inc(s_store, 16)

        @block.sync
        def _(sp):
            sp.dma_start(ident[:], ident_in).then_inc(s_const, 16)
            sp.dma_start(b1_all[:], b1).then_inc(s_const, 16)
            load(sp, 0)
            load_b2(sp, 0)
            store(sp, 0, 0)
            with sp.Fori(1, E_N) as e:
                load(sp, e)
                store(sp, e - 1, 1)
                load_b2(sp, e)
                store(sp, e, 0)
            store(sp, E_N - 1, 1)
            sp.wait_ge(s_store, (CHUNKS + 1) * 16)

        @block.gpsimd
        def _(pool):
            def gather(n, c):
                passed(pool, s_index, n + 1, s_passed_pool)
                for s in range(CT):
                    pool.indirect_dma_start(x[:, c, s, :], None, rows,
                                            bass.IndirectOffsetOnAxis(index[:, c, s:s + 1], 0)).then_inc(s_x[c], 16)

            gather(0, 0)
            with pool.Fori(0, E_N) as e:
                pool.wait_ge(s_w1_hi, e + 1)
                pool.tensor_tensor(w1_lo[:], raw1[:], f32(w1_hi[:]), ALU.subtract).then_inc(s_w1_lo, 1)
                gather(e * CE + 1, 1)
                for half in range(2):
                    cut = slice(half * W2CUT, (half + 1) * W2CUT)
                    pool.wait_ge(s_w2_hi, e * 2 + half + 1)
                    pool.tensor_tensor(w2_lo[:, cut], raw2[:, cut], f32(w2_hi[:, cut]), ALU.subtract).then_inc(s_w2_lo, 1)
                gather(e * CE + 2, 0)

        @block.scalar
        def _(act):
            def transposed(n, c):
                for s in range(CT):
                    act.wait_ge(s_pt, n * CT + s + 1)
                    act.activation(xt_hi[:, :, s * P:(s + 1) * P],
                                   pt[:, (c * CT + s) % 2, :].rearrange("p (d t) -> p d t", d=DT),
                                   ACT.Copy).then_inc(s_xt_hi, 1)

            transposed(0, 0)
            with act.Fori(0, E_N) as e:
                act.wait_ge(s_raw1, (e + 1) * 16)
                act.activation(w1_hi[:], raw1[:], ACT.Copy).then_inc(s_w1_hi, 1)
                act.wait_ge(s_b1, e + 1)
                for c in range(CE):
                    for f in range(FT):
                        i = e * (CE * FT) + c * FT + f
                        act.wait_ge(s_ph, i + 1)
                        act.wait_ge(s_g_lo, i + 1)
                        act.activation(g[:, f % 2].rearrange("p (h t) -> p h t", h=2), ph[:, f % 2, :, :HALF], ACT.Gelu,
                                       bias=b1_col[:, f:f + 1]).then_inc(s_g, 1)
                        act.wait_ge(s_g, i + 3)
                        act.activation(g_hi[:, f, :], g[:, f % 2, :], ACT.Copy).then_inc(s_g_hi, 1)
                        if c == 0 and f in (1, 3):
                            cut = slice(f // 2 * W2CUT, (f // 2 + 1) * W2CUT)
                            act.wait_ge(s_raw2, (e + 1) * 16)
                            act.activation(w2_hi[:, cut], raw2[:, cut], ACT.Copy).then_inc(s_w2_hi, 1)
                    transposed(e * CE + c + 1, 1 - c)

        @block.vector
        def _(dve):
            def put_index(n, c):
                dve.tensor_copy(index[:, c, :], token_of[:, bass.ds(n * CT, CT)]).then_inc(s_index, 1)

            def transposed(n, c):
                for s in range(CT):
                    cut = (slice(None), slice(None), slice(s * P, (s + 1) * P))
                    dve.wait_ge(s_xt_hi, n * CT + s + 1)
                    dve.tensor_tensor(xt_lo[cut], pt[:, (c * CT + s) % 2, :].rearrange("p (d t) -> p d t", d=DT),
                                      f32(xt_hi[cut]), ALU.subtract).then_inc(s_xt, 1)

            for s, n in ((s_xt, 2), (s_g, 2), (s_g_lo, 2), (s_out, 2), (s_store, 16)):
                dve.sem_inc(s, n)
            put_index(0, 0)
            dve.wait_ge(s_const, 32)
            transposed(0, 0)
            with dve.Fori(0, E_N) as e:
                dve.tensor_copy(b1_col[:], b1_all[:, bass.ds(e, 1), :].rearrange("p o f -> p (o f)")).then_inc(s_b1, 1)
                for c in range(CE):
                    n = e * CE + c
                    put_index(n + 1, 1 - c)
                    for f in range(FT):
                        dve.wait_ge(s_g_hi, e * (CE * FT) + c * FT + f + 1)
                        dve.tensor_tensor(g_lo[:, f, :], g[:, f % 2, :], f32(g_hi[:, f, :]), ALU.subtract).then_inc(s_g_lo, 1)
                    transposed(n + 1, 1 - c)
                    dve.wait_ge(s_store, (n + 1) * 16)
                    if c == 0:
                        dve.wait_ge(s_b2, (e + 1) * 16)
                    for s in range(CT):
                        dve.wait_ge(s_po, n * CT + s + 1)
                        dve.tensor_tensor(out[:, s, :], po[:, (c * CT + s) % 2, :], b2_row[:], ALU.add).then_inc(s_out, 1)

        @block.tensor
        def _(pe):
            def transpose(n, c, e):
                pe.wait_ge(s_x[c], (e + 1) * (CT * 16))
                for s in range(CT):
                    pe.wait_ge(s_xt, n * CT + s + 1)
                    for d in range(DT):
                        mm = pe.transpose(pt[:, (c * CT + s) % 2, d * P:(d + 1) * P], x[:, c, s, d * P:(d + 1) * P], ident[:])
                    mm.then_inc(s_pt, 1)

            pe.wait_ge(s_const, 32)
            transpose(0, 0, 0)
            with pe.Fori(0, E_N) as e:
                pe.wait_ge(s_w1_lo, e + 1)
                for c in range(CE):
                    n = e * CE + c
                    pe.wait_ge(s_xt, (n + 1) * CT + 2)
                    for f in range(FT):
                        pe.wait_ge(s_g, n * FT + f + 1)
                        cut = slice(f * P, (f + 1) * P)
                        for half in range(2):
                            part = slice(half * HALF, (half + 1) * HALF)
                            for d in range(DT):
                                ops = ((w1_hi, xt_hi), (w1_hi, xt_lo), (w1_lo, xt_hi))
                                for p, (w, r) in enumerate(ops):
                                    mm = pe.matmul(ph[:, f % 2, half, :HALF], w[:, d, cut], r[:, d, part],
                                                   start=(d == 0 and p == 0), stop=(d == DT - 1 and p == 2))
                        mm.then_inc(s_ph, 1)
                    transpose(n + 1, 1 - c, e if c == 0 else e + 1)
                    if c == 0:
                        pe.wait_ge(s_w2_lo, 2 * e + 2)
                    for s in range(CT):
                        pe.wait_ge(s_out, n * CT + s + 1)
                        cut = slice(s * P, (s + 1) * P)
                        for f in range(FT):
                            if s == 0:
                                pe.wait_ge(s_g_lo, n * FT + f + 3)
                            ops = ((g_hi, w2_hi), (g_hi, w2_lo), (g_lo, w2_hi))
                            for p, (l, w) in enumerate(ops):
                                mm = pe.matmul(po[:, (c * CT + s) % 2, :], l[:, f, cut], w[:, f, :],
                                               start=(f == 0 and p == 0), stop=(f == FT - 1 and p == 2))
                        mm.then_inc(s_po, 1)


def combine(nc, expert_out, x_in, x_out, slot_of, weight):
    with ExitStack() as ctx:
        def sb(name, shape, dt=F32):
            return ctx.enter_context(nc.sbuf_tensor("c_" + name, shape, dt))

        sem = stage_semaphores(nc, ctx, "c_")

        index = sb("index", [P, 2, ST * TOP], I32)
        part = sb("part", [P, 2, ST, TOP, D])
        x = sb("x", [P, 2, ST, D])
        w = sb("w", [P, 2, ST * TOP])
        s_index = [sem("s_index0"), sem("s_index1")]
        s_part = [sem("s_part0"), sem("s_part1")]
        s_x = [sem("s_x0"), sem("s_x1")]
        s_w = sem("s_w")
        s_first = sem("s_first")
        s_sum = sem("s_sum")
        s_store = [sem("s_store0"), sem("s_store1")]
        s_passed = sem("s_passed")
        s_passed_pool = sem("s_passed_pool")
        block = ctx.enter_context(nc.Block())

        def store(sp, b, v):
            passed(sp, s_sum, b + 3, s_passed)
            sp.dma_start(x_out[b].rearrange("(t p) d -> p t d", p=P), x[:, v]).then_inc(s_store[v], 16)

        @block.sync
        def _(sp):
            with sp.Fori(0, B // 2) as bb:
                for v in range(2):
                    passed(sp, s_store[v], (bb + 1) * 16, s_passed)
                    sp.dma_start(x[:, v], x_in[bb * 2 + v].rearrange("(t p) d -> p t d", p=P)).then_inc(s_x[v], 16)
                for v in range(2):
                    store(sp, bb * 2 + v, v)
            for v in range(2):
                sp.wait_ge(s_store[v], (B // 2 + 1) * 16)

        @block.gpsimd
        def _(pool):
            with pool.Fori(0, B // 2) as bb:
                for v in range(2):
                    passed(pool, s_index[v], bb + 1, s_passed_pool)
                    for t in range(ST):
                        for k in range(TOP):
                            pool.indirect_dma_start(part[:, v, t, k, :], None, expert_out,
                                                    bass.IndirectOffsetOnAxis(index[:, v, t * TOP + k:t * TOP + k + 1], 0)
                                                    ).then_inc(s_part[v], 16)

        @block.vector
        def _(dve):
            def put_index(b, v):
                cut = bass.ds(b * ST, ST)
                dve.tensor_copy(index[:, v, :].rearrange("p (t k) -> p t k", k=TOP), slot_of[:, cut, :]).then_inc(s_index[v], 1)

            def body(bb, last):
                for v in range(2):
                    b = bb * 2 + v
                    dve.tensor_copy(w[:, v, :].rearrange("p (t k) -> p t k", k=TOP),
                                    weight[:, bass.ds(b * ST, ST), :]).then_inc(s_w, 1)
                    dve.wait_ge(s_w, b + 1)
                    dve.wait_ge(s_part[v], (bb + 1) * (ST * TOP * 16))
                    dve.wait_ge(s_x[v], (bb + 1) * 16)
                    for t in range(ST):
                        dve.scalar_tensor_tensor(x[:, v, t, :], part[:, v, t, 0, :], w[:, v, t * TOP:t * TOP + 1], x[:, v, t, :],
                                                 ALU.mult, ALU.add).then_inc(s_first, 1)
                    for t in range(ST):
                        dve.wait_ge(s_first, b * ST + t + 1)
                        ins = dve.scalar_tensor_tensor(x[:, v, t, :], part[:, v, t, 1, :], w[:, v, t * TOP + 1:t * TOP + 2],
                                                       x[:, v, t, :], ALU.mult, ALU.add)
                    ins.then_inc(s_sum, 1)
                    if not last:
                        dve.wait_ge(s_sum, b + 3)
                        put_index(b + 2, v)

            dve.sem_inc(s_sum, 2)
            dve.sem_inc(s_store[0], 16)
            dve.sem_inc(s_store[1], 16)
            put_index(0, 0)
            put_index(1, 1)
            with dve.Fori(0, B // 2 - 1) as bb:
                body(bb, False)
            body(B // 2 - 1, True)



def program(nc, x, ctx_t, out, bufs, attn, mlp, moe, g_xattn, g_ffn, consts):
    def column(g, layer):
        return g[:, layer:layer + 1].to_broadcast([P, 1])

    def row(v):
        return v.to_broadcast([P, D])

    def attend(layer, x_in, x_out, hmax):
        a = attn[layer]
        attention(nc, layer, x_in, x_out, bufs["h"], hmax, ctx_t, [a["Wq"], a["Wk"], a["Wv"], a["Wo"]],
                  {"bq": a["bq"], "bk": a["bk"]}, {"bv": row(a["bv"]), "bo": row(a["bo"])},
                  column(g_xattn, layer), consts)

    attend(0, x, bufs["x1"], bufs["hmax"])
    gated_mlp(nc, bufs["h"], bufs["hmax"], bufs["x1"], bufs["x2"], (mlp["w_gate"], mlp["w_up"], mlp["w_down"]),
              column(g_ffn, 0), consts["ident"], bufs)
    attend(1, bufs["x2"], bufs["x1"], None)
    mixture(nc, bufs["h"], bufs["x1"], out, moe["router_w"], moe["router_b"].to_broadcast([P, E_N]),
            moe["w1"], moe["w2"], moe["b1"], moe["b2"], column(g_ffn, 1), consts, bufs)




def heads_inside(a):
    return a.reshape(*a.shape[:-1], G, HG, HD).swapaxes(-1, -2).reshape(a.shape)


def lay_w(w, interleave):
    wt = w.T
    if interleave:
        wt = heads_inside(wt)
    return np.ascontiguousarray(wt.reshape(DT, P, D).transpose(1, 0, 2))


def lay_bias(v):
    return np.ascontiguousarray(heads_inside(v).reshape(G, P).T)


def constants():
    token = np.arange(NT)[None, :, None] * P + np.arange(P)[:, None, None]
    p, c = np.arange(P)[:, None], np.arange(P)[None, :]
    half = HD // 2
    inv_freq = np.float32(1.0) / np.float32(10000.0) ** (np.arange(half, dtype=np.float32) / np.float32(half))
    angle = inv_freq.astype(np.float32)[:, None] * np.arange(S, dtype=np.float32)[None, :]
    cos, sin = np.cos(angle), np.sin(angle)
    return {
        "ident": np.eye(P, dtype=np.float32),
        "masks": np.stack([np.where(c <= p, 0.0, NEG), np.where(c >= p, 0.0, NEG)], 1).astype(np.float32),
        "cos": np.repeat(np.concatenate([cos, cos]), HG, 0),
        "sin": np.repeat(np.concatenate([sin, -sin]), HG, 0),
        "before": np.triu(np.ones((P, P), np.float32), 1),
        "expert": np.ascontiguousarray(np.broadcast_to(np.arange(E_N, dtype=np.float32), (P, NT, E_N))),
        "spare": (SLOTS + np.arange(TOP)[None, None, :] * T + token).astype(np.float32),
        "token_id": token[:, :, 0].astype(np.int32),
    }


def kernel(**inputs):
    import concourse.bacc as bacc
    from concourse.bass_utils import run_bass_kernel_spmd

    a = {k: np.asarray(v) for k, v in inputs.items()}
    ctx = a["ctx_1024"]
    ctx_t = np.concatenate([ctx, ctx[:1]]).transpose(0, 2, 1).reshape(B + 1, DT, P, S).transpose(0, 2, 1, 3)
    arrays = {"x": a["x"], "ctx_t": ctx_t, "g_xattn": a["g_xattn"][None], "g_ffn": a["g_ffn"][None]}
    for layer in range(2):
        at = f"L{layer}_xattn_"
        for n in ("Wq", "Wk", "Wv", "Wo"):
            arrays[at + n] = lay_w(a[at + n], n in ("Wq", "Wk"))
        for n in ("bq", "bk"):
            arrays[at + n] = lay_bias(a[at + n])
        for n in ("bv", "bo"):
            arrays[at + n] = a[at + n][None]
    for n in ("w_gate", "w_up", "w_down"):
        arrays[n] = a["L0_ffn_" + n]
    arrays["router_w"] = a["L1_ffn_router_w"].reshape(DT, P, E_N).transpose(1, 0, 2)
    arrays["router_b"] = a["L1_ffn_router_b"][None]
    arrays["w1"] = a["L1_ffn_w1"].reshape(E_N, DT, P, F).transpose(0, 2, 1, 3)
    arrays["w2"] = a["L1_ffn_w2"].reshape(E_N, FT, P, D).transpose(0, 2, 1, 3)
    arrays["b1"] = a["L1_ffn_b1"].reshape(E_N, FT, P).transpose(2, 0, 1)
    arrays["b2"] = a["L1_ffn_b2"]
    consts = constants()
    arrays.update(consts)
    arrays = {"in_" + k: np.ascontiguousarray(v) for k, v in arrays.items()}

    nc = bacc.Bacc("TRN2", target_bir_lowering=False, num_devices=1)
    t = {k[3:]: nc.dram_tensor(k, v.shape, mybir.dt.from_np(v.dtype), kind="ExternalInput").ap()
         for k, v in arrays.items()}
    out = nc.dram_tensor("out", (B, S, D), F32, kind="ExternalOutput").ap()

    def scratch(name, shape, dt=F32):
        return nc.dram_tensor(name, shape, dt, kind="Internal").ap()

    bufs = {
        "x1": scratch("x1", (B, S, D)), "x2": scratch("x2", (B, S, D)), "h": scratch("h", (B, S, D)),
        "hmax": scratch("hmax", (P, 1)),
        "raw": [scratch(n, (NQ, P, 4, S)) for n in ("gate_raw", "up_raw")],
        "down": scratch("down_split", (2, P, IT, D)),
        "tokens": scratch("tokens", (SLOTS + T * TOP, 1), I32), "expert_out": scratch("expert_out", (SLOTS, D)),
    }
    attn = [{n: t[f"L{layer}_xattn_{n}"] for n in ("Wq", "bq", "Wk", "bk", "Wv", "bv", "Wo", "bo")} for layer in range(2)]
    program(nc, t["x"], t["ctx_t"], out, bufs, attn, t, t, t["g_xattn"], t["g_ffn"], {k: t[k] for k in consts})
    r = run_bass_kernel_spmd(nc, [arrays], core_ids=[0])
    return r.results[0]["out"]
```
